# Optimizing a Trainium2 kernel written in Bass

```python
import numpy as np
import jax
import jax.numpy as jnp

def _softmax(x, axis=-1):
    return jax.nn.softmax(x, axis=axis)

def _gelu(x):
    return jax.nn.gelu(x, approximate=True)

def _silu(x):
    return jax.nn.silu(x)

def _sigmoid(x):
    return jax.nn.sigmoid(x)

def _layernorm(x, axis=-1, eps=1e-05):
    m = jnp.mean(x, axis=axis, keepdims=True)
    v = jnp.var(x, axis=axis, keepdims=True)
    return (x - m) / jnp.sqrt(v + eps)

def _scatter_add(tgt, idx, src, axis=0):
    return tgt.at[idx].add(src)

def _segment_sum(src, seg, n):
    return jax.ops.segment_sum(src, seg, n)
kernel_name = 'mk_adaln_d2_jaxref_r8_c59708'

def setup_inputs(seed: int=0):
    np.random.seed(seed)
    _w = jnp.asarray

    def _L0_attn_setup():
        import jax, jax.numpy as jnp
        import numpy as np
        D_MODEL = 128
        D_STATE = 16
        D_CONV = 4
        EXPAND = 2
        D_INNER = EXPAND * D_MODEL
        DT_RANK = D_MODEL // 16
        BATCH = 4
        SEQ = 256
        key = jax.random.key(seed)
        ks = jax.random.split(key, 9)
        s = lambda k, shape, sc: jax.random.normal(k, shape, jnp.float32) * sc
        x = s(ks[0], (BATCH, SEQ, D_MODEL), 1.0)
        W_in = s(ks[1], (2 * D_INNER, D_MODEL), D_MODEL ** (-0.5))
        conv_w = s(ks[2], (D_INNER, D_CONV), D_CONV ** (-0.5))
        conv_b = s(ks[3], (D_INNER,), 0.02)
        W_xproj = s(ks[4], (DT_RANK + 2 * D_STATE, D_INNER), D_INNER ** (-0.5))
        W_dt = s(ks[5], (D_INNER, DT_RANK), DT_RANK ** (-0.5))
        b_dt = jax.random.uniform(ks[6], (D_INNER,), jnp.float32, -4.0, -1.0)
        A_log = jnp.log(jnp.tile(jnp.arange(1, D_STATE + 1, dtype=jnp.float32), (D_INNER, 1)))
        D_skip = jnp.ones((D_INNER,), jnp.float32)
        W_out = s(ks[7], (D_MODEL, D_INNER), D_INNER ** (-0.5))
        return dict(x=x, W_in=W_in, conv_w=conv_w, conv_b=conv_b, W_xproj=W_xproj, W_dt=W_dt, b_dt=b_dt, A_log=A_log, D_skip=D_skip, W_out=W_out)
    _L0_attn_in = _L0_attn_setup()

    def _L0_ffn_setup():
        import jax, jax.numpy as jnp
        import numpy as np
        E = 8
        K = 2
        key = jax.random.key(seed)
        ks = jax.random.split(key, 8)
        B, T, d = (4, 256, 128)
        h = 4 * d // E
        s = 0.02
        X = jax.random.normal(ks[0], (B, T, d), jnp.float32)
        routing_W = jax.random.normal(ks[1], (E, d), jnp.float32) * s
        expert_bias = jnp.zeros((E,), jnp.float32)
        sW1 = jax.random.normal(ks[2], (d, h), jnp.float32) * s
        sb1 = jnp.zeros((h,), jnp.float32)
        sW2 = jax.random.normal(ks[3], (h, d), jnp.float32) * s
        sb2 = jnp.zeros((d,), jnp.float32)
        rW1 = jax.random.normal(ks[4], (E, d, h), jnp.float32) * s
        rb1 = jnp.zeros((E, h), jnp.float32)
        rW2 = jax.random.normal(ks[5], (E, h, d), jnp.float32) * s
        rb2 = jnp.zeros((E, d), jnp.float32)
        return dict(X=X, routing_W=routing_W, expert_bias=expert_bias, sW1=sW1, sb1=sb1, sW2=sW2, sb2=sb2, rW1=rW1, rb1=rb1, rW2=rW2, rb2=rb2)
    _L0_ffn_in = _L0_ffn_setup()
    _L0_c = _w((lambda *s: np.random.randn(*s).astype(np.float32) * 0.05)(16, 128))
    _L0_wmod = _w((lambda *s: np.random.randn(*s).astype(np.float32) * 0.05)(128, 6 * 128) * 128 ** (-0.5))

    def _L1_attn_setup():
        import jax, jax.numpy as jnp
        import numpy as np
        from jax import lax
        B, T, D = (2, 128, 128)
        H, DK, DV, K = (8, 128, 32, 4)
        EPS = 1e-05

        def short_conv(x, w):
            Kc = w.shape[-1]
            xp = jnp.pad(x, ((0, 0), (Kc - 1, 0), (0, 0))).transpose(0, 2, 1)
            y = lax.conv_general_dilated(xp, w[:, None, :], (1,), 'VALID', feature_group_count=w.shape[0])
            return jax.nn.silu(y.transpose(0, 2, 1))

        def l2norm(x):
            return x * lax.rsqrt(jnp.sum(x * x, axis=-1, keepdims=True) + 1e-06)

        def gated_delta_rule(q, k, v, g, beta):
            scale = q.shape[-1] ** (-0.5)
            q = l2norm(q) * scale
            k = l2norm(k)
            qT, kT, vT = (a.transpose(1, 0, 2, 3) for a in (q, k, v))
            gT, bT = (g.transpose(1, 0, 2), beta.transpose(1, 0, 2))
            S0 = jnp.zeros((q.shape[0], q.shape[2], q.shape[3], v.shape[3]), q.dtype)

            def step(S, inp):
                q_t, k_t, v_t, g_t, b_t = inp
                S = S * jnp.exp(g_t)[..., None, None]
                u = (v_t - jnp.einsum('bhk,bhkv->bhv', k_t, S)) * b_t[..., None]
                S = S + jnp.einsum('bhk,bhv->bhkv', k_t, u)
                o_t = jnp.einsum('bhk,bhkv->bhv', q_t, S)
                return (S, o_t)
            _, oT = lax.scan(step, S0, (qT, kT, vT, gT, bT))
            return oT.transpose(1, 0, 2, 3)
        key = jax.random.key(seed)
        ks = jax.random.split(key, 16)
        s = 0.02
        dt = jax.random.uniform(ks[10], (H,), minval=0.001, maxval=0.1)
        return {'x': jax.random.normal(ks[0], (B, T, D), jnp.float32), 'Wq': jax.random.normal(ks[1], (D, H * DK), jnp.float32) * s, 'Wk': jax.random.normal(ks[2], (D, H * DK), jnp.float32) * s, 'Wv': jax.random.normal(ks[3], (D, H * DV), jnp.float32) * s, 'conv_q': jax.random.normal(ks[4], (H * DK, K), jnp.float32) * 0.2, 'conv_k': jax.random.normal(ks[5], (H * DK, K), jnp.float32) * 0.2, 'conv_v': jax.random.normal(ks[6], (H * DV, K), jnp.float32) * 0.2, 'Wb': jax.random.normal(ks[7], (D, H), jnp.float32) * s, 'Wa': jax.random.normal(ks[8], (D, H), jnp.float32) * s, 'A_log': jnp.log(jax.random.uniform(ks[9], (H,), minval=1.0, maxval=16.0)), 'dt_bias': jnp.log(jnp.expm1(dt)), 'Wg': jax.random.normal(ks[11], (D, H * DV), jnp.float32) * s, 'norm_w': jnp.ones((DV,), jnp.float32), 'Wo': jax.random.normal(ks[12], (H * DV, D), jnp.float32) * s}
    _L1_attn_in = _L1_attn_setup()

    def _L1_ffn_setup():
        import jax, jax.numpy as jnp
        import numpy as np
        B, S, H, D, E = (4, 128, 128, 512, 8)
        key = jax.random.key(seed)
        ks = jax.random.split(key, 12)

        def init(k, shape, fan_in):
            return jax.random.normal(k, shape, jnp.float32) / np.float32(np.sqrt(fan_in))
        return {'x': jax.random.normal(ks[0], (B, S, H), jnp.float32), 'Wq': init(ks[1], (H, H), H), 'bq': jnp.zeros((H,), jnp.float32), 'Wk': init(ks[2], (H, H), H), 'bk': jnp.zeros((H,), jnp.float32), 'Wv': init(ks[3], (H, H), H), 'bv': jnp.zeros((H,), jnp.float32), 'Wo': init(ks[4], (H, H), H), 'bo': jnp.zeros((H,), jnp.float32), 'Wg': init(ks[5], (H, E), H), 'bg': jnp.zeros((E,), jnp.float32), 'W1': init(ks[6], (E, H, D), H), 'b1': jnp.zeros((E, D), jnp.float32), 'W2': init(ks[7], (E, D, H), D), 'b2': jnp.zeros((E, H), jnp.float32)}
    _L1_ffn_in = _L1_ffn_setup()
    _L1_c = _w((lambda *s: np.random.randn(*s).astype(np.float32) * 0.05)(16, 128))
    _L1_wmod = _w((lambda *s: np.random.randn(*s).astype(np.float32) * 0.05)(128, 6 * 128) * 128 ** (-0.5))
    _d = {'L0_attn_x': _L0_attn_in['x'], 'L0_attn_W_in': _L0_attn_in['W_in'], 'L0_attn_conv_w': _L0_attn_in['conv_w'], 'L0_attn_conv_b': _L0_attn_in['conv_b'], 'L0_attn_W_xproj': _L0_attn_in['W_xproj'], 'L0_attn_W_dt': _L0_attn_in['W_dt'], 'L0_attn_b_dt': _L0_attn_in['b_dt'], 'L0_attn_A_log': _L0_attn_in['A_log'], 'L0_attn_D_skip': _L0_attn_in['D_skip'], 'L0_attn_W_out': _L0_attn_in['W_out'], 'L0_ffn_routing_W': _L0_ffn_in['routing_W'], 'L0_ffn_expert_bias': _L0_ffn_in['expert_bias'], 'L0_ffn_sW1': _L0_ffn_in['sW1'], 'L0_ffn_sb1': _L0_ffn_in['sb1'], 'L0_ffn_sW2': _L0_ffn_in['sW2'], 'L0_ffn_sb2': _L0_ffn_in['sb2'], 'L0_ffn_rW1': _L0_ffn_in['rW1'], 'L0_ffn_rb1': _L0_ffn_in['rb1'], 'L0_ffn_rW2': _L0_ffn_in['rW2'], 'L0_ffn_rb2': _L0_ffn_in['rb2'], 'L0_c': _L0_c, 'L0_wmod': _L0_wmod, 'L1_attn_Wq': _L1_attn_in['Wq'], 'L1_attn_Wk': _L1_attn_in['Wk'], 'L1_attn_Wv': _L1_attn_in['Wv'], 'L1_attn_conv_q': _L1_attn_in['conv_q'], 'L1_attn_conv_k': _L1_attn_in['conv_k'], 'L1_attn_conv_v': _L1_attn_in['conv_v'], 'L1_attn_Wb': _L1_attn_in['Wb'], 'L1_attn_Wa': _L1_attn_in['Wa'], 'L1_attn_A_log': _L1_attn_in['A_log'], 'L1_attn_dt_bias': _L1_attn_in['dt_bias'], 'L1_attn_Wg': _L1_attn_in['Wg'], 'L1_attn_norm_w': _L1_attn_in['norm_w'], 'L1_attn_Wo': _L1_attn_in['Wo'], 'L1_ffn_Wq': _L1_ffn_in['Wq'], 'L1_ffn_bq': _L1_ffn_in['bq'], 'L1_ffn_Wk': _L1_ffn_in['Wk'], 'L1_ffn_bk': _L1_ffn_in['bk'], 'L1_ffn_Wv': _L1_ffn_in['Wv'], 'L1_ffn_bv': _L1_ffn_in['bv'], 'L1_ffn_Wo': _L1_ffn_in['Wo'], 'L1_ffn_bo': _L1_ffn_in['bo'], 'L1_ffn_Wg': _L1_ffn_in['Wg'], 'L1_ffn_bg': _L1_ffn_in['bg'], 'L1_ffn_W1': _L1_ffn_in['W1'], 'L1_ffn_b1': _L1_ffn_in['b1'], 'L1_ffn_W2': _L1_ffn_in['W2'], 'L1_ffn_b2': _L1_ffn_in['b2'], 'L1_c': _L1_c, 'L1_wmod': _L1_wmod}
    _x0 = _d['L0_attn_x']
    _d['L0_attn_x'] = jax.random.normal(jax.random.fold_in(jax.random.key(seed), 1), (16, 256, 128), dtype=_x0.dtype)
    del _x0
    return _d

def reference(L0_attn_x, L0_attn_W_in, L0_attn_conv_w, L0_attn_conv_b, L0_attn_W_xproj, L0_attn_W_dt, L0_attn_b_dt, L0_attn_A_log, L0_attn_D_skip, L0_attn_W_out, L0_ffn_routing_W, L0_ffn_expert_bias, L0_ffn_sW1, L0_ffn_sb1, L0_ffn_sW2, L0_ffn_sb2, L0_ffn_rW1, L0_ffn_rb1, L0_ffn_rW2, L0_ffn_rb2, L0_c, L0_wmod, L1_attn_Wq, L1_attn_Wk, L1_attn_Wv, L1_attn_conv_q, L1_attn_conv_k, L1_attn_conv_v, L1_attn_Wb, L1_attn_Wa, L1_attn_A_log, L1_attn_dt_bias, L1_attn_Wg, L1_attn_norm_w, L1_attn_Wo, L1_ffn_Wq, L1_ffn_bq, L1_ffn_Wk, L1_ffn_bk, L1_ffn_Wv, L1_ffn_bv, L1_ffn_Wo, L1_ffn_bo, L1_ffn_Wg, L1_ffn_bg, L1_ffn_W1, L1_ffn_b1, L1_ffn_W2, L1_ffn_b2, L1_c, L1_wmod):

    def _L0_attn_ref(x, W_in, conv_w, conv_b, W_xproj, W_dt, b_dt, A_log, D_skip, W_out):
        import jax, jax.numpy as jnp
        import numpy as np
        D_MODEL = 128
        D_STATE = 16
        D_CONV = 4
        EXPAND = 2
        D_INNER = EXPAND * D_MODEL
        DT_RANK = D_MODEL // 16
        BATCH = 4
        SEQ = 256
        silu = jax.nn.silu
        xz = jnp.einsum('bld,ed->ble', x, W_in)
        xi, z = jnp.split(xz, 2, axis=-1)
        K = conv_w.shape[1]
        L = xi.shape[1]
        xpad = jnp.pad(xi, ((0, 0), (K - 1, 0), (0, 0)))
        xc = sum((xpad[:, k:k + L, :] * conv_w[:, k] for k in range(K)))
        u = silu(xc + conv_b)
        dbl = jnp.einsum('blc,ec->ble', u, W_xproj)
        dt = jax.nn.softplus(jnp.einsum('blr,cr->blc', dbl[..., :DT_RANK], W_dt) + b_dt)
        Bs = dbl[..., DT_RANK:DT_RANK + D_STATE]
        Cs = dbl[..., DT_RANK + D_STATE:]
        A = -jnp.exp(A_log)

        def step(h, inp):
            dt_t, B_t, C_t, u_t = inp
            dA = jnp.exp(dt_t[:, :, None] * A)
            h = h * dA + (dt_t * u_t)[:, :, None] * B_t[:, None, :]
            y = jnp.einsum('bcs,bs->bc', h, C_t)
            return (h, y)
        h0 = jnp.zeros((x.shape[0], D_INNER, D_STATE), x.dtype)
        xs = (jnp.swapaxes(dt, 0, 1), jnp.swapaxes(Bs, 0, 1), jnp.swapaxes(Cs, 0, 1), jnp.swapaxes(u, 0, 1))
        _, ys = jax.lax.scan(step, h0, xs)
        y = jnp.swapaxes(ys, 0, 1) + u * D_skip
        y = y * silu(z)
        return jnp.einsum('blc,dc->bld', y, W_out)

    def _L0_ffn_ref(X, routing_W, expert_bias, sW1, sb1, sW2, sb2, rW1, rb1, rW2, rb2):
        import jax, jax.numpy as jnp
        import numpy as np
        E = 8
        K = 2
        B, T, d = X.shape
        shared = jax.nn.silu(X @ sW1 + sb1) @ sW2 + sb2
        logits = jnp.einsum('btd,ed->bte', X, routing_W) + expert_bias
        activation = jnp.sqrt(jax.nn.softplus(logits))
        top_vals, top_idx = jax.lax.top_k(activation, K)
        combine = jnp.sum(jax.nn.one_hot(top_idx, E, dtype=X.dtype) * top_vals[..., None], axis=-2)
        Xf = X.reshape(-1, d)
        cf = combine.reshape(-1, E)
        hdn = jax.nn.silu(jnp.einsum('nd,edh->enh', Xf, rW1) + rb1[:, None, :])
        y = jnp.einsum('enh,ehd->end', hdn, rW2) + rb2[:, None, :]
        routed = jnp.einsum('ne,end->nd', cf, y).reshape(B, T, d)
        return shared + routed

    def _L1_attn_ref(x, Wq, Wk, Wv, conv_q, conv_k, conv_v, Wb, Wa, A_log, dt_bias, Wg, norm_w, Wo):
        import jax, jax.numpy as jnp
        import numpy as np
        from jax import lax
        B, T, D = (2, 128, 128)
        H, DK, DV, K = (8, 128, 32, 4)
        EPS = 1e-05

        def short_conv(x, w):
            Kc = w.shape[-1]
            xp = jnp.pad(x, ((0, 0), (Kc - 1, 0), (0, 0))).transpose(0, 2, 1)
            y = lax.conv_general_dilated(xp, w[:, None, :], (1,), 'VALID', feature_group_count=w.shape[0])
            return jax.nn.silu(y.transpose(0, 2, 1))

        def l2norm(x):
            return x * lax.rsqrt(jnp.sum(x * x, axis=-1, keepdims=True) + 1e-06)

        def gated_delta_rule(q, k, v, g, beta):
            scale = q.shape[-1] ** (-0.5)
            q = l2norm(q) * scale
            k = l2norm(k)
            qT, kT, vT = (a.transpose(1, 0, 2, 3) for a in (q, k, v))
            gT, bT = (g.transpose(1, 0, 2), beta.transpose(1, 0, 2))
            S0 = jnp.zeros((q.shape[0], q.shape[2], q.shape[3], v.shape[3]), q.dtype)

            def step(S, inp):
                q_t, k_t, v_t, g_t, b_t = inp
                S = S * jnp.exp(g_t)[..., None, None]
                u = (v_t - jnp.einsum('bhk,bhkv->bhv', k_t, S)) * b_t[..., None]
                S = S + jnp.einsum('bhk,bhv->bhkv', k_t, u)
                o_t = jnp.einsum('bhk,bhkv->bhv', q_t, S)
                return (S, o_t)
            _, oT = lax.scan(step, S0, (qT, kT, vT, gT, bT))
            return oT.transpose(1, 0, 2, 3)
        Bx, Tx = (x.shape[0], x.shape[1])
        q = short_conv(x @ Wq, conv_q).reshape(Bx, Tx, H, DK)
        k = short_conv(x @ Wk, conv_k).reshape(Bx, Tx, H, DK)
        v = short_conv(x @ Wv, conv_v).reshape(Bx, Tx, H, DV)
        beta = jax.nn.sigmoid(x @ Wb)
        g = -jnp.exp(A_log) * jax.nn.softplus(x @ Wa + dt_bias)
        o = gated_delta_rule(q, k, v, g, beta)
        gv = (x @ Wg).reshape(Bx, Tx, H, DV)
        o = o * lax.rsqrt(jnp.mean(o * o, axis=-1, keepdims=True) + EPS) * norm_w
        o = o * jax.nn.silu(gv)
        return o.reshape(Bx, Tx, H * DV) @ Wo

    def _L1_ffn_ref(x, Wq, bq, Wk, bk, Wv, bv, Wo, bo, Wg, bg, W1, b1, W2, b2):
        import jax, jax.numpy as jnp
        import numpy as np
        B, S, H, D, E = (4, 128, 128, 512, 8)
        q = x @ Wq + bq
        k = x @ Wk + bk
        v = x @ Wv + bv
        scale = jnp.asarray(1.0 / np.sqrt(H), x.dtype)
        scores = jnp.einsum('bqh,bkh->bqk', q, k) * scale
        attn = jax.nn.softmax(scores, axis=-1)
        a = jnp.einsum('bqk,bkh->bqh', attn, v) @ Wo + bo
        x = x + a
        gates = jax.nn.softmax(x @ Wg + bg, axis=-1)
        hmid = jax.nn.relu(jnp.einsum('bsh,ehd->bsed', x, W1) + b1)
        eout = jnp.einsum('bsed,edh->bseh', hmid, W2) + b2
        y = jnp.einsum('bse,bseh->bsh', gates, eout)
        return x + y
    x = L0_attn_x
    mod = (_silu(L0_c) @ L0_wmod).reshape(L0_c.shape[0], 6, 1, -1)
    sa, ca, ga, sb, cb, gb = (mod[:, 0], mod[:, 1], mod[:, 2], mod[:, 3], mod[:, 4], mod[:, 5])
    ga = (2 * (ga >= 0) - 1) * jnp.maximum(jnp.abs(ga), 0.25)
    gb = (2 * (gb >= 0) - 1) * jnp.maximum(jnp.abs(gb), 0.25)
    h = _layernorm(x, axis=-1) * (1 + ca) + sa
    x = x + ga * _L0_attn_ref(h, L0_attn_W_in, L0_attn_conv_w, L0_attn_conv_b, L0_attn_W_xproj, L0_attn_W_dt, L0_attn_b_dt, L0_attn_A_log, L0_attn_D_skip, L0_attn_W_out)
    h = _layernorm(x, axis=-1) * (1 + cb) + sb
    x = x + gb * _L0_ffn_ref(h, L0_ffn_routing_W, L0_ffn_expert_bias, L0_ffn_sW1, L0_ffn_sb1, L0_ffn_sW2, L0_ffn_sb2, L0_ffn_rW1, L0_ffn_rb1, L0_ffn_rW2, L0_ffn_rb2)
    mod = (_silu(L1_c) @ L1_wmod).reshape(L1_c.shape[0], 6, 1, -1)
    sa, ca, ga, sb, cb, gb = (mod[:, 0], mod[:, 1], mod[:, 2], mod[:, 3], mod[:, 4], mod[:, 5])
    ga = (2 * (ga >= 0) - 1) * jnp.maximum(jnp.abs(ga), 0.25)
    gb = (2 * (gb >= 0) - 1) * jnp.maximum(jnp.abs(gb), 0.25)
    h = _layernorm(x, axis=-1) * (1 + ca) + sa
    x = x + ga * _L1_attn_ref(h, L1_attn_Wq, L1_attn_Wk, L1_attn_Wv, L1_attn_conv_q, L1_attn_conv_k, L1_attn_conv_v, L1_attn_Wb, L1_attn_Wa, L1_attn_A_log, L1_attn_dt_bias, L1_attn_Wg, L1_attn_norm_w, L1_attn_Wo)
    h = _layernorm(x, axis=-1) * (1 + cb) + sb
    x = x + gb * _L1_ffn_ref(h, L1_ffn_Wq, L1_ffn_bq, L1_ffn_Wk, L1_ffn_bk, L1_ffn_Wv, L1_ffn_bv, L1_ffn_Wo, L1_ffn_bo, L1_ffn_Wg, L1_ffn_bg, L1_ffn_W1, L1_ffn_b1, L1_ffn_W2, L1_ffn_b2)
    return x

_drawn_inputs = setup_inputs


def setup_inputs(seed=0):
    import zlib

    import numpy as np

    out = dict(_drawn_inputs(seed))
    spreads = {'L0_attn_D_skip': (1.0, 0.6),
     'L0_ffn_expert_bias': (0.0, 0.348),
     'L0_ffn_sb1': (0.0, 0.8),
     'L0_ffn_sb2': (0.0, 0.282),
     'L0_ffn_rb1': (0.0, 0.8),
     'L0_ffn_rb2': (0.0, 0.1),
     'L1_attn_norm_w': (1.0, 0.6),
     'L1_ffn_bq': (0.0, 2.0),
     'L1_ffn_bk': (0.0, 2.0),
     'L1_ffn_bv': (0.0, 0.331),
     'L1_ffn_bo': (0.0, 0.323),
     'L1_ffn_bg': (0.0, 0.8),
     'L1_ffn_b1': (0.0, 0.8),
     'L1_ffn_b2': (0.0, 0.658)}
    factors = {'L0_attn_conv_b': 8.0,
     'L0_attn_A_log': 2.712,
     'L0_ffn_sW1': 8.0,
     'L0_ffn_sW2': 8.0,
     'L0_ffn_rW1': 8.0,
     'L0_ffn_rW2': 8.0,
     'L1_attn_Wq': 8.0,
     'L1_attn_Wk': 8.0,
     'L1_attn_Wv': 8.0,
     'L1_attn_conv_q': 8.0,
     'L1_attn_conv_k': 8.0,
     'L1_attn_conv_v': 8.0,
     'L1_attn_Wb': 8.0,
     'L1_attn_Wa': 8.0,
     'L1_attn_A_log': 8.0,
     'L1_attn_dt_bias': 8.0,
     'L1_attn_Wg': 8.0,
     'L1_attn_Wo': 8.0}
    for name, (base, spread) in spreads.items():
        noise = np.random.default_rng([zlib.crc32(name.encode()), seed]).standard_normal(out[name].shape)
        drawn = base * np.exp(spread * noise) if base else spread * noise
        out[name] = jnp.asarray(drawn.astype(out[name].dtype))
    for name, factor in factors.items():
        out[name] = (out[name] * factor).astype(out[name].dtype)
    return out
```

```python
from contextlib import ExitStack

import numpy as np
import concourse.bass as bass
from concourse import mybir

F32 = mybir.dt.float32
BF16 = mybir.dt.bfloat16
U32 = mybir.dt.uint32
ALU = mybir.AluOpType
ACT = mybir.ActivationFunctionType
X = mybir.AxisListType.X

P = 128
T = 256
TILES = T // P
D = 128
CB = 2
TAPS = 4
NS = 16
RANK = 8
SG = 4
NG = NS // SG
E0 = 8
H0 = 64
BLK0 = 5
NH = 8
DV = 32
HG = 4
GROUPS = TILES * NH // HG
LEVELS = [2, 4, 8, 16, 32, 64]
E1 = 8
HB1 = 4
LN_EPS = 1e-5
L2_EPS = 1e-6
RMS_EPS = 1e-5
SP_STEPS = 13
LOG1P_TERMS = 7

C_ID = 0
C_MASK2 = 128
C_MERGE = 256
C_GT = C_MERGE + 128 * len(LEVELS)
C_LE = C_GT + 128
C_HIDE = C_LE + 128
C_SEL = C_HIDE + 128
C_IOTA = C_SEL + 4 * 128
C_LT = C_IOTA + 8
C_N = C_LT + 128


def constants():
    c = np.zeros((P, C_N), np.float32)
    r = np.arange(P)
    row, col = r[:, None], r[None, :]
    c[:, C_ID:C_ID + P] = row == col
    c[:, C_MASK2:C_MASK2 + P] = (col % 2 == 1) & (row == col - 1)
    for n, s in enumerate(LEVELS):
        low = (row // (2 * s) == col // (2 * s)) & (row // s % 2 == 1) & (col // s % 2 == 0)
        c[:, C_MERGE + n * P:C_MERGE + (n + 1) * P] = low | (row == col)
    c[:, C_GT:C_GT + P] = row > col
    c[:, C_LE:C_LE + P] = row <= col
    c[:, C_HIDE:C_HIDE + P] = np.where(col < row, -32768.0, 0.0)
    for m in range(4):
        c[:E0, C_SEL + m * P:C_SEL + (m + 1) * P] = r[:E0, None] == 2 * m + (col // H0)
    c[:, C_IOTA:C_IOTA + 8] = np.arange(8)
    c[:, C_LT:C_LT + P] = row < col
    return c


class Signal:

    def __init__(self, handle, n):
        self.h, self.n = handle, n

    def wait(self, eng, i, k):
        assert k > 0
        eng.wait_ge(self.h, i * self.n + k)

    def wait_apart(self, eng, i, k, carrier):
        self.wait(eng, i, k)
        eng.tensor_copy(*carrier)


def build(nc, a, out, NB):
    with ExitStack() as ctx:
        def sb(name, shape, dt=F32):
            return ctx.enter_context(nc.sbuf_tensor(name, shape, dt))

        def sem(name):
            return ctx.enter_context(nc.semaphore(name))

        def sig(name, n=1):
            return Signal(sem(name), n)

        PS = ctx.enter_context(nc.psum_tensor("banks", [P, 8, 512], F32))

        def bank(n, w=512, at=0):
            return PS[:, n, at:at + w]

        con = sb("con", [P, C_N])
        ident = con[:, C_ID:C_ID + P]
        zero_col = con[:, C_LT:C_LT + 1]
        carrier = (sb("carried", [P, 1])[:], zero_col)
        identb = sb("identb", [P, P], BF16)
        hideb = sb("hideb", [P, P], BF16)
        w_in = sb("w_in", [D, 4 * P])
        conv0 = sb("conv0", [P, CB, TAPS])
        conv0b = sb("conv0b", [P, CB])
        w_bc = sb("w_bc", [P, CB, 2 * NS])
        w_rank = sb("w_rank", [P, CB, RANK])
        w_dt = sb("w_dt", [RANK, CB * P])
        b_dt = sb("b_dt", [P, CB])
        a_neg = sb("a_neg", [P, CB, NS])
        d_half = sb("d_half", [P, CB])
        w_out = sb("w_out", [P, CB, D])
        rout_w = sb("rout_w", [D, E0])
        rout_b = sb("rout_b", [P, E0])
        up0 = sb("up0", [D, 9 * H0])
        up0b = sb("up0b", [P, BLK0])
        down0 = sb("down0", [P, BLK0, D])
        down0b = sb("down0b", [9, D])
        w_k = sb("w_k", [D, NH * P])
        w_q = sb("w_q", [D, NH * P])
        w_v = sb("w_v", [D, NH * DV])
        w_g = sb("w_g", [D, NH * DV])
        conv1 = sb("conv1", [P, 18, TAPS])
        w_ba = sb("w_ba", [D, 2 * NH])
        expA = sb("expA", [P, NH])
        dt_bias = sb("dt_bias", [P, NH])
        norm_half = sb("norm_half", [P, DV])
        w_o1 = sb("w_o1", [P, 2, D])
        at_w = sb("at_w", [D, 4, D])
        at_b = sb("at_b", [D, 4])
        gate_w = sb("gate_w", [D, E1])
        gate_b = sb("gate_b", [P, E1])
        up1 = sb("up1", [D, E1, HB1 * P])
        up1b = sb("up1b", [P, E1 * HB1])
        down1 = sb("down1", [P, E1 * HB1, D])
        down1b = sb("down1b", [E1, D])
        ones_col = sb("ones_col", [P, 1])
        expo = sb("expo", [P, 2])
        cT = sb("cT", [D, 2, NB])
        shift_scale = sb("shift_scale", [D, 8, NB])
        gates = sb("gates", [NB, 4, D])
        gates_bc = sb("gates_bc", [P, 4, D])
        gates_dram = nc.dram_tensor("gate_rows", (NB, 4 * D), F32, kind="Internal").ap()

        x = [sb(f"x{n}", [P, TILES, D]) for n in range(5)]
        stats = sb("stats", [P, TILES, 6])
        mv = sb("mv", [P, TILES, 2])
        xn = sb("xn", [P, TILES, D])
        hT = sb("hT", [D, T])
        res = sb("res", [P, TILES, D])

        pad0 = sb("pad0", [P, CB, T + 3])
        kq = sb("kq", [P, NH, 2, T])
        xc, th, u2, zs, vb, ev, dt, dtu = [kq[:, n] for n in range(8)]
        bc_sb = sb("bc_sb", [2 * NS, T])
        rank_sb = sb("rank_sb", [RANK, T])
        big = sb("big", [P, 12, SG * T])
        wmod = big[:, 0:2, 0:6 * D]
        decay = [big[:, n, :] for n in (0, 1)]
        drive = [big[:, n, :] for n in (2, 3)]
        state = [big[:, n, :] for n in (4, 5)]
        read = [big[:, n, :] for n in (6, 7)]
        c_sb = [big[:, n, :] for n in (8, 9, 10, 11)]
        ysT = sb("ysT", [P, CB, T])

        sp = sb("sp", [P, 10, 16])
        lg = sb("lg", [P, TILES, E0])
        top = sb("top", [P, TILES, 8])
        topi = sb("topi", [P, TILES, 8], U32)
        topf = sb("topf", [P, TILES, 8])
        pick = sb("pick", [P, TILES, 2, E0])
        cf = sb("cf", [P, TILES, 9])
        cfT = sb("cfT", [9, T])
        half0, thh, mix0 = [kq[:, n] for n in (4, 5, 6)]
        hs0 = kq[:, 0:3].rearrange("p a b t -> p (a b) t")[:, 0:BLK0]

        pad1 = [sb(f"pad1_{n}", [P, 2, T + 3]) for n in range(2)]
        xc1 = [sb(f"xc1_{n}", [P, 2, T]) for n in range(2)]
        th1 = [sb(f"th1_{n}", [P, 2, T]) for n in range(2)]
        v2 = sb("v2", [P, 2, T])
        sq = [sb(f"sq{n}", [P, 2, T]) for n in range(2)]
        ssq = sb("ssq", [P, 2, TILES, NH])
        rq = sb("rq", [P, TILES, NH])
        rk2 = sb("rk2", [P, TILES, NH])
        vscale = sb("vscale", [P, TILES, NH])
        beta = sb("beta", [P, TILES, NH])
        bax = sb("bax", [P, TILES, 2 * NH])
        gl = sb("gl", [P, TILES, NH])
        cU = sb("cU", [P, TILES, NH])
        negc = sb("negc", [P, TILES, NH])
        eGS = sb("eGS", [P, TILES, 2, NH])
        gmask = [big[:, 10 + n, 512:1024].rearrange("p (h t) -> p h t", t=P) for n in range(2)]
        et = [sb(f"ets{n}", [P, HG, P]) for n in range(2)]
        MT = [big[:, n, 0:512].rearrange("p (h t) -> p h t", t=P) for n in range(4)]
        AT = [big[:, n, 512:1024].rearrange("p (h t) -> p h t", t=P) for n in range(4)]
        TT = [big[:, 4 + n, 0:512].rearrange("p (h t) -> p h t", t=P) for n in range(4)]
        TN = [big[:, 4 + n, 512:1024].rearrange("p (h t) -> p h t", t=P) for n in range(4)]
        WW = [big[:, 8 + n, 0:512].rearrange("p (h t) -> p h t", t=P) for n in range(4)]
        ktok = [big[:, 8 + n, 512:1024].rearrange("p (h d) -> p h d", d=P) for n in range(2)]
        vtok = sb("vtok", [P, TILES, NH, DV])
        gv = sb("gv", [P, TILES, NH * DV])
        gvt = sb("gvt", [P, TILES, NH * DV])
        gnw = sb("gnw", [P, TILES, NH * DV])
        R = sb("R", [P, NH, DV])
        kSd = sb("kSd", [P, NH, DV])
        U = sb("U", [P, NH, DV])
        Uw = sb("Uw", [P, NH, DV])
        S1 = sb("S1", [P, NH, DV])
        ou = sb("ou", [P, TILES, NH, DV])
        o2s = sb("o2s", [P, NH, DV])
        osq = sb("osq", [P, TILES, NH, DV])
        rms = sb("rms", [P, TILES, NH])
        og = sb("og", [P, TILES, NH * DV])
        oT = sb("oT", [P, 2, T])

        qkT, prob, probT = [kq[:, n] for n in range(3)]
        avT, xxT = kq[:, 3, 0], kq[:, 3, 1]
        v_sb = sb("v_sb", [P, TILES, D])
        smax = sb("smax", [P, 4])
        ssum = sb("ssum", [P, 4])
        gt = sb("gt", [P, TILES, E1])
        gm = sb("gm", [P, 4])
        gT = sb("gT", [E1, T])
        yacc = sb("yacc", [P, TILES, D])
        hm = [big[:, n, :].rearrange("p (m t) -> p m t", t=T) for n in range(2)]

        loaded = sem("weights_loaded")
        mod_done = sem("modulation_products")
        silu_c = sem("silu_of_c")
        prep_act = sem("prologue_scalar")
        prep_dve = sem("prologue_vector")
        prep_pool = sem("prologue_pool")
        gates_stored = sem("gate_rows_stored")

        x_loaded = sig("x_loaded", 16)
        out_stored = sig("out_stored", 16)
        out_ready = sig("out_ready")
        gate_loaded = sig("gate_loaded", 16)
        vch = {}

        def chain(name, n):
            vch[name] = sig("v_" + name, n)
            return vch[name]

        ln_step = chain("ln", 4 * 5)
        ln_var = sig("ln_variance", 4)
        ln_rstd = sig("ln_rstd", 4)
        ln_x = sig("ln_normalised", 4)
        ln_t = sig("ln_transposed", 4)
        ln_h = sig("ln_modulated", 4)
        res_v = sig("gated_branch", 4)
        x_new = sig("x_new", 3)
        a_xi = sig("a_xi_ps"); a_z = sig("a_z_ps")
        a_pad = sig("a_pad"); a_zth = sig("a_zth"); a_zs = sig("a_zs")
        a_conv = sig("a_conv", CB * TAPS); a_uth = sig("a_uth"); a_u = sig("a_u")
        a_bcp = sig("a_bc_ps"); a_bc = sig("a_bc", 2); a_dtp = sig("a_dt_ps")
        a_vb = sig("a_vb", 2); a_na = sig("a_neg_abs"); a_e = sig("a_exp"); a_ln = sig("a_log")
        a_zero = sig("a_decay_zeroed")
        a_dt = sig("a_dt"); a_dtu = sig("a_dtu")
        a_B = sig("a_B_spread", NG); a_C = sig("a_C_spread", NG); a_Cs = sig("a_C_copied", NG)
        a_dec = sig("a_decay", NG * CB); a_drv = sig("a_drive", NG * CB)
        a_h = sig("a_state", NG * CB); a_rd = sig("a_read", NG * CB)
        a_y = sig("a_y_summed", NG * CB); a_y1 = sig("a_y_skip", 2); a_ys = sig("a_y_gated", 2)
        a_out = sig("a_out_ps")
        sp_in = sig("sp_neg_abs", 2); sp_e = sig("sp_exp", 2)
        sp_step = chain("sp", 2 * SP_STEPS)
        b_lgp = sig("b_logits_ps"); b_lg = chain("b_logits", 1)
        b_sel = chain("b_select", 4); b_root = sig("b_root"); b_cf = sig("b_cf"); b_cfTp = sig("b_cfT_ps"); b_cfT = sig("b_cfT")
        b_up = sig("b_up_ps", BLK0); b_cfb = sig("b_cf_spread", 4)
        b_half = sig("b_half", BLK0); b_th = sig("b_tanh", BLK0)
        b_mix = sig("b_mix", 4); b_hs = sig("b_hidden", BLK0); b_out = sig("b_out_ps")
        c_bap = sig("c_ba_ps"); c_ba = chain("c_ba", 1); c_ebeta = sig("c_exp_beta")
        c_b1 = chain("c_beta", 3); c_g = sig("c_g"); c_dec = sig("c_decay_ps"); c_eGS = sig("c_decay_exp")
        c_gvp = sig("c_gv_ps"); c_gvt = sig("c_gv_tanh"); c_gv = sig("c_gv"); c_gnw = sig("c_gate")
        c_pp = sig("c_proj_ps", 9); c_pad = sig("c_pad", 9); c_conv = sig("c_conv", 72)
        c_th = sig("c_tanh", 9); c_kq = sig("c_silu", 9); c_sq = sig("c_squares", 8)
        c_ssp = sig("c_ssq_ps", 8); c_ss = chain("c_scales", 6); c_root = sig("c_roots", 2)
        c_vt = sig("c_v_turned"); c_vtok = sig("c_v_tokens")
        c_kt = sig("c_k_turned", 2); c_ktok = sig("c_k_tokens", 2)
        c_gm = sig("c_gmask", GROUPS); c_D = sig("c_logdecay_ps", GROUPS); c_et = sig("c_decay_matrix", GROUPS)
        c_kk = sig("c_kk_ps", 2 * GROUPS); c_MT = sig("c_MT_heads", 4 * GROUPS); c_AT = sig("c_AT", 2 * GROUPS)
        c_t2 = sig("c_T2_step", 2 * GROUPS); c_MTs = sig("c_MT_strict", GROUPS)
        NL = len(LEVELS)
        c_Z = sig("c_Z_ps", NL * GROUPS); c_W = sig("c_W", NL * GROUPS)
        c_TTp = sig("c_TT_ps", NL * GROUPS); c_TT = sig("c_TT", NL * GROUPS)
        c_Tp = sig("c_T_ps", NL * GROUPS); c_T = sig("c_T", NL * GROUPS)
        c_kS = sig("c_kS_ps"); c_R = chain("c_R", 5)
        c_X = sig("c_X_ps", 2); c_U = sig("c_U", 2); c_Uw = sig("c_Uw")
        c_Sp = sig("c_S_ps"); c_S = sig("c_S"); c_O = sig("c_O_ps", 2); c_O2 = sig("c_O2_ps")
        c_o = chain("c_o", 4); c_osq = sig("c_osq"); c_rms = chain("c_rms", 3); c_rrms = sig("c_rrms"); c_og = sig("c_og")
        c_oTp = sig("c_oT_ps"); c_oT = sig("c_oT"); c_out = sig("c_out_ps")
        d_qk = sig("d_qk_ps"); d_qks = sig("d_qk", 2); d_vp = sig("d_v_ps"); d_v = sig("d_v")
        d_sc = sig("d_scores_ps"); d_mx = chain("d_max", 2); d_e = sig("d_exp", 2); d_rs = chain("d_rsum", 1)
        d_p = sig("d_prob", 2); d_pT = sig("d_probT_ps"); d_pTs = sig("d_probT"); d_avp = sig("d_av_ps")
        d_av = sig("d_av"); d_ap = sig("d_a_ps"); d_xx = sig("d_xx"); d_glp = sig("d_gate_ps")
        d_g1 = chain("d_gate", 4); d_ge = sig("d_gate_exp"); d_gt = chain("d_gate2", 4)
        d_gTp = sig("d_gateT_ps"); d_gT = sig("d_gateT"); d_yi = sig("d_yinit_ps"); d_y0 = sig("d_yinit")
        d_up = sig("d_up_ps", 2 * E1); d_hma = sig("d_hidden_act", 2 * E1); d_hmv = sig("d_hidden_dve", 2 * E1)
        d_eo = sig("d_expert_ps", E1); d_acc = sig("d_mixed", 2 * E1)

        block = ctx.enter_context(nc.Block())
        loads = [
            (con[:], a["con"]), (cT[:, 0, :], a["c0T"]), (cT[:, 1, :], a["c1T"]),
            (wmod[:, 0, :], a["wmod0"]), (wmod[:, 1, :], a["wmod1"]),
            (w_in[:], a["w_inT"]),
            (conv0[:], a["conv_w0"].rearrange("(c p) k -> p c k", p=P)),
            (conv0b[:], a["conv_b0"]),
            (w_bc[:], a["w_xT"].rearrange("(c p) e -> p c e", p=P)[:, :, RANK:RANK + 2 * NS]),
            (w_rank[:], a["w_xT"].rearrange("(c p) e -> p c e", p=P)[:, :, 0:RANK]),
            (w_dt[:], a["w_dtT"]), (b_dt[:], a["b_dt"]),
            (a_neg[:], a["A_log0"].rearrange("(c p) s -> p c s", p=P)),
            (d_half[:], a["D_skip"]),
            (w_out[:], a["w_outT"].rearrange("(c p) d -> p c d", p=P)),
            (rout_w[:], a["routT"]), (rout_b[:], a["exp_bias"].partition_broadcast(P)),
            (up0[:], a["up0"]), (up0b[:], a["up0b"]), (down0[:], a["down0"].rearrange("(m p) d -> p m d", p=P)),
            (down0b[:], a["down0b"]),
            (w_k[:], a["Wk1"]), (w_q[:], a["Wq1"]), (w_v[:], a["Wv1"]), (w_g[:], a["Wg1"]),
            (conv1[:], a["conv1"].rearrange("(m p) k -> p m k", p=P)),
            (w_ba[:, 0:NH], a["Wb1"]), (w_ba[:, NH:2 * NH], a["Wa1"]),
            (expA[:], a["A_log1"].partition_broadcast(P)), (dt_bias[:], a["dt_bias1"].partition_broadcast(P)),
            (norm_half[:], a["norm_w"].partition_broadcast(P)),
            (w_o1[:], a["Wo1"].rearrange("(c p) d -> p c d", p=P)),
            (at_w[:, 0, :], a["fWq"]), (at_w[:, 1, :], a["fWk"]), (at_w[:, 2, :], a["fWv"]), (at_w[:, 3, :], a["fWo"]),
            (at_b[:], a["fb"]), (gate_w[:], a["fWg"]), (gate_b[:], a["fbg"].partition_broadcast(P)),
            (up1[:], a["W1"].rearrange("e d f -> d e f")),
            (up1b[:], a["b1"]),
            (down1[:], a["W2"].rearrange("e (m p) d -> p (e m) d", p=P)),
            (down1b[:], a["b2"]),
        ]
        LOADED = 16 * len(loads)

        @block.sync
        def _(sp_):
            for dst, src in loads:
                sp_.dma_start(dst, src).then_inc(loaded, 16)
            sp_.wait_ge(prep_dve, 12)
            sp_.dma_start(gates_dram, gates[:].rearrange("b n d -> b (n d)")).then_inc(gates_stored, 16)
            sp_.wait_ge(gates_stored, 16)

            def load_x(i):
                sp_.dma_start(x[0][:], a["x"][bass.ds(i, 1), :, :].rearrange("b (t p) d -> p (b t) d", p=P)).then_inc(x_loaded.h, 16)

            def load_gates(i):
                sp_.dma_start(gates_bc[:].rearrange("p n d -> p (n d)"),
                              gates_dram[bass.ds(i, 1), :].rearrange("b e -> (b e)").partition_broadcast(P)).then_inc(gate_loaded.h, 16)

            def store(i):
                sp_.dma_start(out[bass.ds(i, 1), :, :].rearrange("b (t p) d -> p (b t) d", p=P), x[4][:]).then_inc(out_stored.h, 16)

            load_x(0)
            load_gates(0)
            with sp_.Fori(0, NB - 1) as i:
                x_new.wait(sp_, i, 1)
                load_x(i + 1)
                out_ready.wait(sp_, i, 1)
                store(i)
                out_stored.wait(sp_, i, 16)
                load_gates(i + 1)
            sp_.wait_ge(out_ready.h, NB)
            store(NB - 1)
            sp_.wait_ge(out_stored.h, 16 * NB)

        @block.gpsimd
        def _(g):
            g.wait_ge(loaded, LOADED)
            g.memset(ones_col[:], 1.0)
            g.memset(expo[:, 0:1], -0.5)
            g.memset(expo[:, 1:2], 0.5)
            g.memset(pad0[:], 0.0)
            for n in range(2):
                g.memset(pad1[n][:], 0.0)
            for n in range(TILES):
                g.memset(cf[:, n, 8:9], 1.0)
            g.tensor_copy(identb[:], ident)
            g.tensor_copy(hideb[:], con[:, C_HIDE:C_HIDE + P]).then_inc(prep_pool, 1)
            g.wait_ge(prep_pool, 1)
            with g.Fori(0, NB) as i:
                def power(io, which):
                    n = io.free_size()
                    return g.tensor_tensor(io, io, expo[:, which:which + 1].broadcast_to([P, n]), ALU.pow)

                def rstd(n):
                    ln_var.wait(g, i, n + 1)
                    power(mv[:, :, 1], 0).then_inc(ln_rstd.h, 1)

                rstd(0)
                ln_t.wait(g, i, 1)
                for n in range(2):
                    last = g.tensor_tensor(decay[n].rearrange("p (q t) -> p q t", t=T)[:, :, 0:1],
                                         *[zero_col.unsqueeze(1).broadcast_to([P, SG, 1])] * 2, ALU.mult)
                last.then_inc(a_zero.h, 1)
                for s in range(NG * CB):
                    a_h.wait(g, i, s + 1)
                    a_Cs.wait(g, i, s // CB + 1)
                    if s >= 2:
                        a_y.wait(g, i, s - 1)
                    g.tensor_tensor(read[s % 2], state[s % 2], c_sb[s // CB], ALU.mult).then_inc(a_rd.h, 1)
                rstd(1)
                sp_step.wait(g, i, SP_STEPS)
                g.tensor_tensor(lg[:].rearrange("p j e -> p (j e)"), sp[:, 0, :], expo[:, 1:2].broadcast_to([P, TILES * E0]),
                                ALU.pow).then_inc(b_root.h, 1)
                rstd(2)
                for m in range(8):
                    c_kq.wait(g, i, m + 1)
                    if m >= 2:
                        c_ssp.wait(g, i, m - 1)
                    g.tensor_tensor(sq[m % 2][:], kq[:, m, :, :], kq[:, m, :, :], ALU.mult).then_inc(c_sq.h, 1)
                c_gv.wait(g, i, 1)
                g.tensor_tensor(gnw[:].rearrange("p c (h v) -> p (c h) v", v=DV), gv[:].rearrange("p c (h v) -> p (c h) v", v=DV),
                                norm_half[:].unsqueeze(1).broadcast_to([P, TILES * NH, DV]), ALU.mult).then_inc(c_gnw.h, 1)
                c_g.wait(g, i, 1)
                for gr in range(GROUPS):
                    ch, hg = gr // 2, gr % 2
                    if gr >= 2:
                        c_D.wait(g, i, gr - 1)
                    g.tensor_tensor(gmask[gr % 2], gl[:, ch, hg * HG:(hg + 1) * HG].unsqueeze(2).broadcast_to([P, HG, P]),
                                    con[:, C_LE:C_LE + P].unsqueeze(1).broadcast_to([P, HG, P]), ALU.mult).then_inc(c_gm.h, 1)
                c_ss.wait(g, i, 4)
                power(vscale[:].rearrange("p c h -> p (c h)"), 1).then_inc(c_root.h, 1)
                power(rq[:].rearrange("p c h -> p (c h)"), 0).then_inc(c_root.h, 1)
                for gr in range(GROUPS):
                    c_MT.wait(g, i, 4 * gr + 4)
                    g.tensor_tensor(MT[gr], MT[gr], con[:, C_LT:C_LT + P].unsqueeze(1).broadcast_to([P, HG, P]), ALU.mult).then_inc(c_MTs.h, 1)
                c_o.wait(g, i, 4)
                g.tensor_tensor(osq[:], ou[:], ou[:], ALU.mult).then_inc(c_osq.h, 1)
                c_rms.wait(g, i, 2)
                power(rms[:].rearrange("p c h -> p (c h)"), 0).then_inc(c_rrms.h, 1)
                rstd(3)

        @block.scalar
        def _(s):
            s.wait_ge(loaded, LOADED)
            s.activation(xc[:, 0, 0:2 * NB].rearrange("p (l b) -> p l b", l=2), cT[:], ACT.Exp, scale=-1.0).then_inc(silu_c, 1)
            s.activation(a_neg[:], a_neg[:], ACT.Exp).then_inc(prep_act, 1)
            s.activation(expA[:], expA[:], ACT.Exp).then_inc(prep_act, 1)
            s.wait_ge(prep_act, 2)
            s.mul(a_neg[:], a_neg[:], -1.0).then_inc(prep_act, 1)
            s.mul(expA[:], expA[:], -1.0).then_inc(prep_act, 1)
            s.mul(d_half[:], d_half[:], 0.5).then_inc(prep_act, 1)
            s.mul(norm_half[:], norm_half[:], 0.5).then_inc(prep_act, 1)
            s.mul(up0b[:], up0b[:], 0.5).then_inc(prep_act, 1)
            s.wait_ge(prep_act, 7)
            s.wait_ge(prep_pool, 1)
            s.wait_ge(prep_dve, 12)
            with s.Fori(0, NB) as i:
                def modulate(n):
                    ln_t.wait(s, i, n + 1)
                    s.activation(hT[:], bank(0, T), ACT.Identity, bias=shift_scale[:, 2 * n, bass.ds(i, 1)],
                                 scale=shift_scale[:, 2 * n + 1, bass.ds(i, 1)]).then_inc(ln_h.h, 1)

                modulate(0)
                a_xi.wait(s, i, 1)
                s.copy(pad0[:, :, 3:3 + T], bank(1).rearrange("p (c t) -> p c t", c=CB)).then_inc(a_pad.h, 1)
                a_z.wait(s, i, 1)
                s.activation(th, bank(2).rearrange("p (c t) -> p c t", c=CB), ACT.Tanh, scale=0.5).then_inc(a_zth.h, 1)
                a_conv.wait(s, i, CB * TAPS)
                a_zs.wait(s, i, 1)
                s.activation(th, xc, ACT.Tanh, scale=0.5).then_inc(a_uth.h, 1)
                a_bcp.wait(s, i, 1)
                s.mul(bc_sb[:], PS[0:2 * NS, 3, 0:T], 0.5).then_inc(a_bc.h, 1)
                s.mul(rank_sb[:], PS[0:RANK, 3, T:2 * T], 0.5).then_inc(a_bc.h, 1)
                a_na.wait(s, i, 1)
                s.activation(ev, ev, ACT.Exp).then_inc(a_e.h, 1)
                a_e.wait(s, i, 1)
                s.activation(ev, ev, ACT.Ln, bias=1.0).then_inc(a_ln.h, 1)
                a_dt.wait(s, i, 1)
                for st in range(NG * CB):
                    gq, cb = st // CB, st % CB
                    if cb == 0:
                        a_C.wait(s, i, gq + 1)
                        s.copy(c_sb[gq], PS[:, 4:6, :].rearrange("p a b -> p (a b)")).then_inc(a_Cs.h, 1)
                    if st >= 2:
                        a_h.wait(s, i, st - 1)
                    for q in range(SG):
                        last = s.activation(decay[st % 2][:, q * T + 1:(q + 1) * T], dt[:, cb, 1:T], ACT.Exp,
                                            scale=a_neg[:, cb, gq * SG + q:gq * SG + q + 1])
                    last.then_inc(a_dec.h, 1)

                modulate(1)
                sp_in.wait(s, i, 1)
                s.activation(sp[:, 1, :], sp[:, 1, :], ACT.Exp).then_inc(sp_e.h, 1)
                for m in range(BLK0):
                    M = P if m < 4 else H0
                    b_up.wait(s, i, m + 1)
                    if m >= 2:
                        b_hs.wait(s, i, m - 1)
                    s.activation(half0[0:M, m % 2, :], PS[0:M, 2 + m % 2, 0:T], ACT.Identity, bias=up0b[0:M, m:m + 1],
                                 scale=0.5).then_inc(b_half.h, 1)
                    b_half.wait(s, i, m + 1)
                    s.activation(thh[0:M, m % 2, :], half0[0:M, m % 2, :], ACT.Tanh).then_inc(b_th.h, 1)

                modulate(2)
                c_ba.wait(s, i, 1)
                s.activation(beta[:], bax[:, :, 0:NH], ACT.Exp, scale=-1.0).then_inc(c_ebeta.h, 1)
                c_gvp.wait(s, i, 1)
                s.activation(gvt[:], bank(2).rearrange("p (c v) -> p c v", c=TILES), ACT.Tanh, scale=0.5).then_inc(c_gvt.h, 1)
                sp_in.wait(s, i, 2)
                s.activation(sp[:, 1, :], sp[:, 1, :], ACT.Exp).then_inc(sp_e.h, 1)

                def silu_tanh(m):
                    c_conv.wait(s, i, 8 * (m + 1))
                    s.activation(th1[m % 2][:], xc1[m % 2][:], ACT.Tanh, scale=0.5).then_inc(c_th.h, 1)

                for m in range(9):
                    c_pp.wait(s, i, m + 1)
                    if m >= 2:
                        c_conv.wait(s, i, 8 * (m - 1))
                    s.copy(pad1[m % 2][:, :, 3:3 + T], bank(3 + m % 2).rearrange("p (c t) -> p c t", c=2)).then_inc(c_pad.h, 1)
                    if m >= 1:
                        if m >= 3:
                            c_kq.wait(s, i, m - 2)
                        silu_tanh(m - 1)
                c_kq.wait(s, i, 7)
                silu_tanh(8)
                for n in range(2):
                    c_kt.wait(s, i, n + 1)
                    s.copy(ktok[n], bank(6 + n).rearrange("p (h d) -> p h d", h=4)).then_inc(c_ktok.h, 1)
                c_vt.wait(s, i, 1)
                s.copy(vtok[:].rearrange("p c h v -> p (c h v)"), bank(1)).then_inc(c_vtok.h, 1)
                c_dec.wait(s, i, 1)
                s.activation(eGS[:].rearrange("p c k h -> p (c k h)"), bank(2, 32), ACT.Exp).then_inc(c_eGS.h, 1)
                for gr in range(GROUPS):
                    c_D.wait(s, i, gr + 1)
                    if gr >= 2:
                        c_AT.wait(s, i, 2 * (gr - 1))
                    s.activation(et[gr % 2][:].rearrange("p h t -> p (h t)"), bank(gr % 2), ACT.Exp).then_inc(c_et.h, 1)
                for l in range(NL):
                    for gr in range(GROUPS):
                        n = l * GROUPS + gr
                        c_Tp.wait(s, i, n + 1)
                        s.copy(TN[gr].rearrange("p h t -> p (h t)"), bank(4 + gr % 2)).then_inc(c_T.h, 1)
                    for gr in range(GROUPS):
                        n = l * GROUPS + gr
                        c_TTp.wait(s, i, n + 1)
                        s.copy(TT[gr].rearrange("p h t -> p (h t)"), bank(2 + gr % 2)).then_inc(c_TT.h, 1)
                c_Sp.wait(s, i, 1)
                s.copy(S1[:].rearrange("p h v -> p (h v)"), bank(4, 256)).then_inc(c_S.h, 1)
                c_oTp.wait(s, i, 1)
                s.copy(oT[:].rearrange("p c t -> p (c t)"), bank(0)).then_inc(c_oT.h, 1)

                modulate(3)
                d_qk.wait(s, i, 1)
                for n in range(2):
                    s.activation(qkT[:, n, :], bank(1, T, n * T), ACT.Identity, bias=at_b[:, n:n + 1]).then_inc(d_qks.h, 1)
                d_mx.wait(s, i, 2)
                for n in range(TILES):
                    s.activation(prob[:, n, :], bank(3, T, n * T), ACT.Exp, bias=smax[:, 2 + n:3 + n], scale=float(D) ** -0.5,
                                 accum_out=ssum[:, n:n + 1]).then_inc(d_e.h, 1)
                d_pT.wait(s, i, 1)
                s.copy(probT.rearrange("p c t -> p (c t)"), bank(4)).then_inc(d_pTs.h, 1)
                d_avp.wait(s, i, 1)
                s.activation(avT, bank(5, T), ACT.Identity, bias=at_b[:, 2:3]).then_inc(d_av.h, 1)
                d_g1.wait(s, i, 4)
                s.activation(gt[:], gt[:], ACT.Exp).then_inc(d_ge.h, 1)
                d_yi.wait(s, i, 1)
                s.copy(yacc[:].rearrange("p c d -> p (c d)"), bank(5, T)).then_inc(d_y0.h, 1)
                for e in range(E1):
                    d_up.wait(s, i, 2 * e + 1)
                    if e >= 2:
                        d_eo.wait(s, i, e - 1)
                    for q in range(2):
                        s.activation(hm[e % 2][:, q, :], bank(0, T, q * T), ACT.Relu,
                                     bias=up1b[:, HB1 * e + q:HB1 * e + q + 1]).then_inc(d_hma.h, 1)

        @block.tensor
        def _(t):
            t.wait_ge(loaded, LOADED)
            t.wait_ge(prep_dve, 3)
            for l in range(2):
                for n, part in enumerate((0, 1, 3, 4)):
                    t.matmul(bank(4, NB, NB * (4 * l + n)), wmod[:, l, part * D:(part + 1) * D],
                             cT[:, l, :], start=True, stop=True)
            t.matmul(PS[0:NB, 5, 0:D], cT[:, 0, :], wmod[:, 0, 2 * D:3 * D], start=True, stop=True)
            t.matmul(PS[0:NB, 5, D:2 * D], cT[:, 0, :], wmod[:, 0, 5 * D:6 * D], start=True, stop=True)
            t.matmul(PS[0:NB, 5, 2 * D:3 * D], cT[:, 1, :], wmod[:, 1, 2 * D:3 * D], start=True, stop=True)
            t.matmul(PS[0:NB, 5, 3 * D:4 * D], cT[:, 1, :], wmod[:, 1, 5 * D:6 * D], start=True, stop=True).then_inc(mod_done, 1)
            t.wait_ge(prep_dve, 12)
            t.wait_ge(prep_act, 7)
            t.wait_ge(prep_pool, 1)
            with t.Fori(0, NB) as i:
                def turn_x(n):
                    ln_x.wait(t, i, n + 1)
                    for j in range(TILES):
                        last = t.transpose(bank(0, P, j * P), xn[:, j, :], ident)
                    last.then_inc(ln_t.h, 1)
                    ln_h.wait(t, i, n + 1)

                turn_x(0)
                for c in range(CB):
                    last = t.matmul(bank(1, T, c * T), w_in[:, c * P:(c + 1) * P], hT[:], start=True, stop=True)
                last.then_inc(a_xi.h, 1)
                for c in range(CB):
                    last = t.matmul(bank(2, T, c * T), w_in[:, (CB + c) * P:(CB + c + 1) * P], hT[:], start=True, stop=True)
                last.then_inc(a_z.h, 1)
                a_u.wait(t, i, 1)
                for c in range(CB):
                    t.matmul(PS[0:2 * NS, 3, 0:T], w_bc[:, c, :], u2[:, c, :], start=c == 0, stop=c == CB - 1)
                for c in range(CB):
                    last = t.matmul(PS[0:RANK, 3, T:2 * T], w_rank[:, c, :], u2[:, c, :], start=c == 0, stop=c == CB - 1)
                last.then_inc(a_bcp.h, 1)
                a_bc.wait(t, i, 2)
                for c in range(CB):
                    last = t.matmul(bank(4, T, c * T), w_dt[:, c * P:(c + 1) * P], rank_sb[:], start=True, stop=True)
                last.then_inc(a_dtp.h, 1)

                def spread(row, first_bank):
                    for q in range(SG):
                        r = row + q
                        last = t.matmul(PS[:, first_bank + q // 2, (q % 2) * T:(q % 2 + 1) * T],
                                        con[0:2 * NS, r:r + 1].broadcast_to([2 * NS, P]), bc_sb[:], start=True, stop=True)
                    return last

                a_zs.wait(t, i, 1)
                a_vb.wait(t, i, 2)
                spread(0, 0).then_inc(a_B.h, 1)
                spread(NS, 4).then_inc(a_C.h, 1)
                spread(SG, 2).then_inc(a_B.h, 1)
                for st in range(NG * CB):
                    gq, cb = st // CB, st % CB
                    if cb == 0 and gq + 1 < NG:
                        a_Cs.wait(t, i, gq + 1)
                        spread(NS + (gq + 1) * SG, 4).then_inc(a_C.h, 1)
                    if cb == 0 and 1 <= gq and gq + 1 < NG:
                        a_drv.wait(t, i, 2 * gq)
                        spread((gq + 1) * SG, 2 * ((gq + 1) % 2)).then_inc(a_B.h, 1)
                    a_rd.wait(t, i, st + 1)
                    for q in range(SG):
                        last = t.matmul(bank(6 + cb, T), ident, read[st % 2][:, q * T:(q + 1) * T],
                                        start=gq == 0 and q == 0, stop=gq == NG - 1 and q == SG - 1)
                    last.then_inc(a_y.h, 1)
                a_ys.wait(t, i, 2)
                for j in range(TILES):
                    for c in range(CB):
                        last = t.matmul(bank(4, D, j * D), ysT[:, c, j * P:(j + 1) * P], w_out[:, c, :],
                                        start=c == 0, stop=c == CB - 1)
                last.then_inc(a_out.h, 1)

                turn_x(1)
                for j in range(TILES):
                    last = t.matmul(bank(1, E0, j * E0), hT[:, j * P:(j + 1) * P], rout_w[:], start=True, stop=True)
                last.then_inc(b_lgp.h, 1)

                def up_block(m):
                    M = P if m < 4 else H0
                    if m >= 2:
                        b_half.wait(t, i, m - 1)
                    t.matmul(PS[0:M, 2 + m % 2, 0:T], up0[:, m * P:m * P + M], hT[:], start=True, stop=True).then_inc(b_up.h, 1)

                def spread_cf(m):
                    if m >= 2:
                        b_mix.wait(t, i, m - 1)
                    t.matmul(bank(4 + m % 2, T), con[0:E0, C_SEL + m * P:C_SEL + (m + 1) * P], cfT[0:E0, :],
                             start=True, stop=True).then_inc(b_cfb.h, 1)

                up_block(0)
                up_block(1)
                b_cf.wait(t, i, 1)
                for j in range(TILES):
                    last = t.transpose(PS[0:9, 1, j * P:(j + 1) * P], cf[:, j, :], ident)
                last.then_inc(b_cfTp.h, 1)
                b_cfT.wait(t, i, 1)
                for m in range(BLK0):
                    if m < 4:
                        spread_cf(m)
                    if m >= 2:
                        up_block(m)
                b_hs.wait(t, i, BLK0)
                for j in range(TILES):
                    for m in range(BLK0):
                        M = P if m < 4 else H0
                        t.matmul(bank(6, D, j * D), hs0[0:M, m, j * P:(j + 1) * P], down0[0:M, m, :], start=m == 0, stop=False)
                    last = t.matmul(bank(6, D, j * D), cfT[:, j * P:(j + 1) * P], down0b[:], start=False, stop=True)
                last.then_inc(b_out.h, 1)

                turn_x(2)
                for j in range(TILES):
                    last = t.matmul(bank(1, 2 * NH, j * 2 * NH), hT[:, j * P:(j + 1) * P], w_ba[:], start=True, stop=True)
                last.then_inc(c_bap.h, 1)
                for j in range(TILES):
                    last = t.matmul(bank(2, 256, j * 256), hT[:, j * P:(j + 1) * P], w_g[:], start=True, stop=True)
                last.then_inc(c_gvp.h, 1)

                def norms(m):
                    c_sq.wait(t, i, m + 1)
                    for kind in range(2):
                        for ch in range(TILES):
                            last = t.matmul(bank(5, 1, (kind * TILES + ch) * NH + m), sq[m % 2][:, kind, ch * P:(ch + 1) * P],
                                            ones_col[:], start=True, stop=True)
                    last.then_inc(c_ssp.h, 1)

                for m in range(9):
                    if m >= 2:
                        c_pad.wait(t, i, m - 1)
                    for n in range(2):
                        w = (w_k if n == 0 else w_q)[:, m * P:(m + 1) * P] if m < 8 else w_v[:, n * P:(n + 1) * P]
                        last = t.matmul(bank(3 + m % 2, T, n * T), w, hT[:], start=True, stop=True)
                    last.then_inc(c_pp.h, 1)
                for m in range(8):
                    norms(m)
                for n in range(2):
                    for h in range(4):
                        last = t.transpose(bank(6 + n, P, h * P), kq[:, 4 * n + h, 0, 0:P], ident)
                    last.then_inc(c_kt.h, 1)
                c_kq.wait(t, i, 9)
                for ch in range(TILES):
                    for n in range(2):
                        last = t.transpose(bank(1, P, ch * 256 + n * P), v2[:, n, ch * P:(ch + 1) * P], ident)
                last.then_inc(c_vt.h, 1)
                c_g.wait(t, i, 1)
                c_gv.wait(t, i, 1)
                for ch in range(TILES):
                    for n, tri in enumerate((C_LE, C_GT)):
                        last = t.matmul(bank(2, NH, (2 * ch + n) * NH), con[:, tri:tri + P], gl[:, ch, :], start=True, stop=True)
                last.then_inc(c_dec.h, 1)
                c_vtok.wait(t, i, 1)

                def log_decay(gr):
                    c_gm.wait(t, i, gr + 1)
                    if gr >= 2:
                        c_et.wait(t, i, gr - 1)
                    t.matmul(bank(gr % 2), con[:, C_GT:C_GT + P], gmask[gr % 2].rearrange("p h t -> p (h t)"), start=True, stop=False)
                    t.matmul(bank(gr % 2), identb[:], hideb[:].unsqueeze(1).broadcast_to([P, HG, P]), start=False,
                             stop=True).then_inc(c_D.h, 1)

                def products(gr):
                    ch, hg = gr // 2, gr % 2
                    for half in range(2):
                        n = 2 * gr + half
                        if n == 0:
                            c_eGS.wait(t, i, 1)
                        if n >= 2:
                            c_AT.wait(t, i, n - 1)
                        for y in range(2):
                            h = hg * HG + 2 * half + y
                            last = t.matmul(bank(2 + n % 2, 256, y * 256), kq[:, h, 0, ch * P:(ch + 1) * P],
                                            kq[:, h, :, ch * P:(ch + 1) * P], start=True, stop=True)
                        last.then_inc(c_kk.h, 1)

                def turn_T(l, gr):
                    if l == 0:
                        c_t2.wait(t, i, 2 * gr + 2)
                    else:
                        c_TT.wait(t, i, (l - 1) * GROUPS + gr + 1)
                    n = l * GROUPS + gr
                    if n >= 2:
                        c_T.wait(t, i, n - 1)
                    for h in range(HG):
                        last = t.transpose(bank(4 + gr % 2, P, h * P), TT[gr][:, h, :], ident)
                    last.then_inc(c_Tp.h, 1)

                log_decay(0)
                log_decay(1)
                for gr in range(GROUPS):
                    products(gr)
                    if gr + 2 < GROUPS:
                        log_decay(gr + 2)
                for l in range(NL):
                    for gr in range(GROUPS):
                        turn_T(l, gr)
                    for gr in range(GROUPS):
                        n = l * GROUPS + gr
                        if l == 0:
                            c_MTs.wait(t, i, gr + 1)
                        c_T.wait(t, i, n + 1)
                        if n >= 2:
                            c_W.wait(t, i, n - 1)
                        t.matmul(bank(gr % 2), identb[:], identb[:].unsqueeze(1).broadcast_to([P, HG, P]), start=True, stop=False,
                                 skip_group_check=True)
                        for h in range(HG):
                            last = t.matmul(bank(gr % 2, P, h * P), MT[gr][:, h, :], TN[gr][:, h, :], start=False, stop=h == HG - 1,
                                            skip_group_check=True)
                        last.then_inc(c_Z.h, 1)
                    for gr in range(GROUPS):
                        n = l * GROUPS + gr
                        c_W.wait(t, i, n + 1)
                        if n >= 2:
                            c_TT.wait(t, i, n - 1)
                        for h in range(HG):
                            last = t.matmul(bank(2 + gr % 2, P, h * P), WW[gr][:, h, :], TT[gr][:, h, :], start=True, stop=True)
                        last.then_inc(c_TTp.h, 1)
                c_TT.wait(t, i, NL * GROUPS)
                for ch in range(TILES):
                    if ch == 1:
                        c_S.wait(t, i, 1)
                        for h in range(NH):
                            last = t.matmul(bank(6, DV, h * DV), kq[:, h, 0, P:2 * P], S1[:, h, :], start=True, stop=True)
                        last.then_inc(c_kS.h, 1)
                        for h in range(NH):
                            last = t.matmul(bank(7, DV, h * DV), kq[:, h, 1, P:2 * P], S1[:, h, :], start=True, stop=True)
                        last.then_inc(c_O2.h, 1)
                    c_R.wait(t, i, 2 if ch == 0 else 5)
                    for h in range(NH):
                        last = t.matmul(bank(2 + ch, DV, h * DV), TT[2 * ch + h // HG][:, h % HG, :], R[:, h, :], start=True, stop=True)
                    last.then_inc(c_X.h, 1)
                    c_U.wait(t, i, ch + 1)
                    for h in range(NH):
                        last = t.matmul(bank(5 - 5 * ch, DV, h * DV), AT[2 * ch + h // HG][:, h % HG, :], U[:, h, :], start=True, stop=True)
                    last.then_inc(c_O.h, 1)
                    if ch == 0:
                        c_Uw.wait(t, i, 1)
                        for h in range(NH):
                            last = t.matmul(bank(4, DV, h * DV), ktok[h // 4][:, h % 4, :], Uw[:, h, :], start=True, stop=True)
                        last.then_inc(c_Sp.h, 1)
                c_og.wait(t, i, 1)
                for blk in range(2):
                    for j in range(TILES):
                        last = t.transpose(bank(0, P, blk * T + j * P), og[:, j, blk * P:(blk + 1) * P], ident)
                last.then_inc(c_oTp.h, 1)
                c_oT.wait(t, i, 1)
                for j in range(TILES):
                    for blk in range(2):
                        last = t.matmul(bank(1, D, j * D), oT[:, blk, j * P:(j + 1) * P], w_o1[:, blk, :], start=blk == 0, stop=blk == 1)
                last.then_inc(c_out.h, 1)

                turn_x(3)
                for n in range(2):
                    last = t.matmul(bank(1, T, n * T), at_w[:, n, :], hT[:], start=True, stop=True)
                last.then_inc(d_qk.h, 1)
                for j in range(TILES):
                    last = t.matmul(bank(2, D, j * D), hT[:, j * P:(j + 1) * P], at_w[:, 2, :], start=True, stop=True)
                last.then_inc(d_vp.h, 1)
                d_qks.wait(t, i, 2)
                for j in range(TILES):
                    last = t.matmul(bank(3, T, j * T), qkT[:, 0, j * P:(j + 1) * P], qkT[:, 1, :], start=True, stop=True)
                last.then_inc(d_sc.h, 1)
                d_p.wait(t, i, 2)
                for kt in range(TILES):
                    for j in range(TILES):
                        last = t.transpose(bank(4, P, kt * T + j * P), prob[:, j, kt * P:(kt + 1) * P], ident)
                last.then_inc(d_pT.h, 1)
                d_pTs.wait(t, i, 1)
                d_v.wait(t, i, 1)
                for kt in range(TILES):
                    last = t.matmul(bank(5, T), v_sb[:, kt, :], probT[:, kt, :], start=kt == 0, stop=kt == TILES - 1)
                last.then_inc(d_avp.h, 1)
                d_av.wait(t, i, 1)
                t.matmul(bank(6, T), at_w[:, 3, :], avT, start=True, stop=True).then_inc(d_ap.h, 1)
                d_xx.wait(t, i, 1)
                for j in range(TILES):
                    last = t.matmul(bank(7, E1, j * E1), xxT[:, j * P:(j + 1) * P], gate_w[:], start=True, stop=True)
                last.then_inc(d_glp.h, 1)

                def up(e):
                    for half in range(2):
                        n = 2 * e + half
                        if e >= 1:
                            (d_hma if half == 0 else d_hmv).wait(t, i, 2 * e)
                        for q in range(2):
                            m = 2 * half + q
                            last = t.matmul(bank(half, T, q * T), up1[:, e, m * P:(m + 1) * P], xxT, start=True, stop=True)
                        last.then_inc(d_up.h, 1)

                def down(e):
                    d_hma.wait(t, i, 2 * e + 2)
                    d_hmv.wait(t, i, 2 * e + 2)
                    if e >= 2:
                        d_acc.wait(t, i, 2 * (e - 1))
                    for j in range(TILES):
                        for m in range(HB1):
                            last = t.matmul(bank(2 + e % 2, D, j * D), hm[e % 2][:, m, j * P:(j + 1) * P], down1[:, HB1 * e + m, :],
                                            start=m == 0, stop=m == HB1 - 1)
                    last.then_inc(d_eo.h, 1)

                up(0)
                d_gt.wait(t, i, 4)
                for j in range(TILES):
                    last = t.transpose(PS[0:E1, 7, j * P:(j + 1) * P], gt[:, j, :], ident)
                last.then_inc(d_gTp.h, 1)
                d_gT.wait(t, i, 1)
                for j in range(TILES):
                    t.matmul(bank(5, D, j * D), xxT[:, j * P:(j + 1) * P], ident, start=True, stop=False)
                    last = t.matmul(bank(5, D, j * D), gT[:, j * P:(j + 1) * P], down1b[:], start=False, stop=True)
                last.then_inc(d_yi.h, 1)
                up(1)
                for e in range(E1):
                    down(e)
                    if e + 2 < E1:
                        up(e + 2)

        @block.vector
        def _(v):
            v.wait_ge(loaded, LOADED)
            v.memset(sp[:], 0.0).then_inc(prep_dve, 1)
            v.wait_ge(silu_c, 1)
            ec = xc[:, 0, 0:2 * NB].rearrange("p (l b) -> p l b", l=2)
            v.tensor_scalar(ec, ec, 1.0, None, ALU.add).then_inc(silu_c, 1)
            v.wait_ge(silu_c, 2)
            v.reciprocal(ec, ec).then_inc(prep_dve, 1)
            v.wait_ge(prep_dve, 2)
            v.tensor_tensor(cT[:], cT[:], ec, ALU.mult).then_inc(prep_dve, 1)
            v.wait_ge(mod_done, 1)
            v.tensor_copy(shift_scale[:].rearrange("p n b -> p (n b)"), bank(4, 8 * NB)).then_inc(prep_dve, 1)
            v.wait_ge(prep_dve, 4)
            for n in range(4):
                v.tensor_scalar(shift_scale[:, 2 * n + 1, :], shift_scale[:, 2 * n + 1, :], 1.0, None, ALU.add).then_inc(prep_dve, 1)
            g4 = PS[0:NB, 5, :]
            gflat = gates[:].rearrange("b n d -> b (n d)")
            sgn = big[0:NB, 4, 0:512]
            mag = big[0:NB, 5, 0:512]
            neg = big[0:NB, 6, 0:512]
            v.tensor_scalar(sgn, g4, 0.0, 2.0, ALU.is_ge, ALU.mult).then_inc(prep_dve, 1)
            v.tensor_scalar(mag, g4, -1.0, -0.25, ALU.mult, ALU.min).then_inc(prep_dve, 1)
            v.wait_ge(prep_dve, 10)
            v.tensor_scalar(neg, g4, -0.25, None, ALU.min).then_inc(silu_c, 1)
            v.wait_ge(silu_c, 3)
            v.tensor_tensor(mag, mag, neg, ALU.min).then_inc(silu_c, 1)
            v.tensor_scalar(sgn, sgn, 1.0, -1.0, ALU.subtract, ALU.mult).then_inc(silu_c, 1)
            v.wait_ge(silu_c, 5)
            v.tensor_tensor(gflat, sgn, mag, ALU.mult).then_inc(prep_dve, 1)
            v.wait_ge(prep_dve, 11)
            v.tensor_scalar(gates[:, 0, :], gates[:, 0, :], 0.5, None, ALU.mult).then_inc(prep_dve, 1)
            v.wait_ge(prep_dve, 12)
            v.wait_ge(prep_act, 7)
            v.wait_ge(prep_pool, 1)
            with v.Fori(0, NB) as i:
                def ln(n):
                    k = 5 * n
                    for j in range(TILES):
                        v.bn_stats(stats[:, j, :], x[n][:, j, :]).then_inc(ln_step.h, 1)
                    ln_step.wait_apart(v, i, k + 2, carrier)
                    for j in range(TILES):
                        v.bn_aggr(mv[:, j, :], stats[:, j, :]).then_inc(ln_step.h, 1)
                    ln_step.wait(v, i, k + 4)
                    v.tensor_scalar(mv[:, :, 1], mv[:, :, 1], LN_EPS, None, ALU.add).then_inc(ln_var.h, 1)
                    ln_rstd.wait(v, i, n + 1)
                    v.tensor_scalar(xn[:, 0, :], x[n][:, 0, :], mv[:, 0, 0:1], mv[:, 0, 1:2], ALU.subtract, ALU.mult).then_inc(ln_step.h, 1)
                    v.tensor_scalar(xn[:, 1, :], x[n][:, 1, :], mv[:, 1, 0:1], mv[:, 1, 1:2], ALU.subtract, ALU.mult).then_inc(ln_x.h, 1)

                def residual(n, branch):
                    v.tensor_tensor(res[:], branch, gates_bc[:, n:n + 1, :].broadcast_to([P, TILES, D]), ALU.mult).then_inc(res_v.h, 1)
                    res_v.wait(v, i, n + 1)
                    ins = v.tensor_tensor(x[n + 1][:], x[n][:], res[:], ALU.add)
                    ins.then_inc(x_new.h if n < 3 else out_ready.h, 1)
                    if n < 3:
                        x_new.wait(v, i, n + 1)

                def softplus16(which, src):
                    k = [SP_STEPS * which]

                    def step(ins):
                        ins.then_inc(sp_step.h, 1)
                        k[0] += 1
                        sp_step.wait(v, i, k[0])

                    v.scalar_tensor_tensor(sp[:, 1, :], src, -1.0, src, ALU.mult, ALU.min).then_inc(sp_in.h, 1)
                    sp_e.wait(v, i, which + 1)
                    step(v.tensor_scalar(sp[:, 2, :], sp[:, 1, :], 2.0, None, ALU.add))
                    step(v.reciprocal(sp[:, 2, :], sp[:, 2, :]))
                    step(v.scalar_tensor_tensor(sp[:, 3, :], sp[:, 1, :], 2.0, sp[:, 2, :], ALU.mult, ALU.mult))
                    step(v.scalar_tensor_tensor(sp[:, 4, :], sp[:, 3, :], 0.25, sp[:, 3, :], ALU.mult, ALU.mult))
                    step(v.tensor_scalar(sp[:, 5, :], sp[:, 4, :], 1.0 / (2 * LOG1P_TERMS + 1), None, ALU.mult))
                    a_, b_ = 5, 6
                    for m in range(LOG1P_TERMS - 1, 0, -1):
                        step(v.scalar_tensor_tensor(sp[:, b_, :], sp[:, a_, :], 1.0 / (2 * m + 1), sp[:, 4, :], ALU.add, ALU.mult))
                        a_, b_ = b_, a_
                    step(v.scalar_tensor_tensor(sp[:, 7, :], sp[:, a_, :], 1.0, sp[:, 3, :], ALU.add, ALU.mult))
                    step(v.scalar_tensor_tensor(sp[:, 0, :], src, 0.0, sp[:, 7, :], ALU.max, ALU.add))
                    assert k[0] == SP_STEPS * (which + 1)

                x_loaded.wait(v, i, 16)
                ln(0)
                a_zth.wait(v, i, 1)
                v.scalar_tensor_tensor(zs, th, 1.0, bank(2).rearrange("p (c t) -> p c t", c=CB), ALU.add, ALU.mult).then_inc(a_zs.h, 1)
                a_pad.wait(v, i, 1)
                for k in range(TAPS):
                    for c in range(CB):
                        if k == 0:
                            v.tensor_scalar(xc[:, c, :], pad0[:, c, 0:T], conv0[:, c, 0:1], conv0b[:, c:c + 1], ALU.mult, ALU.add).then_inc(a_conv.h, 1)
                        else:
                            a_conv.wait(v, i, CB * (k - 1) + c + 1)
                            v.scalar_tensor_tensor(xc[:, c, :], pad0[:, c, k:k + T], conv0[:, c, k:k + 1], xc[:, c, :],
                                                   ALU.mult, ALU.add).then_inc(a_conv.h, 1)
                a_conv.wait(v, i, CB * TAPS)
                a_uth.wait(v, i, 1)
                v.scalar_tensor_tensor(u2, th, 1.0, xc, ALU.add, ALU.mult).then_inc(a_u.h, 1)
                a_u.wait(v, i, 1)
                a_dtp.wait(v, i, 1)
                for c in range(CB):
                    v.tensor_scalar(vb[:, c, :], bank(4, T, c * T), b_dt[:, c:c + 1], None, ALU.add).then_inc(a_vb.h, 1)
                a_vb.wait(v, i, 2)
                v.scalar_tensor_tensor(ev, vb, -1.0, vb, ALU.mult, ALU.min).then_inc(a_na.h, 1)
                a_ln.wait(v, i, 1)
                v.scalar_tensor_tensor(dt, vb, 0.0, ev, ALU.max, ALU.add).then_inc(a_dt.h, 1)
                a_dt.wait(v, i, 1)
                v.scalar_tensor_tensor(dtu, dt, 0.5, u2, ALU.mult, ALU.mult).then_inc(a_dtu.h, 1)
                a_dtu.wait(v, i, 1)

                def drive_step(st):
                    gq, cb = st // CB, st % CB
                    a_B.wait(v, i, gq + 1)
                    b0 = 2 * (gq % 2)
                    v.tensor_tensor(drive[st % 2].rearrange("p (q t) -> p q t", q=SG),
                                    PS[:, b0:b0 + 2, :].rearrange("p a (q t) -> p (a q) t", t=T),
                                    dtu[:, cb, :].unsqueeze(1).broadcast_to([P, SG, T]), ALU.mult).then_inc(a_drv.h, 1)

                drive_step(0)
                for st in range(NG * CB):
                    if st + 1 < NG * CB:
                        if st >= 1:
                            a_h.wait(v, i, st)
                        drive_step(st + 1)
                    a_dec.wait(v, i, st + 1)
                    a_drv.wait(v, i, st + 1)
                    if st >= 2:
                        a_rd.wait(v, i, st - 1)
                    if st == 0:
                        a_zero.wait(v, i, 1)
                    v.tensor_tensor_scan(state[st % 2], decay[st % 2], drive[st % 2], 0.0, ALU.mult, ALU.add).then_inc(a_h.h, 1)
                for c in range(CB):
                    a_y.wait(v, i, NG * CB - 1 + c)
                    v.scalar_tensor_tensor(ysT[:, c, :], u2[:, c, :], d_half[:, c:c + 1], bank(6 + c, T), ALU.mult, ALU.add).then_inc(a_y1.h, 1)
                    a_y1.wait(v, i, c + 1)
                    v.tensor_tensor(ysT[:, c, :], ysT[:, c, :], zs[:, c, :], ALU.mult).then_inc(a_ys.h, 1)
                a_out.wait(v, i, 1)
                gate_loaded.wait(v, i, 16)
                residual(0, bank(4, TILES * D).rearrange("p (j d) -> p j d", d=D))

                ln(1)
                b_lgp.wait(v, i, 1)
                v.tensor_tensor(lg[:], bank(1, TILES * E0).rearrange("p (j e) -> p j e", e=E0),
                                rout_b[:].unsqueeze(1).broadcast_to([P, TILES, E0]), ALU.add).then_inc(b_lg.h, 1)
                b_lg.wait(v, i, 1)
                softplus16(0, lg[:].rearrange("p j e -> p (j e)"))
                b_root.wait_apart(v, i, 1, carrier)
                for j in range(TILES):
                    last = v.max(top[:, j, :], lg[:, j, :])
                last.then_inc(b_sel.h, 1)
                b_sel.wait_apart(v, i, 1, carrier)
                for j in range(TILES):
                    last = v.max_index(topi[:, j, :], top[:, j, :], lg[:, j, :])
                last.then_inc(b_sel.h, 1)
                b_sel.wait(v, i, 2)
                v.tensor_copy(topf[:], topi[:]).then_inc(b_sel.h, 1)
                b_sel.wait(v, i, 3)
                for j in range(TILES):
                    for n in range(2):
                        last = v.tensor_scalar(pick[:, j, n, :], con[:, C_IOTA:C_IOTA + 8], topf[:, j, n:n + 1], top[:, j, n:n + 1],
                                               ALU.is_equal, ALU.mult)
                last.then_inc(b_sel.h, 1)
                b_sel.wait(v, i, 4)
                v.tensor_tensor(cf[:, :, 0:8], pick[:, :, 0, :], pick[:, :, 1, :], ALU.add).then_inc(b_cf.h, 1)
                b_cfTp.wait(v, i, 1)
                v.tensor_copy(cfT[:], PS[0:9, 1, 0:T]).then_inc(b_cfT.h, 1)
                for m in range(BLK0):
                    M = P if m < 4 else H0
                    if m < 4:
                        b_half.wait(v, i, m + 1)
                        b_cfb.wait(v, i, m + 1)
                        v.tensor_tensor(mix0[:, m % 2, :], half0[:, m % 2, :], bank(4 + m % 2, T), ALU.mult).then_inc(b_mix.h, 1)
                        b_mix.wait(v, i, m + 1)
                    b_th.wait(v, i, m + 1)
                    src = mix0 if m < 4 else half0
                    v.scalar_tensor_tensor(hs0[0:M, m, :], thh[0:M, m % 2, :], 1.0, src[0:M, m % 2, :], ALU.add, ALU.mult).then_inc(b_hs.h, 1)
                b_out.wait(v, i, 1)
                residual(1, bank(6, TILES * D).rearrange("p (j d) -> p j d", d=D))

                ln(2)
                c_bap.wait(v, i, 1)
                v.tensor_copy(bax[:].rearrange("p j n -> p (j n)"), bank(1, TILES * 2 * NH)).then_inc(c_ba.h, 1)
                c_ba.wait(v, i, 1)
                c_ebeta.wait(v, i, 1)
                v.tensor_scalar(beta[:], beta[:], 1.0, None, ALU.add).then_inc(c_b1.h, 1)
                c_b1.wait(v, i, 1)
                v.reciprocal(beta[:], beta[:]).then_inc(c_b1.h, 1)
                v.tensor_tensor(lg[:], bax[:, :, NH:2 * NH], dt_bias[:].unsqueeze(1).broadcast_to([P, TILES, NH]), ALU.add).then_inc(c_b1.h, 1)
                c_b1.wait(v, i, 3)
                softplus16(1, lg[:].rearrange("p j e -> p (j e)"))
                v.tensor_tensor(gl[:], sp[:, 0, :].rearrange("p (j h) -> p j h", h=NH), expA[:].unsqueeze(1).broadcast_to([P, TILES, NH]),
                                ALU.mult).then_inc(c_g.h, 1)
                c_gvt.wait(v, i, 1)
                v.scalar_tensor_tensor(gv[:], gvt[:], 1.0, bank(2).rearrange("p (c v) -> p c v", c=TILES), ALU.add, ALU.mult).then_inc(c_gv.h, 1)

                def silu_out(m):
                    c_th.wait(v, i, m + 1)
                    dst = kq[:, m, :, :] if m < 8 else v2[:]
                    v.scalar_tensor_tensor(dst, th1[m % 2][:], 1.0, xc1[m % 2][:], ALU.add, ALU.mult).then_inc(c_kq.h, 1)

                for m in range(9):
                    c_pad.wait(v, i, m + 1)
                    if m >= 2:
                        c_kq.wait(v, i, m - 1)
                    for k in range(TAPS):
                        for n in range(2):
                            w = conv1[:, 2 * m + n, k:k + 1]
                            src = pad1[m % 2][:, n, k:k + T]
                            dst = xc1[m % 2][:, n, :]
                            if k == 0:
                                v.tensor_scalar(dst, src, w, None, ALU.mult).then_inc(c_conv.h, 1)
                            else:
                                c_conv.wait(v, i, 8 * m + 2 * (k - 1) + n + 1)
                                v.scalar_tensor_tensor(dst, src, w, dst, ALU.mult, ALU.add).then_inc(c_conv.h, 1)
                    if m >= 1:
                        silu_out(m - 1)
                silu_out(8)
                c_ssp.wait(v, i, 8)
                v.tensor_copy(ssq[:].rearrange("p a b c -> p (a b c)"), bank(5, 32)).then_inc(c_ss.h, 1)
                c_ss.wait(v, i, 1)
                v.tensor_scalar(rk2[:], ssq[:, 0], 4 * L2_EPS, None, ALU.add).then_inc(c_ss.h, 1)
                v.tensor_scalar(vscale[:], ssq[:, 0], 0.25, L2_EPS, ALU.mult, ALU.add).then_inc(c_ss.h, 1)
                v.tensor_scalar(rq[:], ssq[:, 1], float(P), 4 * L2_EPS * P, ALU.mult, ALU.add).then_inc(c_ss.h, 1)
                c_ss.wait(v, i, 4)
                v.reciprocal(rk2[:], rk2[:]).then_inc(c_ss.h, 1)
                c_ss.wait(v, i, 5)
                v.tensor_tensor(cU[:], beta[:], rk2[:], ALU.mult).then_inc(c_ss.h, 1)
                c_ss.wait(v, i, 6)
                v.tensor_scalar(negc[:], cU[:], -1.0, None, ALU.mult).then_inc(c_R.h, 1)
                c_R.wait(v, i, 1)
                for gr in range(GROUPS):
                    ch, hg = gr // 2, gr % 2
                    c_et.wait(v, i, gr + 1)
                    for half in range(2):
                        n = 2 * gr + half
                        c_kk.wait(v, i, n + 1)
                        for y in range(2):
                            hh = 2 * half + y
                            h = hg * HG + hh
                            v.scalar_tensor_tensor(MT[gr][:, hh, :], bank(2 + n % 2, P, y * 256), negc[:, ch, h:h + 1], et[gr % 2][:, hh, :],
                                                   ALU.mult, ALU.mult).then_inc(c_MT.h, 1)
                        v.tensor_tensor(AT[gr][:, 2 * half:2 * half + 2, :],
                                        bank(2 + n % 2).rearrange("p (y k t) -> p y k t", y=2, k=2)[:, :, 1, :],
                                        et[gr % 2][:, 2 * half:2 * half + 2, :], ALU.mult).then_inc(c_AT.h, 1)
                    c_MTs.wait(v, i, gr + 1)
                    v.tensor_tensor(TT[gr], MT[gr], con[:, C_MASK2:C_MASK2 + P].unsqueeze(1).broadcast_to([P, HG, P]), ALU.mult).then_inc(c_t2.h, 1)
                    c_t2.wait(v, i, 2 * gr + 1)
                    v.tensor_tensor(TT[gr], TT[gr], ident.unsqueeze(1).broadcast_to([P, HG, P]), ALU.add).then_inc(c_t2.h, 1)
                for l in range(NL):
                    for gr in range(GROUPS):
                        n = l * GROUPS + gr
                        c_Z.wait(v, i, n + 1)
                        v.tensor_tensor(WW[gr], bank(gr % 2).rearrange("p (h t) -> p h t", h=HG),
                                        con[:, C_MERGE + l * P:C_MERGE + (l + 1) * P].unsqueeze(1).broadcast_to([P, HG, P]),
                                        ALU.mult).then_inc(c_W.h, 1)

                def by_head(ap):
                    return ap.unsqueeze(2).broadcast_to([P, NH, DV])

                c_vtok.wait(v, i, 1)
                c_eGS.wait(v, i, 1)
                c_root.wait(v, i, 2)
                v.tensor_tensor(R[:], vtok[:, 0], by_head(vscale[:, 0]), ALU.mult).then_inc(c_R.h, 1)
                c_X.wait(v, i, 1)
                v.tensor_tensor(U[:], bank(2, 256).rearrange("p (h v) -> p h v", v=DV), by_head(cU[:, 0]), ALU.mult).then_inc(c_U.h, 1)
                c_U.wait(v, i, 1)
                v.tensor_tensor(Uw[:], U[:], by_head(eGS[:, 0, 1]), ALU.mult).then_inc(c_Uw.h, 1)
                c_O.wait(v, i, 1)
                v.tensor_tensor(ou[:, 0], bank(5, 256).rearrange("p (h v) -> p h v", v=DV), by_head(rq[:, 0]), ALU.mult).then_inc(c_o.h, 1)
                c_kS.wait(v, i, 1)
                v.tensor_tensor(kSd[:], bank(6, 256).rearrange("p (h v) -> p h v", v=DV), by_head(eGS[:, 1, 0]), ALU.mult).then_inc(c_R.h, 1)
                v.tensor_tensor(R[:], vtok[:, 1], by_head(vscale[:, 1]), ALU.mult).then_inc(c_R.h, 1)
                c_R.wait(v, i, 4)
                v.tensor_tensor(R[:], R[:], kSd[:], ALU.subtract).then_inc(c_R.h, 1)
                c_X.wait(v, i, 2)
                v.tensor_tensor(U[:], bank(3, 256).rearrange("p (h v) -> p h v", v=DV), by_head(cU[:, 1]), ALU.mult).then_inc(c_U.h, 1)
                c_O2.wait(v, i, 1)
                v.tensor_tensor(o2s[:], bank(7, 256).rearrange("p (h v) -> p h v", v=DV), by_head(eGS[:, 1, 0]), ALU.mult).then_inc(c_o.h, 1)
                c_o.wait(v, i, 2)
                c_O.wait(v, i, 2)
                v.tensor_tensor(o2s[:], bank(0, 256).rearrange("p (h v) -> p h v", v=DV), o2s[:], ALU.add).then_inc(c_o.h, 1)
                c_o.wait(v, i, 3)
                v.tensor_tensor(ou[:, 1], o2s[:], by_head(rq[:, 1]), ALU.mult).then_inc(c_o.h, 1)
                c_o.wait(v, i, 4)
                c_osq.wait(v, i, 1)
                v.tensor_reduce(rms[:], osq[:], X, ALU.add).then_inc(c_rms.h, 1)
                c_rms.wait(v, i, 1)
                v.tensor_scalar(rms[:], rms[:], 1.0 / DV, RMS_EPS, ALU.mult, ALU.add).then_inc(c_rms.h, 1)
                c_rrms.wait(v, i, 1)
                ogh = og[:].rearrange("p c (h v) -> p (c h) v", v=DV)
                v.tensor_tensor(ogh, ou[:].rearrange("p c h v -> p (c h) v"),
                                rms[:].rearrange("p c h -> p (c h)").unsqueeze(2).broadcast_to([P, TILES * NH, DV]), ALU.mult).then_inc(c_rms.h, 1)
                c_rms.wait(v, i, 3)
                c_gnw.wait(v, i, 1)
                v.tensor_tensor(og[:], og[:], gnw[:], ALU.mult).then_inc(c_og.h, 1)
                c_out.wait(v, i, 1)
                residual(2, bank(1, TILES * D).rearrange("p (j d) -> p j d", d=D))

                ln(3)
                d_vp.wait(v, i, 1)
                v.tensor_copy(v_sb[:].rearrange("p j d -> p (j d)"), bank(2, TILES * D)).then_inc(d_v.h, 1)
                d_sc.wait(v, i, 1)
                v.tensor_reduce(smax[:, 0:2], bank(3).rearrange("p (j t) -> p j t", t=T), X, ALU.max).then_inc(d_mx.h, 1)
                d_mx.wait(v, i, 1)
                v.tensor_scalar(smax[:, 2:4], smax[:, 0:2], -float(D) ** -0.5, None, ALU.mult).then_inc(d_mx.h, 1)
                d_e.wait(v, i, 2)
                v.reciprocal(ssum[:, 2:4], ssum[:, 0:2]).then_inc(d_rs.h, 1)
                d_rs.wait(v, i, 1)
                for n in range(TILES):
                    v.tensor_scalar(prob[:, n, :], prob[:, n, :], ssum[:, 2 + n:3 + n], None, ALU.mult).then_inc(d_p.h, 1)
                d_ap.wait(v, i, 1)
                v.scalar_tensor_tensor(xxT, bank(6, T), at_b[:, 3:4], hT[:], ALU.add, ALU.add).then_inc(d_xx.h, 1)
                d_glp.wait(v, i, 1)
                v.tensor_tensor(gt[:], bank(7, TILES * E1).rearrange("p (j e) -> p j e", e=E1),
                                gate_b[:].unsqueeze(1).broadcast_to([P, TILES, E1]), ALU.add).then_inc(d_g1.h, 1)
                d_g1.wait(v, i, 1)
                v.tensor_reduce(gm[:, 0:2], gt[:], X, ALU.max).then_inc(d_g1.h, 1)
                d_g1.wait(v, i, 2)
                for j in range(TILES):
                    v.tensor_scalar(gt[:, j, :], gt[:, j, :], gm[:, j:j + 1], None, ALU.subtract).then_inc(d_g1.h, 1)
                d_ge.wait(v, i, 1)
                v.tensor_reduce(gm[:, 2:4], gt[:], X, ALU.add).then_inc(d_gt.h, 1)
                d_gt.wait(v, i, 1)
                v.reciprocal(gm[:, 2:4], gm[:, 2:4]).then_inc(d_gt.h, 1)
                d_gt.wait(v, i, 2)
                for j in range(TILES):
                    v.tensor_scalar(gt[:, j, :], gt[:, j, :], gm[:, 2 + j:3 + j], None, ALU.mult).then_inc(d_gt.h, 1)
                d_gTp.wait(v, i, 1)
                v.tensor_copy(gT[:], PS[0:E1, 7, 0:T]).then_inc(d_gT.h, 1)

                def hidden(e):
                    d_up.wait(v, i, 2 * e + 2)
                    if e >= 2:
                        d_eo.wait(v, i, e - 1)
                    for q in range(2):
                        v.tensor_scalar(hm[e % 2][:, 2 + q, :], bank(1, T, q * T), up1b[:, HB1 * e + 2 + q:HB1 * e + 3 + q], 0.0,
                                        ALU.add, ALU.max).then_inc(d_hmv.h, 1)

                hidden(0)
                d_y0.wait(v, i, 1)
                for e in range(E1):
                    if e + 1 < E1:
                        hidden(e + 1)
                    d_eo.wait(v, i, e + 1)
                    for j in range(TILES):
                        if e >= 1:
                            d_acc.wait(v, i, 2 * (e - 1) + j + 1)
                        v.scalar_tensor_tensor(yacc[:, j, :], bank(2 + e % 2, D, j * D), gt[:, j, e:e + 1], yacc[:, j, :],
                                               ALU.mult, ALU.add).then_inc(d_acc.h, 1)
                d_acc.wait(v, i, 2 * E1)
                residual(3, yacc[:])


def kernel(**k):
    import concourse.bacc as bacc
    from concourse.bass_utils import run_bass_kernel_spmd as run

    n = {key: np.asarray(val) for key, val in k.items()}
    NB = n["L0_attn_x"].shape[0]
    conv1 = np.concatenate([
        np.stack([n["L1_attn_conv_k"].reshape(NH, P, TAPS), n["L1_attn_conv_q"].reshape(NH, P, TAPS)], 1).reshape(2 * NH * P, TAPS),
        n["L1_attn_conv_v"]])
    up0b = np.zeros((BLK0 * P,), np.float32)
    up0b[:E0 * H0] = n["L0_ffn_rb1"].reshape(-1)
    up0b[E0 * H0:9 * H0] = n["L0_ffn_sb1"]
    down0 = np.zeros((BLK0 * P, D), np.float32)
    down0[:E0 * H0] = n["L0_ffn_rW2"].reshape(E0 * H0, D)
    down0[E0 * H0:9 * H0] = n["L0_ffn_sW2"]
    arrays = {
        "x": n["L0_attn_x"], "con": constants(), "c0T": n["L0_c"].T, "c1T": n["L1_c"].T,
        "wmod0": n["L0_wmod"], "wmod1": n["L1_wmod"],
        "w_inT": n["L0_attn_W_in"].T, "conv_w0": n["L0_attn_conv_w"], "conv_b0": n["L0_attn_conv_b"].reshape(CB, P).T,
        "w_xT": n["L0_attn_W_xproj"].T, "w_dtT": n["L0_attn_W_dt"].T, "b_dt": n["L0_attn_b_dt"].reshape(CB, P).T,
        "A_log0": n["L0_attn_A_log"], "D_skip": n["L0_attn_D_skip"].reshape(CB, P).T, "w_outT": n["L0_attn_W_out"].T,
        "routT": n["L0_ffn_routing_W"].T, "exp_bias": n["L0_ffn_expert_bias"],
        "up0": np.concatenate([n["L0_ffn_rW1"].transpose(1, 0, 2).reshape(D, E0 * H0), n["L0_ffn_sW1"]], 1),
        "up0b": up0b.reshape(BLK0, P).T, "down0": down0,
        "down0b": np.concatenate([n["L0_ffn_rb2"], n["L0_ffn_sb2"][None]], 0),
        "Wk1": n["L1_attn_Wk"], "Wq1": n["L1_attn_Wq"], "Wv1": n["L1_attn_Wv"], "Wg1": n["L1_attn_Wg"],
        "conv1": conv1, "Wb1": n["L1_attn_Wb"], "Wa1": n["L1_attn_Wa"], "A_log1": n["L1_attn_A_log"],
        "dt_bias1": n["L1_attn_dt_bias"], "norm_w": n["L1_attn_norm_w"], "Wo1": n["L1_attn_Wo"],
        "fWq": n["L1_ffn_Wq"], "fWk": n["L1_ffn_Wk"], "fWv": n["L1_ffn_Wv"], "fWo": n["L1_ffn_Wo"],
        "fb": np.stack([n["L1_ffn_bq"], n["L1_ffn_bk"], n["L1_ffn_bv"], n["L1_ffn_bo"]], 1),
        "fWg": n["L1_ffn_Wg"], "fbg": n["L1_ffn_bg"], "W1": n["L1_ffn_W1"], "b1": n["L1_ffn_b1"].reshape(E1 * HB1, P).T,
        "W2": n["L1_ffn_W2"], "b2": n["L1_ffn_b2"],
    }
    arrays = {key: np.ascontiguousarray(val) for key, val in arrays.items()}
    nc = bacc.Bacc("TRN2", target_bir_lowering=False, num_devices=1)
    aps = {key: nc.dram_tensor("in_" + key, val.shape, F32, kind="ExternalInput").ap() for key, val in arrays.items()}
    out = nc.dram_tensor("out", n["L0_attn_x"].shape, F32, kind="ExternalOutput").ap()
    build(nc, aps, out, NB)
    r = run(nc, [{"in_" + key: val for key, val in arrays.items()}], core_ids=[0])
    return r.results[0]["out"]
```

```python
from contextlib import ExitStack

import numpy as np
import concourse.bass as bass
from concourse import mybir

F32 = mybir.dt.float32
BF16 = mybir.dt.bfloat16
U32 = mybir.dt.uint32
ALU = mybir.AluOpType
ACT = mybir.ActivationFunctionType
X = mybir.AxisListType.X

P = 128
T = 256
TILES = T // P
D = 128
CB = 2
TAPS = 4
NS = 16
RANK = 8
SG = 2
NG = NS // SG
E0 = 8
H0 = 64
BLK0 = 5
NH = 8
DV = 32
HG = 4
GROUPS = TILES * NH // HG
LEVELS = [2, 4, 8, 16, 32, 64]
E1 = 8
HB1 = 4
LN_EPS = 1e-5
L2_EPS = 1e-6
RMS_EPS = 1e-5
SP_STEPS = 13
LOG1P_TERMS = 7

C_ID = 0
C_MASK2 = 128
C_MERGE = 256
C_GT = C_MERGE + 128 * len(LEVELS)
C_LE = C_GT + 128
C_HIDE = C_LE + 128
C_SEL = C_HIDE + 128
C_IOTA = C_SEL + 4 * 128
C_LT = C_IOTA + 8
C_SEL3 = C_LT + 128
C_N = C_SEL3 + 2 * NS


def constants():
    c = np.zeros((P, C_N), np.float32)
    r = np.arange(P)
    row, col = r[:, None], r[None, :]
    c[:, C_ID:C_ID + P] = row == col
    c[:, C_MASK2:C_MASK2 + P] = (col % 2 == 1) & (row == col - 1)
    for n, s in enumerate(LEVELS):
        low = (row // (2 * s) == col // (2 * s)) & (row // s % 2 == 1) & (col // s % 2 == 0)
        c[:, C_MERGE + n * P:C_MERGE + (n + 1) * P] = low | (row == col)
    c[:, C_GT:C_GT + P] = row > col
    c[:, C_LE:C_LE + P] = row <= col
    c[:, C_HIDE:C_HIDE + P] = np.where(col < row, -32768.0, 0.0)
    for m in range(4):
        c[:E0, C_SEL + m * P:C_SEL + (m + 1) * P] = r[:E0, None] == 2 * m + (col // H0)
    c[:, C_IOTA:C_IOTA + 8] = np.arange(8)
    c[:, C_LT:C_LT + P] = row < col
    c[:3 * 2 * NS, C_SEL3:C_SEL3 + 2 * NS] = r[:3 * 2 * NS, None] % (2 * NS) == r[None, :2 * NS]
    return c


SCAN = [("a_norm",), ("a_norm2",), ("a_turn",), ("a_in",), ("a_conv",), ("a_zgate",), ("a_silu",), ("a_silu2",),
        ("a_xproj",), ("a_dt",), ("a_split",), ("a_soft",), ("a_step",)]
SCAN += [("a_scan", st) for st in range(NG + 2)]
SCAN += [("a_y",), ("a_out",), ("a_res",)]
ROUTED = [("b_norm",), ("b_norm2",), ("b_turn",), ("b_logits",), ("b_soft",), ("b_soft2",), ("b_root",),
          ("b_select",), ("b_coef",)]
ROUTED += [("b_up", m) for m in range(BLK0 + 1)] + [("b_out",), ("b_res",)]
PROJECT = [("c_norm",), ("c_norm2",), ("c_turn",), ("c_ba",), ("c_beta",), ("c_soft",), ("c_soft2",), ("c_gmask", 0), ("c_gmask", 1)]
PROJECT += [("c_proj", m) for m in range(12)]
PROJECT += [("c_gate",)]
PROJECT += [("c_turn_k", 0), ("c_turn_k", 1), ("c_scales",), ("c_turn_v",), ("c_decay",)]
for gr in range(GROUPS):
    PROJECT += [("c_logd", gr), ("c_prod", gr, 0), ("c_prod", gr, 1), ("c_strict", gr)]
    if gr + 2 < GROUPS:
        PROJECT += [("c_gmask", gr + 2)]
PROJECT += [("c_roots",)]
INVERT = [("keep_x",)] + [("c_first", gr) for gr in range(GROUPS)] + [("lev_T", 0, 0), ("lev_T", 0, 1), ("lev_T", 0, 2)]
for lv in range(len(LEVELS)):
    INVERT += [("lev_Z", lv, 0), ("lev_T", lv, 3), ("lev_Z", lv, 1), ("lev_Z", lv, 2), ("lev_Z", lv, 3)]
    for gr in range(GROUPS):
        INVERT += [("lev_TT", lv, gr)]
        if lv + 1 < len(LEVELS) and gr >= 1:
            INVERT += [("lev_T", lv + 1, gr - 1)]
APPLY = [("c_R", 0), ("c_X", 0), ("c_U", 0), ("c_O", 0), ("c_S",), ("c_o", 0), ("c_kS",), ("c_R", 1), ("c_X", 1),
         ("c_U", 1), ("c_O", 1), ("c_o", 1), ("c_squares",), ("c_rms",), ("c_gated",), ("c_turn_o",),
         ("c_out",), ("c_res",)]
ATTEND = [("d_norm",), ("d_norm2",), ("d_turn",), ("d_qkv",), ("d_v",), ("d_scores",), ("d_max",), ("d_exp",),
          ("d_prob",), ("d_turn_p",), ("d_av",), ("d_a",), ("d_xx",), ("d_gates",), ("d_gsub",), ("d_up", 0, 0),
          ("d_gexp",), ("d_up", 0, 1), ("d_gnorm",), ("d_turn_g",), ("d_yinit",)]
EXPERTS = [("d_up", 1, 0), ("d_up", 1, 1)]
for e in range(E1):
    EXPERTS += [("d_down", e, 0), ("d_down", e, 1)]
    if e + 2 < E1:
        EXPERTS += [("d_up", e + 2, 0), ("d_up", e + 2, 1)]
    EXPERTS += [("d_mix", e)]
EXPERTS += [("d_res",)]


FIRST_HALF = SCAN + ROUTED + PROJECT
SECOND_HALF = INVERT + APPLY + ATTEND + EXPERTS
TURNS = {
    "tensor": (
        "yyyyxyyxyyyyyyxyyxyyyyyyyyyxyyyyxyyyxyyyxyyyxyyxyyyyxyyyyyxyyyyyyyyxyyxyyyyyyyyyxyyyyyyxyxyyyyxy"
        "xxxxxxyyxyyyxxyxyyyxyyxxyyyyxyyyyxyyxyxyyxyyyyyyyxyyxyyxxxyxxxxxxxxyxxxxxxyyyyyy"),
    "vector": (
        "yyyxyxyyxxyxyxxyyyxyxxyyxyxyxxyyxyyxyxyxyxyyyxxyxyyyxyxyxyxyxxyxxyxxyyyxxxyyxyxyxxyyyyyxyxyxyxyy"
        "xxyyyyxyyxxyyyyxxyyxxxxxxxxyyyyyy"),
    "scalar": (
        "yyyyyxxyxyyyxyyyyxyyyxyyxyyxyxyyyxyyxyyxyxyyxyyyyyyyxyyyyyyyyyyyxxyxxxxxyyxyxyxxyxyxyyxyxyyyxyxy"
        "xyxyxyxyyxxxxxxxyxxxyyyy"),
    "gpsimd": (
        "xxxxxxxxxxxxxyyyxxxxxxxxxxxxxxxxxxxxxxx"),
}


class Signal:

    def __init__(self, handle, n, first=0):
        self.h, self.n, self.first = handle, n, first

    def at(self, i, k):
        assert k > 0
        return i * self.n + self.first + k


def build(nc, a, out, NB):
    with ExitStack() as ctx:
        def sb(name, shape, dt=F32):
            return ctx.enter_context(nc.sbuf_tensor(name, shape, dt))

        def sem(name):
            return ctx.enter_context(nc.semaphore(name))

        def sig(name, n=1):
            return Signal(sem(name), n)

        def sigs(name, *counts):
            handle = sem(name)
            return [Signal(handle, sum(counts), sum(counts[:n])) for n in range(len(counts))]

        PS = ctx.enter_context(nc.psum_tensor("banks", [P, 8, 512], F32))

        def bank(n, w=512, at=0):
            return PS[:, n, at:at + w]

        con = sb("con", [P, C_N])
        ident = con[:, C_ID:C_ID + P]
        zero_col = con[:, C_LT:C_LT + 1]
        carrier = (sb("carried", [P, 1])[:], zero_col)
        identb = sb("identb", [P, P], BF16)
        hideb = sb("hideb", [P, P], BF16)
        sel3b = sb("sel3b", [3 * 2 * NS, 2 * NS], BF16)
        w_in = sb("w_in", [D, 4 * P])
        conv0 = sb("conv0", [P, CB, TAPS])
        conv0b = sb("conv0b", [P, CB])
        w_bc = sb("w_bc", [P, CB, 3 * 2 * NS])
        w_rank = sb("w_rank", [P, CB, RANK])
        w_dt = sb("w_dt", [RANK, CB * P])
        b_dt = sb("b_dt", [P, CB])
        a_neg = sb("a_neg", [P, CB, NS])
        d_half = sb("d_half", [P, CB])
        w_out = sb("w_out", [P, CB, D])
        rout_w = sb("rout_w", [D, E0])
        rout_b = sb("rout_b", [P, E0])
        up0 = sb("up0", [D, 9 * H0])
        up0b = sb("up0b", [P, BLK0])
        down0 = sb("down0", [P, BLK0, D])
        down0b = sb("down0b", [9, D])
        w_k = sb("w_k", [D, NH * P])
        w_q = sb("w_q", [D, NH * P])
        w_v = sb("w_v", [D, NH * DV])
        w_g = sb("w_g", [D, NH * DV])
        conv1 = sb("conv1", [P, 18, TAPS])
        w_ba = sb("w_ba", [D, 2 * NH])
        expA = sb("expA", [P, NH])
        dt_bias = sb("dt_bias", [P, NH])
        norm_half = sb("norm_half", [P, DV])
        w_o1 = sb("w_o1", [P, 2, D])
        at_w = sb("at_w", [D, 4, D])
        at_b = sb("at_b", [D, 4])
        gate_w = sb("gate_w", [D, E1])
        gate_b = sb("gate_b", [P, E1])
        up1 = sb("up1", [D, E1, HB1 * P])
        up1b = sb("up1b", [P, E1 * HB1])
        down1 = sb("down1", [P, E1 * HB1, D])
        down1b = sb("down1b", [E1, D])
        ones_col = sb("ones_col", [P, 1])
        expo = sb("expo", [P, 2])
        wide = sb("wide", [P, 8, 1024])
        wmod = wide[:, 0:2, 0:6 * D]
        cT = sb("cT", [D, 2, NB])
        shift_scale = sb("shift_scale", [D, 8, NB])
        gates = sb("gates", [NB, 4, D])
        gates_bc = sb("gates_bc", [P, 4, D])
        gates_dram = nc.dram_tensor("gate_rows", (NB, 4 * D), F32, kind="Internal").ap()

        def two(name):
            return [sb(f"{name}_{n}", [P, TILES, D]) for n in ("x", "y")]

        x = [sb(f"x{n}", [P, TILES, D]) for n in range(4)]
        x2_kept = sb("x2_kept", [P, TILES, D])
        stats = [sb(f"stats_{n}", [P, TILES, 6]) for n in ("x", "y")]
        mv = [sb(f"mv_{n}", [P, TILES, 2]) for n in ("x", "y")]
        xn = two("xn")
        x.append(xn[1])
        hT = [sb(f"hT_{n}", [D, T]) for n in ("x", "y")]

        small = sb("small", [P, 6, CB, T])
        xc, th, u2, zs, dt, dtu = [small[:, n] for n in range(6)]
        vb, ev, ysT = xc, th, xc
        pad0 = sb("pad0", [P, CB, T + 3])
        bcf = dtu[0:3 * 2 * NS, 0]
        bcr = dtu[0:3 * 2 * NS, 1]
        bcm = sb("bcm", [3 * 2 * NS, T], BF16)
        bc3 = sb("bc3", [3 * 2 * NS, T], BF16)
        rank_sb = sb("rank_sb", [RANK, T])
        decay = [wide[:, n] for n in (0, 1)]
        drive = [wide[:, n] for n in (2, 3)]
        state = [wide[:, n] for n in (4, 5)]
        c_sb = [wide[:, 6, 512 * n:512 * n + 512].rearrange("p (q t) -> p q t", q=SG) for n in range(2)]
        ysum = sb("ysum", [P, T])
        ypart = [wide[:, 7, 512 * n:512 * n + 512] for n in range(2)]

        sp = sb("sp", [P, 9, 16])
        lg = sb("lg", [P, TILES, E0])
        top = sb("top", [P, TILES, 8])
        topi = sb("topi", [P, TILES, 8], U32)
        topf = sb("topf", [P, TILES, 8])
        pick = sb("pick", [P, TILES, 2, E0])
        cf = sb("cf", [P, TILES, 9])
        cfT = sb("cfT", [9, T])
        half0 = wide[:, 5, 0:512].rearrange("p (n t) -> p n t", n=2)
        thh = wide[:, 5, 512:1024].rearrange("p (n t) -> p n t", n=2)
        mix0 = wide[:, 6, 0:512].rearrange("p (n t) -> p n t", n=2)
        hs0 = wide[:, 0:2].rearrange("p a (b t) -> p (a b) t", t=T)[:, 0:BLK0]

        pad1 = [sb(f"pad1_{n}", [P, 2, T + 3]) for n in range(2)]
        xc1 = [wide[:, blk, at:at + 512].rearrange("p (n t) -> p n t", n=2) for blk, at in ((0, 0), (0, 512), (5, 0))]
        th1 = [wide[:, 1, 512 * n:512 * n + 512].rearrange("p (n t) -> p n t", n=2) for n in range(2)]
        sq = [wide[:, 2, 512 * n:512 * n + 512].rearrange("p (n t) -> p n t", n=2) for n in range(2)]
        gmask = [wide[:, 3, 512 * n:512 * n + 512].rearrange("p (h t) -> p h t", t=P) for n in range(2)]
        et = [wide[:, 4, 512 * n:512 * n + 512].rearrange("p (h t) -> p h t", t=P) for n in range(2)]
        v2 = wide[:, 7, 0:512].rearrange("p (n t) -> p n t", n=2)
        gvt = wide[:, 7, 512:1024].rearrange("p (c v) -> p c v", c=TILES)
        gv = wide[:, 6, 512:1024].rearrange("p (c v) -> p c v", c=TILES)
        kq = sb("kq", [P, NH, 2, T])
        ssq = sb("ssq", [P, 2, TILES, NH])
        rq = sb("rq", [P, TILES, NH])
        rk2 = sb("rk2", [P, TILES, NH])
        vscale = sb("vscale", [P, TILES, NH])
        beta = sb("beta", [P, TILES, NH])
        bax = sb("bax", [P, TILES, 2 * NH])
        gl = sb("gl", [P, TILES, NH])
        cU = sb("cU", [P, TILES, NH])
        negc = sb("negc", [P, TILES, NH])
        eGS = sb("eGS", [P, TILES, 2, NH])
        mats = sb("mats", [P, 2, GROUPS, HG, P])
        MT = [mats[:, 0, n] for n in range(GROUPS)]
        AT = [mats[:, 1, n] for n in range(GROUPS)]
        ktok = [sb(f"ktok{n}", [P, 4, P]) for n in range(2)]
        vtok = sb("vtok", [P, TILES, NH, DV])
        gnw = sb("gnw", [P, TILES, NH * DV])
        inv = sb("inv", [P, 12, 512])
        TT = [inv[:, n].rearrange("p (h t) -> p h t", t=P) for n in range(4)]
        TN = [inv[:, 4 + n].rearrange("p (h t) -> p h t", t=P) for n in range(4)]
        WW = [inv[:, 8 + n].rearrange("p (h t) -> p h t", t=P) for n in range(4)]
        R, kSd, U, Uw, S1 = [inv[:, 4 + n // 2, 256 * (n % 2):256 * (n % 2) + 256].rearrange("p (h v) -> p h v", v=DV) for n in range(5)]
        ou = inv[:, 7].rearrange("p (c h v) -> p c h v", c=TILES, h=NH)
        o2s = kSd
        osq = inv[:, 8].rearrange("p (c h v) -> p c h v", c=TILES, h=NH)
        og = inv[:, 9].rearrange("p (c v) -> p c v", c=TILES)
        oT = inv[:, 10].rearrange("p (c t) -> p c t", c=2)
        rms = sb("rms", [P, TILES, NH])

        qkT, prob, probT = [inv[:, n].rearrange("p (a t) -> p a t", a=2) for n in (0, 1, 2)]
        avT, xxT = inv[:, 3, 0:T], inv[:, 3, T:2 * T]
        hm = [inv[:, 4 + 2 * n:6 + 2 * n].rearrange("p a (b t) -> p (a b) t", t=T) for n in range(2)]
        v_sb, yacc = [inv[:, 8, 256 * n:256 * n + 256].rearrange("p (j d) -> p j d", d=D) for n in range(2)]
        gT = inv[0:E1, 9, 0:T]
        smax = sb("smax", [P, 4])
        ssum = sb("ssum", [P, 4])
        gt = sb("gt", [P, TILES, E1])
        gm = sb("gm", [P, 4])

        loaded = sem("weights_loaded")
        mod_done = sem("modulation_products")
        silu_c = sem("silu_of_c")
        prep_act = sem("prologue_scalar")
        prep_dve = sem("prologue_vector")
        prep_pool = sem("prologue_pool")
        gates_stored = sem("gate_rows_stored")

        x_loaded = sig("x_loaded", 16)
        gx_loaded = sig("gates0_loaded", 16)
        gy_loaded = sig("gates1_loaded", 16)
        out_stored = sig("out_stored", 16)
        ln_step = sigs("lnx_stats", 4, 4, 4) + sigs("lny_stats", 4)
        ln_var = sigs("lnx_variance", 1, 1, 1) + sigs("lny_variance", 1)
        ln_rstd = sigs("lnx_rstd", 1, 1, 1) + sigs("lny_rstd", 1)
        ln_x = sigs("lnx_normalised", 1, 1, 1) + sigs("lny_normalised", 1)
        ln_t = sigs("lnx_turned", 1, 1, 1) + sigs("lny_turned", 1)
        ln_h = sigs("lnx_modulated", 1, 1, 1) + sigs("lny_modulated", 1)
        gated = sigs("xx_gated", 1, 1) + sigs("xy_gated", 1, 1)
        x_new = sigs("xx_new", 1, 1) + sigs("xy_new", 1, 1)
        a_xi = sig("a_xi_ps"); a_z = sig("a_z_ps"); a_pad = sig("a_pad"); a_zs = sig("a_zs")
        a_conv = sig("a_conv", CB * TAPS); a_zth, a_uth = sigs("a_tanh", 1, 1); a_u = sig("a_u")
        a_bcp = sig("a_bc_ps"); a_bc = sig("a_bc", 2); a_split = sig("a_bc_split", 6); a_dtp = sig("a_dt_ps")
        a_vb, a_na = sigs("a_softplus_in", 2, 1); a_e, a_ln = sigs("a_exp_log", 1, 1); a_zero = sig("a_decay_zeroed")
        a_dt, a_dtu = sigs("a_steps", 1, 1)
        a_B = sig("a_B_spread", NG); a_C = sig("a_C_spread", NG); a_Cs = sig("a_C_copied", NG)
        a_dec = sig("a_decay", NG); a_drv = sig("a_drive", NG); a_h = sig("a_state", NG); a_rd = sig("a_read", NG)
        a_yp = sig("a_y_pair", NG); a_y = sig("a_y_summed", NG - 1); a_yq = sig("a_y_summed_ps", NG); a_y1 = sig("a_y_skip", 2); a_ys = sig("a_y_gated", 2)
        a_out = sig("a_out_ps")
        sp_in = sig("sp_neg_abs", 2); sp_e = sig("sp_exp", 2); sp_step = sig("sp_step", 2 * SP_STEPS)
        b_lgp = sig("b_logits_ps"); b_lg = sig("b_logits"); b_sel = sig("b_select", 4); b_root = sig("b_root")
        b_cf = sig("b_cf"); b_cfTp = sig("b_cfT_ps"); b_cfT = sig("b_cfT")
        b_up = sig("b_up_ps", BLK0); b_cfb = sig("b_cf_spread", 4); b_half = sig("b_half", BLK0); b_th = sig("b_tanh", BLK0)
        b_mix = sig("b_mix", 4); b_hs = sig("b_hidden", BLK0); b_out = sig("b_out_ps")
        c_bap = sig("c_ba_ps"); c_ba = sig("c_ba"); c_ebeta = sig("c_exp_beta")
        c_b1 = sig("c_beta", 3); c_g = sig("c_g"); c_dec = sig("c_decay_ps"); c_eGS = sig("c_decay_exp")
        c_gvp = sig("c_gv_ps"); c_gvt = sig("c_gv_tanh"); c_gv = sig("c_gv"); c_gnw = sig("c_gate")
        c_pp = sig("c_proj_ps", 9); c_pad = sig("c_pad", 9); x_kept = sig("x2_kept"); c_tap = sig("c_newest_tap", 9); c_conv = sig("c_conv", 54)
        c_th = sig("c_tanh", 9); c_kq = sig("c_silu", 9); c_sq = sig("c_squares", 8)
        c_ssp = sig("c_ssq_ps", 8); c_ss = sig("c_scales", 7); c_root = sig("c_roots", 2)
        c_kt = sig("c_k_turned", 2); c_ktok = sig("c_k_tokens", 2); c_vt = sig("c_v_turned"); c_vtok = sig("c_v_tokens")
        c_gm = sig("c_gmask", GROUPS); c_D = sig("c_logdecay_ps", GROUPS); c_et = sig("c_decay_matrix", GROUPS)
        c_kk = sig("c_kk_ps", 2 * GROUPS); c_MT = sig("c_MT_heads", 4 * GROUPS); c_AT = sig("c_AT", 2 * GROUPS)
        c_MTs = sig("c_MT_strict", GROUPS); c_t2 = sig("c_T2_step", 2 * GROUPS)
        NL = len(LEVELS)
        c_Z = sig("c_Z_ps", NL * GROUPS); c_W = sig("c_W", NL * GROUPS)
        c_TTp = sig("c_TT_ps", NL * GROUPS); c_TT = sig("c_TT", NL * GROUPS)
        c_Tp = sig("c_T_ps", NL * GROUPS); c_T = sig("c_T", NL * GROUPS)
        c_kS = sig("c_kS_ps"); c_R0, c_R1 = sigs("c_R", 1, 3)
        c_X = sig("c_X_ps", 2); c_U = sig("c_U", 2); c_Uw = sig("c_Uw")
        c_Sp = sig("c_S_ps"); c_S = sig("c_S"); c_O = sig("c_O_ps", 2); c_O2 = sig("c_O2_ps")
        c_o = sig("c_o", 4); c_osq = sig("c_osq"); c_rms, c_og = sigs("c_rms", 3, 1); c_rrms = sig("c_rrms")
        c_oTp = sig("c_oT_ps"); c_oT = sig("c_oT"); c_out = sig("c_out_ps")
        d_qk = sig("d_qk_ps"); d_qks = sig("d_qk", 2); d_vp = sig("d_v_ps"); d_v = sig("d_v")
        d_sc = sig("d_scores_ps"); d_mx, d_rs, d_p = sigs("d_prob", 2, 1, 2); d_e = sig("d_exp", 2)
        d_pT = sig("d_probT_ps"); d_pTs = sig("d_probT"); d_avp = sig("d_av_ps")
        d_av = sig("d_av"); d_ap = sig("d_a_ps"); d_xx = sig("d_xx"); d_glp = sig("d_gate_ps")
        d_g1, d_gt = sigs("d_gates", 4, 4); d_ge = sig("d_gate_exp")
        d_gTp = sig("d_gateT_ps"); d_gT = sig("d_gateT"); d_yi = sig("d_yinit_ps"); d_y0 = sig("d_yinit")
        d_up = sig("d_up_ps", 2 * E1); d_hma = sig("d_hidden_act", 2 * E1); d_hmv = sig("d_hidden_dve", 2 * E1)
        d_eo = sig("d_expert_ps", E1); d_acc = sig("d_mixed", 2 * E1)

        block = ctx.enter_context(nc.Block())
        loads = [
            (con[:], a["con"]), (cT[:, 0, :], a["c0T"]), (cT[:, 1, :], a["c1T"]),
            (wmod[:, 0, :], a["wmod0"]), (wmod[:, 1, :], a["wmod1"]),
            (w_in[:], a["w_inT"]),
            (conv0[:], a["conv_w0"].rearrange("(c p) k -> p c k", p=P)),
            (conv0b[:], a["conv_b0"]),
            (w_bc[:], a["w_bc3"].rearrange("(c p) e -> p c e", p=P)),
            (w_rank[:], a["w_rankT"].rearrange("(c p) e -> p c e", p=P)),
            (w_dt[:], a["w_dtT"]), (b_dt[:], a["b_dt"]),
            (a_neg[:], a["A_log0"].rearrange("(c p) s -> p c s", p=P)),
            (d_half[:], a["D_skip"]),
            (w_out[:], a["w_outT"].rearrange("(c p) d -> p c d", p=P)),
            (rout_w[:], a["routT"]), (rout_b[:], a["exp_bias"].partition_broadcast(P)),
            (up0[:], a["up0"]), (up0b[:], a["up0b"]), (down0[:], a["down0"].rearrange("(m p) d -> p m d", p=P)),
            (down0b[:], a["down0b"]),
            (w_k[:], a["Wk1"]), (w_q[:], a["Wq1"]), (w_v[:], a["Wv1"]), (w_g[:], a["Wg1"]),
            (conv1[:], a["conv1"].rearrange("(m p) k -> p m k", p=P)),
            (w_ba[:, 0:NH], a["Wb1"]), (w_ba[:, NH:2 * NH], a["Wa1"]),
            (expA[:], a["A_log1"].partition_broadcast(P)), (dt_bias[:], a["dt_bias1"].partition_broadcast(P)),
            (norm_half[:], a["norm_w"].partition_broadcast(P)),
            (w_o1[:], a["Wo1"].rearrange("(c p) d -> p c d", p=P)),
            (at_w[:, 0, :], a["fWq"]), (at_w[:, 1, :], a["fWk"]), (at_w[:, 2, :], a["fWv"]), (at_w[:, 3, :], a["fWo"]),
            (at_b[:], a["fb"]), (gate_w[:], a["fWg"]), (gate_b[:], a["fbg"].partition_broadcast(P)),
            (up1[:], a["W1"].rearrange("e d f -> d e f")),
            (up1b[:], a["b1"]),
            (down1[:], a["W2"].rearrange("e (m p) d -> p (e m) d", p=P)),
            (down1b[:], a["b2"]),
        ]
        LOADED = 16 * len(loads)

        def follow(eng, turns, steps):
            first = [step for step in FIRST_HALF if step[0] in steps]
            second = [step for step in SECOND_HALF if step[0] in steps]
            for name, *args in first:
                steps[name](0, *args)
            with eng.Fori(1, NB) as i:
                at = {"x": 0, "y": 0}
                for half in turns:
                    name, *args = (first if half == "x" else second)[at[half]]
                    at[half] += 1
                    steps[name](i if half == "x" else i - 1, *args)
            assert at == {"x": len(first), "y": len(second)}
            for name, *args in second:
                steps[name](NB - 1, *args)

        @block.sync
        def _(sp_):
            for dst, src in loads:
                sp_.dma_start(dst, src).then_inc(loaded, 16)
            sp_.wait_ge(prep_dve, 12)
            sp_.dma_start(gates_dram, gates[:].rearrange("b n d -> b (n d)")).then_inc(gates_stored, 16)
            sp_.wait_ge(gates_stored, 16)

            def load_x(i):
                sp_.dma_start(x[0][:], a["x"][bass.ds(i, 1), :, :].rearrange("b (t p) d -> p (b t) d", p=P)).then_inc(x_loaded.h, 16)

            def load_gates(i, half, done):
                sp_.dma_start(gates_bc[:, 2 * half:2 * half + 2, :].rearrange("p n d -> p (n d)"),
                              gates_dram[bass.ds(i, 1), 2 * half * D:2 * (half + 1) * D].rearrange("b e -> (b e)").partition_broadcast(P)).then_inc(done.h, 16)

            def store(i):
                sp_.dma_start(out[bass.ds(i, 1), :, :].rearrange("b (t p) d -> p (b t) d", p=P), x[4][:]).then_inc(out_stored.h, 16)

            load_x(0)
            load_gates(0, 0, gx_loaded)
            load_gates(0, 1, gy_loaded)
            sp_.wait_ge(x_new[0].h, x_new[0].at(0, 1))
            load_x(1)
            sp_.wait_ge(x_new[1].h, x_new[1].at(0, 1))
            load_gates(1, 0, gx_loaded)
            with sp_.Fori(1, NB - 1) as i:
                sp_.wait_ge(x_new[0].h, x_new[0].at(i, 1))
                load_x(i + 1)
                sp_.wait_ge(x_new[3].h, x_new[3].at(i - 1, 1))
                store(i - 1)
                sp_.wait_ge(out_stored.h, out_stored.at(i - 1, 16))
                load_gates(i, 1, gy_loaded)
                sp_.wait_ge(x_new[1].h, x_new[1].at(i, 1))
                load_gates(i + 1, 0, gx_loaded)
            for i in (NB - 2, NB - 1):
                sp_.wait_ge(x_new[3].h, x_new[3].at(i, 1))
                store(i)
                sp_.wait_ge(out_stored.h, out_stored.at(i, 16))
                if i == NB - 2:
                    load_gates(NB - 1, 1, gy_loaded)

        @block.gpsimd
        def _(g):
            g.wait_ge(loaded, LOADED)
            g.memset(ones_col[:], 1.0)
            g.memset(expo[:, 0:1], -0.5)
            g.memset(expo[:, 1:2], 0.5)
            g.memset(pad0[:], 0.0)
            for n in range(2):
                g.memset(pad1[n][:], 0.0)
            for n in range(TILES):
                g.memset(cf[:, n, 8:9], 1.0)
            g.tensor_copy(identb[:], ident)
            g.tensor_copy(sel3b[:], con[0:3 * 2 * NS, C_SEL3:C_SEL3 + 2 * NS])
            g.tensor_copy(hideb[:], con[:, C_HIDE:C_HIDE + P]).then_inc(prep_pool, 1)
            g.wait_ge(prep_pool, 1)
            g.wait_ge(prep_dve, 12)

            def power(io, which):
                n = io.free_size()
                return g.tensor_tensor(io, io, expo[:, which:which + 1].broadcast_to([P, n]), ALU.pow)

            def rstd(i, n):
                g.wait_ge(ln_var[n].h, ln_var[n].at(i, 1))
                power(mv[n // 3][:, :, 1], 0).then_inc(ln_rstd[n].h, 1)

            def a_norm(i):
                rstd(i, 0)
                for n in range(2):
                    last = g.tensor_tensor(decay[n].rearrange("p (q t) -> p q t", t=T)[:, :, 0:1],
                                           *[zero_col.unsqueeze(1).broadcast_to([P, SG * CB, 1])] * 2, ALU.mult)
                last.then_inc(a_zero.h, 1)

            def a_scan(i, st):
                if st >= 3:
                    p = st - 2
                    g.wait_ge(a_yp.h, a_yp.at(i, p + 1))
                    if p >= 2:
                        g.wait_ge(a_y.h, a_y.at(i, p - 1))
                    g.tensor_tensor(ysum[:], ypart[0][:, T:2 * T] if p == 1 else ysum[:], ypart[p % 2][:, T:2 * T],
                                    ALU.add).then_inc(a_y.h, 1)
                if st < NG:
                    g.wait_ge(a_h.h, a_h.at(i, st + 1))
                    g.wait_ge(a_Cs.h, a_Cs.at(i, st + 1))
                    for q in range(SG):
                        last = g.tensor_tensor(state[st % 2][:, q * 512:(q + 1) * 512].rearrange("p (c t) -> p c t", t=T),
                                               state[st % 2][:, q * 512:(q + 1) * 512].rearrange("p (c t) -> p c t", t=T),
                                               c_sb[st % 2][:, q:q + 1, :].broadcast_to([P, CB, T]), ALU.mult)
                    last.then_inc(a_rd.h, 1)

            def b_root_(i):
                g.wait_ge(sp_step.h, sp_step.at(i, SP_STEPS))
                g.tensor_tensor(lg[:].rearrange("p j e -> p (j e)"), sp[:, 0, :], expo[:, 1:2].broadcast_to([P, TILES * E0]),
                                ALU.pow).then_inc(b_root.h, 1)

            def c_gate(i):
                g.wait_ge(c_gv.h, c_gv.at(i, 1))
                g.tensor_tensor(gnw[:].rearrange("p c (h v) -> p (c h) v", v=DV), gv.rearrange("p c (h v) -> p (c h) v", v=DV),
                                norm_half[:].unsqueeze(1).broadcast_to([P, TILES * NH, DV]), ALU.mult).then_inc(c_gnw.h, 1)

            def c_proj(i, m):
                if 0 <= m - 3 < 8:
                    m -= 3
                    g.wait_ge(c_kq.h, c_kq.at(i, m + 1))
                    if m >= 2:
                        g.wait_ge(c_ssp.h, c_ssp.at(i, m - 1))
                    g.tensor_tensor(sq[m % 2], kq[:, m], kq[:, m], ALU.mult).then_inc(c_sq.h, 1)

            def c_gmask(i, gr):
                ch, hg = gr // 2, gr % 2
                if gr == 0:
                    g.wait_ge(c_g.h, c_g.at(i, 1))
                if gr >= 2:
                    g.wait_ge(c_D.h, c_D.at(i, gr - 1))
                g.tensor_tensor(gmask[gr % 2], gl[:, ch, hg * HG:(hg + 1) * HG].unsqueeze(2).broadcast_to([P, HG, P]),
                                con[:, C_LE:C_LE + P].unsqueeze(1).broadcast_to([P, HG, P]), ALU.mult).then_inc(c_gm.h, 1)

            def c_roots(i):
                g.wait_ge(c_ss.h, c_ss.at(i, 4))
                power(vscale[:].rearrange("p c h -> p (c h)"), 1).then_inc(c_root.h, 1)
                power(rq[:].rearrange("p c h -> p (c h)"), 0).then_inc(c_root.h, 1)

            def c_strict(i, gr):
                g.wait_ge(c_MT.h, c_MT.at(i, 4 * gr + 4))
                g.tensor_tensor(MT[gr], MT[gr], con[:, C_LT:C_LT + P].unsqueeze(1).broadcast_to([P, HG, P]), ALU.mult).then_inc(c_MTs.h, 1)

            def c_squares(i):
                g.wait_ge(c_o.h, c_o.at(i, 4))
                g.tensor_tensor(osq, ou[:], ou[:], ALU.mult).then_inc(c_osq.h, 1)

            def c_rms_(i):
                g.wait_ge(c_rms.h, c_rms.at(i, 2))
                power(rms[:].rearrange("p c h -> p (c h)"), 0).then_inc(c_rrms.h, 1)

            follow(g, TURNS["gpsimd"], dict(a_norm=a_norm, a_scan=a_scan, b_norm=lambda i: rstd(i, 1), b_root=b_root_, c_norm=lambda i: rstd(i, 2),
                           c_gate=c_gate, c_proj=c_proj, c_gmask=c_gmask, c_roots=c_roots, c_strict=c_strict,
                           c_squares=c_squares, c_rms=c_rms_, d_norm=lambda i: rstd(i, 3)))

        @block.scalar
        def _(s):
            s.wait_ge(loaded, LOADED)
            s.activation(xc[:, 0, 0:2 * NB].rearrange("p (l b) -> p l b", l=2), cT[:], ACT.Exp, scale=-1.0).then_inc(silu_c, 1)
            s.activation(a_neg[:], a_neg[:], ACT.Exp).then_inc(prep_act, 1)
            s.activation(expA[:], expA[:], ACT.Exp).then_inc(prep_act, 1)
            s.wait_ge(prep_act, 2)
            s.mul(a_neg[:], a_neg[:], -1.0).then_inc(prep_act, 1)
            s.mul(expA[:], expA[:], -1.0).then_inc(prep_act, 1)
            s.mul(d_half[:], d_half[:], 0.5).then_inc(prep_act, 1)
            s.mul(norm_half[:], norm_half[:], 0.5).then_inc(prep_act, 1)
            s.mul(up0b[:], up0b[:], 0.5).then_inc(prep_act, 1)
            s.wait_ge(prep_act, 7)
            s.wait_ge(prep_pool, 1)
            s.wait_ge(prep_dve, 12)

            def modulate(i, n, bk):
                s.wait_ge(ln_t[n].h, ln_t[n].at(i, 1))
                s.activation(hT[n // 3][:], bank(bk, T), ACT.Identity, bias=shift_scale[:, 2 * n, bass.ds(i, 1)],
                             scale=shift_scale[:, 2 * n + 1, bass.ds(i, 1)]).then_inc(ln_h[n].h, 1)

            def a_in(i):
                s.wait_ge(a_xi.h, a_xi.at(i, 1))
                s.copy(pad0[:, :, 3:3 + T], bank(1).rearrange("p (c t) -> p c t", c=CB)).then_inc(a_pad.h, 1)
                s.wait_ge(a_z.h, a_z.at(i, 1))
                s.activation(th, bank(2).rearrange("p (c t) -> p c t", c=CB), ACT.Tanh, scale=0.5).then_inc(a_zth.h, 1)

            def a_silu(i):
                s.wait_ge(a_conv.h, a_conv.at(i, CB * TAPS))
                s.wait_ge(a_zs.h, a_zs.at(i, 1))
                s.activation(th, xc, ACT.Tanh, scale=0.5).then_inc(a_uth.h, 1)

            def a_xproj(i):
                s.wait_ge(a_bcp.h, a_bcp.at(i, 1))
                s.mul(bcf[:], PS[0:3 * 2 * NS, 0, 0:T], 0.5).then_inc(a_bc.h, 1)
                s.mul(rank_sb[:], PS[0:RANK, 0, T:2 * T], 0.5).then_inc(a_bc.h, 1)

            def a_soft(i):
                s.wait_ge(a_na.h, a_na.at(i, 1))
                s.activation(ev, ev, ACT.Exp).then_inc(a_e.h, 1)
                s.wait_ge(a_e.h, a_e.at(i, 1))
                s.activation(ev, ev, ACT.Ln, bias=1.0).then_inc(a_ln.h, 1)

            def a_scan(i, st):
                if st < NG:
                    s.wait_ge(a_C.h, a_C.at(i, st + 1))
                    if st >= 2:
                        s.wait_ge(a_rd.h, a_rd.at(i, st - 1))
                    s.copy(c_sb[st % 2][:].rearrange("p q t -> p (q t)"), bank(1)).then_inc(a_Cs.h, 1)
                    if st == 0:
                        s.wait_ge(a_dt.h, a_dt.at(i, 1))
                        s.wait_ge(a_zero.h, a_zero.at(i, 1))
                    if st >= 2:
                        s.wait_ge(a_h.h, a_h.at(i, st - 1))
                    for q in range(SG):
                        for c in range(CB):
                            at = (CB * q + c) * T
                            last = s.activation(decay[st % 2][:, at + 1:at + T], dt[:, c, 1:T], ACT.Exp,
                                                scale=a_neg[:, c, st * SG + q:st * SG + q + 1])
                    last.then_inc(a_dec.h, 1)

            def sp_exp(i, which):
                s.wait_ge(sp_in.h, sp_in.at(i, which + 1))
                s.activation(sp[:, 1, :], sp[:, 1, :], ACT.Exp).then_inc(sp_e.h, 1)

            def b_up_(i, m):
                if m < BLK0:
                    M = P if m < 4 else H0
                    s.wait_ge(b_up.h, b_up.at(i, m + 1))
                    if m >= 2:
                        s.wait_ge(b_hs.h, b_hs.at(i, m - 1))
                    s.activation(half0[0:M, m % 2, :], PS[0:M, 2 * (m % 2), 0:T], ACT.Identity, bias=up0b[0:M, m:m + 1],
                                 scale=0.5).then_inc(b_half.h, 1)
                    s.wait_ge(b_half.h, b_half.at(i, m + 1))
                    s.activation(thh[0:M, m % 2, :], half0[0:M, m % 2, :], ACT.Tanh).then_inc(b_th.h, 1)

            def c_beta(i):
                s.wait_ge(c_ba.h, c_ba.at(i, 1))
                s.activation(beta[:], bax[:, :, 0:NH], ACT.Exp, scale=-1.0).then_inc(c_ebeta.h, 1)
                s.wait_ge(c_gvp.h, c_gvp.at(i, 1))
                s.activation(gvt, bank(2).rearrange("p (c v) -> p c v", c=TILES), ACT.Tanh, scale=0.5).then_inc(c_gvt.h, 1)

            def c_proj(i, m):
                if m < 9:
                    s.wait_ge(c_pp.h, c_pp.at(i, m + 1))
                    if m >= 2:
                        s.wait_ge(c_conv.h, c_conv.at(i, 6 * (m - 1)))
                    s.copy(pad1[m % 2][:, :, 3:3 + T], bank(m % 2).rearrange("p (c t) -> p c t", c=2)).then_inc(c_pad.h, 1)
                    if m >= 3:
                        s.wait_ge(c_kq.h, c_kq.at(i, m - 2))
                    for n in range(2):
                        last = s.mul(xc1[m % 3][:, n, :], bank(m % 2, T, n * T), conv1[:, 2 * m + n, TAPS - 1:TAPS])
                    last.then_inc(c_tap.h, 1)
                if 0 <= m - 2 < 9:
                    m -= 2
                    s.wait_ge(c_conv.h, c_conv.at(i, 6 * (m + 1)))
                    if m >= 2:
                        s.wait_ge(c_kq.h, c_kq.at(i, m - 1))
                    s.activation(th1[m % 2], xc1[m % 3], ACT.Tanh, scale=0.5).then_inc(c_th.h, 1)

            def c_turn_k(i, n):
                s.wait_ge(c_kt.h, c_kt.at(i, n + 1))
                s.copy(ktok[n][:], bank(n).rearrange("p (h d) -> p h d", h=4)).then_inc(c_ktok.h, 1)

            def c_turn_v(i):
                s.wait_ge(c_vt.h, c_vt.at(i, 1))
                s.copy(vtok[:].rearrange("p c h v -> p (c h v)"), bank(0)).then_inc(c_vtok.h, 1)

            def c_decay(i):
                s.wait_ge(c_dec.h, c_dec.at(i, 1))
                s.activation(eGS[:].rearrange("p c k h -> p (c k h)"), bank(1, 32), ACT.Exp).then_inc(c_eGS.h, 1)

            def c_logd(i, gr):
                s.wait_ge(c_D.h, c_D.at(i, gr + 1))
                if gr >= 2:
                    s.wait_ge(c_AT.h, c_AT.at(i, 2 * (gr - 1)))
                s.activation(et[gr % 2].rearrange("p h t -> p (h t)"), bank(2), ACT.Exp).then_inc(c_et.h, 1)

            def keep_x(i):
                s.wait_ge(x_new[1].h, x_new[1].at(i, 1))
                s.copy(x2_kept[:], x[2][:]).then_inc(x_kept.h, 1)

            def lev_T(i, l, gr):
                s.wait_ge(c_Tp.h, c_Tp.at(i, l * GROUPS + gr + 1))
                s.copy(TN[gr].rearrange("p h t -> p (h t)"), bank(7)).then_inc(c_T.h, 1)

            def lev_TT(i, l, gr):
                s.wait_ge(c_TTp.h, c_TTp.at(i, l * GROUPS + gr + 1))
                s.copy(TT[gr].rearrange("p h t -> p (h t)"), bank(5 + gr % 2)).then_inc(c_TT.h, 1)

            def c_S_(i):
                s.wait_ge(c_Sp.h, c_Sp.at(i, 1))
                s.copy(S1[:].rearrange("p h v -> p (h v)"), bank(7, 256)).then_inc(c_S.h, 1)

            def c_turn_o(i):
                s.wait_ge(c_oTp.h, c_oTp.at(i, 1))
                s.copy(oT.rearrange("p c t -> p (c t)"), bank(3)).then_inc(c_oT.h, 1)

            def d_qkv(i):
                s.wait_ge(d_qk.h, d_qk.at(i, 1))
                for n in range(2):
                    s.activation(qkT[:, n, :], bank(3, T, n * T), ACT.Identity, bias=at_b[:, n:n + 1]).then_inc(d_qks.h, 1)

            def d_exp(i):
                s.wait_ge(d_mx.h, d_mx.at(i, 2))
                for n in range(TILES):
                    s.activation(prob[:, n, :], bank(5, T, n * T), ACT.Exp, bias=smax[:, 2 + n:3 + n], scale=float(D) ** -0.5,
                                 accum_out=ssum[:, n:n + 1]).then_inc(d_e.h, 1)

            def d_turn_p(i):
                s.wait_ge(d_pT.h, d_pT.at(i, 1))
                s.copy(probT.rearrange("p c t -> p (c t)"), bank(6)).then_inc(d_pTs.h, 1)

            def d_av_(i):
                s.wait_ge(d_avp.h, d_avp.at(i, 1))
                s.activation(avT, bank(7, T), ACT.Identity, bias=at_b[:, 2:3]).then_inc(d_av.h, 1)

            def d_gexp(i):
                s.wait_ge(d_g1.h, d_g1.at(i, 4))
                s.activation(gt[:], gt[:], ACT.Exp).then_inc(d_ge.h, 1)

            def d_yinit_(i):
                s.wait_ge(d_yi.h, d_yi.at(i, 1))
                s.copy(yacc[:].rearrange("p c d -> p (c d)"), bank(5, T)).then_inc(d_y0.h, 1)

            def d_up_(i, e, half):
                if half == 0:
                    s.wait_ge(d_up.h, d_up.at(i, 2 * e + 1))
                    if e >= 2:
                        s.wait_ge(d_eo.h, d_eo.at(i, e - 1))
                    for q in range(2):
                        s.activation(hm[e % 2][:, q, :], bank(3, T, q * T), ACT.Relu,
                                     bias=up1b[:, HB1 * e + q:HB1 * e + q + 1]).then_inc(d_hma.h, 1)

            follow(s, TURNS["scalar"], dict(a_turn=lambda i: modulate(i, 0, 0), a_in=a_in, a_silu=a_silu, a_xproj=a_xproj, a_soft=a_soft,
                           a_scan=a_scan, b_turn=lambda i: modulate(i, 1, 0), b_soft=lambda i: sp_exp(i, 0), b_up=b_up_,
                           c_turn=lambda i: modulate(i, 2, 0), c_beta=c_beta, c_soft=lambda i: sp_exp(i, 1), c_proj=c_proj,
                           c_turn_k=c_turn_k, c_turn_v=c_turn_v, c_decay=c_decay, c_logd=c_logd, lev_T=lev_T, lev_TT=lev_TT,
                           keep_x=keep_x, c_S=c_S_, c_turn_o=c_turn_o, d_turn=lambda i: modulate(i, 3, 7), d_qkv=d_qkv, d_exp=d_exp,
                           d_turn_p=d_turn_p, d_av=d_av_, d_gexp=d_gexp, d_yinit=d_yinit_, d_up=d_up_))

        @block.tensor
        def _(t):
            t.wait_ge(loaded, LOADED)
            t.wait_ge(prep_dve, 3)
            for l in range(2):
                for n, part in enumerate((0, 1, 3, 4)):
                    t.matmul(bank(4, NB, NB * (4 * l + n)), wmod[:, l, part * D:(part + 1) * D],
                             cT[:, l, :], start=True, stop=True)
            for n, (l, part) in enumerate(((0, 2), (0, 5), (1, 2), (1, 5))):
                last = t.matmul(PS[0:NB, 5, n * D:(n + 1) * D], cT[:, l, :], wmod[:, l, part * D:(part + 1) * D], start=True, stop=True)
            last.then_inc(mod_done, 1)
            t.wait_ge(prep_dve, 12)
            t.wait_ge(prep_act, 7)
            t.wait_ge(prep_pool, 1)

            def turn_x(i, n, bk):
                t.wait_ge(ln_x[n].h, ln_x[n].at(i, 1))
                for j in range(TILES):
                    last = t.transpose(bank(bk, P, j * P), xn[n // 3][:, j, :], ident)
                last.then_inc(ln_t[n].h, 1)

            hx, hy = hT

            def a_in(i):
                t.wait_ge(ln_h[0].h, ln_h[0].at(i, 1))
                for c in range(CB):
                    last = t.matmul(bank(1, T, c * T), w_in[:, c * P:(c + 1) * P], hx[:], start=True, stop=True)
                last.then_inc(a_xi.h, 1)
                for c in range(CB):
                    last = t.matmul(bank(2, T, c * T), w_in[:, (CB + c) * P:(CB + c + 1) * P], hx[:], start=True, stop=True)
                last.then_inc(a_z.h, 1)

            def a_xproj(i):
                t.wait_ge(a_u.h, a_u.at(i, 1))
                for c in range(CB):
                    t.matmul(PS[0:3 * 2 * NS, 0, 0:T], w_bc[:, c, :], u2[:, c, :], start=c == 0, stop=c == CB - 1)
                for c in range(CB):
                    last = t.matmul(PS[0:RANK, 0, T:2 * T], w_rank[:, c, :], u2[:, c, :], start=c == 0, stop=c == CB - 1)
                last.then_inc(a_bcp.h, 1)

            def a_dt_(i):
                t.wait_ge(a_bc.h, a_bc.at(i, 2))
                t.wait_ge(a_pad.h, a_pad.at(i, 1))
                for c in range(CB):
                    last = t.matmul(bank(1, T, c * T), w_dt[:, c * P:(c + 1) * P], rank_sb[:], start=True, stop=True)
                last.then_inc(a_dtp.h, 1)

            def spread(row, bk):
                for q in range(SG):
                    last = t.matmul(bank(bk, T, q * T), sel3b[:, row + q:row + q + 1].broadcast_to([3 * 2 * NS, P]), bc3[:],
                                    start=True, stop=True)
                return last

            def a_scan(i, st):
                if st == 0:
                    t.wait_ge(a_split.h, a_split.at(i, 6))
                    t.wait_ge(a_vb.h, a_vb.at(i, 2))
                    t.wait_ge(a_zs.h, a_zs.at(i, 1))
                    spread(0, 0).then_inc(a_B.h, 1)
                    spread(NS, 1).then_inc(a_C.h, 1)
                if st + 1 < NG:
                    t.wait_ge(a_drv.h, a_drv.at(i, st + 1))
                    spread((st + 1) * SG, 0).then_inc(a_B.h, 1)
                    t.wait_ge(a_Cs.h, a_Cs.at(i, st + 1))
                    spread(NS + (st + 1) * SG, 1).then_inc(a_C.h, 1)
                if st >= 2:
                    t.wait_ge(a_yp.h, a_yp.at(i, st - 1))
                    t.matmul(bank(2, T), ident, ypart[st % 2][:, 0:T], start=st == 2, stop=st == NG + 1).then_inc(a_yq.h, 1)

            def a_out_(i):
                t.wait_ge(a_ys.h, a_ys.at(i, 2))
                for j in range(TILES):
                    for c in range(CB):
                        last = t.matmul(bank(1, D, j * D), ysT[:, c, j * P:(j + 1) * P], w_out[:, c, :],
                                        start=c == 0, stop=c == CB - 1)
                last.then_inc(a_out.h, 1)

            def b_logits(i):
                t.wait_ge(ln_h[1].h, ln_h[1].at(i, 1))
                t.wait_ge(x_new[0].h, x_new[0].at(i, 1))
                for j in range(TILES):
                    last = t.matmul(bank(1, E0, j * E0), hx[:, j * P:(j + 1) * P], rout_w[:], start=True, stop=True)
                last.then_inc(b_lgp.h, 1)

            def b_up_(i, m):
                if m < BLK0:
                    M = P if m < 4 else H0
                    if m >= 2:
                        t.wait_ge(b_half.h, b_half.at(i, m - 1))
                    t.matmul(PS[0:M, 2 * (m % 2), 0:T], up0[:, m * P:m * P + M], hx[:], start=True, stop=True).then_inc(b_up.h, 1)
                if m < 4:
                    if m == 0:
                        t.wait_ge(b_cfT.h, b_cfT.at(i, 1))
                    else:
                        t.wait_ge(b_mix.h, b_mix.at(i, m))
                    t.matmul(bank(1, T), con[0:E0, C_SEL + m * P:C_SEL + (m + 1) * P], cfT[0:E0, :], start=True,
                             stop=True).then_inc(b_cfb.h, 1)

            def b_coef(i):
                t.wait_ge(b_cf.h, b_cf.at(i, 1))
                for j in range(TILES):
                    last = t.transpose(PS[0:9, 1, j * P:(j + 1) * P], cf[:, j, :], ident)
                last.then_inc(b_cfTp.h, 1)

            def b_out_(i):
                t.wait_ge(b_hs.h, b_hs.at(i, BLK0))
                for j in range(TILES):
                    for m in range(BLK0):
                        M = P if m < 4 else H0
                        t.matmul(bank(2, D, j * D), hs0[0:M, m, j * P:(j + 1) * P], down0[0:M, m, :], start=m == 0, stop=False)
                    last = t.matmul(bank(2, D, j * D), cfT[:, j * P:(j + 1) * P], down0b[:], start=False, stop=True)
                last.then_inc(b_out.h, 1)

            def c_ba_(i):
                t.wait_ge(ln_h[2].h, ln_h[2].at(i, 1))
                for j in range(TILES):
                    last = t.matmul(bank(1, 2 * NH, j * 2 * NH), hx[:, j * P:(j + 1) * P], w_ba[:], start=True, stop=True)
                last.then_inc(c_bap.h, 1)
                for j in range(TILES):
                    last = t.matmul(bank(2, 256, j * 256), hx[:, j * P:(j + 1) * P], w_g[:], start=True, stop=True)
                last.then_inc(c_gvp.h, 1)

            def c_proj(i, m):
                if m < 9:
                    if m == 1:
                        t.wait_ge(c_ba.h, c_ba.at(i, 1))
                    if m >= 2:
                        t.wait_ge(c_tap.h, c_tap.at(i, m - 1))
                    for n in range(2):
                        w = (w_k if n == 0 else w_q)[:, m * P:(m + 1) * P] if m < 8 else w_v[:, n * P:(n + 1) * P]
                        last = t.matmul(bank(m % 2, T, n * T), w, hx[:], start=True, stop=True)
                    last.then_inc(c_pp.h, 1)
                if 0 <= m - 4 < 8:
                    m -= 4
                    if m == 0:
                        t.wait_ge(c_gv.h, c_gv.at(i, 1))
                    t.wait_ge(c_sq.h, c_sq.at(i, m + 1))
                    for kind in range(2):
                        for ch in range(TILES):
                            last = t.matmul(bank(2, 1, (kind * TILES + ch) * NH + m), sq[m % 2][:, kind, ch * P:(ch + 1) * P],
                                            ones_col[:], start=True, stop=True)
                    last.then_inc(c_ssp.h, 1)

            def c_turn_k(i, n):
                t.wait_ge(c_tap.h, c_tap.at(i, 9))
                for h in range(4):
                    last = t.transpose(bank(n, P, h * P), kq[:, 4 * n + h, 0, 0:P], ident)
                last.then_inc(c_kt.h, 1)

            def c_turn_v(i):
                t.wait_ge(c_kq.h, c_kq.at(i, 9))
                t.wait_ge(c_ktok.h, c_ktok.at(i, 1))
                for ch in range(TILES):
                    for n in range(2):
                        last = t.transpose(bank(0, P, ch * 256 + n * P), v2[:, n, ch * P:(ch + 1) * P], ident)
                last.then_inc(c_vt.h, 1)

            def c_decay(i):
                t.wait_ge(c_g.h, c_g.at(i, 1))
                t.wait_ge(c_ktok.h, c_ktok.at(i, 2))
                for ch in range(TILES):
                    for n, tri in enumerate((C_LE, C_GT)):
                        last = t.matmul(bank(1, NH, (2 * ch + n) * NH), con[:, tri:tri + P], gl[:, ch, :], start=True, stop=True)
                last.then_inc(c_dec.h, 1)

            def c_logd(i, gr):
                t.wait_ge(c_gm.h, c_gm.at(i, gr + 1))
                if gr == 0:
                    t.wait_ge(c_ss.h, c_ss.at(i, 1))
                else:
                    t.wait_ge(c_et.h, c_et.at(i, gr))
                t.matmul(bank(2), con[:, C_GT:C_GT + P], gmask[gr % 2].rearrange("p h t -> p (h t)"), start=True, stop=False)
                t.matmul(bank(2), identb[:], hideb[:].unsqueeze(1).broadcast_to([P, HG, P]), start=False, stop=True).then_inc(c_D.h, 1)

            def c_prod(i, gr, half):
                ch, hg = gr // 2, gr % 2
                n = 2 * gr + half
                if n == 0:
                    t.wait_ge(c_vtok.h, c_vtok.at(i, 1))
                elif n == 1:
                    t.wait_ge(c_eGS.h, c_eGS.at(i, 1))
                else:
                    t.wait_ge(c_AT.h, c_AT.at(i, n - 1))
                for y in range(2):
                    h = hg * HG + 2 * half + y
                    last = t.matmul(bank(n % 2, 256, y * 256), kq[:, h, 0, ch * P:(ch + 1) * P],
                                    kq[:, h, :, ch * P:(ch + 1) * P], start=True, stop=True)
                last.then_inc(c_kk.h, 1)

            def lev_T(i, l, gr):
                if l == 0:
                    t.wait_ge(c_t2.h, c_t2.at(i, 2 * gr + 2))
                else:
                    t.wait_ge(c_TT.h, c_TT.at(i, (l - 1) * GROUPS + gr + 1))
                n = l * GROUPS + gr
                if n >= 1:
                    t.wait_ge(c_T.h, c_T.at(i, n))
                for h in range(HG):
                    last = t.transpose(bank(7, P, h * P), TT[gr][:, h, :], ident)
                last.then_inc(c_Tp.h, 1)

            def lev_Z(i, l, gr):
                n = l * GROUPS + gr
                t.wait_ge(c_T.h, c_T.at(i, n + 1))
                if n >= 2:
                    t.wait_ge(c_W.h, c_W.at(i, n - 1))
                t.matmul(bank(3 + gr % 2), identb[:], identb[:].unsqueeze(1).broadcast_to([P, HG, P]), start=True, stop=False,
                         skip_group_check=True)
                for h in range(HG):
                    last = t.matmul(bank(3 + gr % 2, P, h * P), MT[gr][:, h, :], TN[gr][:, h, :], start=False, stop=h == HG - 1,
                                    skip_group_check=True)
                last.then_inc(c_Z.h, 1)

            def lev_TT(i, l, gr):
                n = l * GROUPS + gr
                t.wait_ge(c_W.h, c_W.at(i, n + 1))
                if n >= 2:
                    t.wait_ge(c_TT.h, c_TT.at(i, n - 1))
                for h in range(HG):
                    last = t.matmul(bank(5 + gr % 2, P, h * P), WW[gr][:, h, :], TT[gr][:, h, :], start=True, stop=True)
                last.then_inc(c_TTp.h, 1)

            def c_X_(i, ch):
                if ch == 0:
                    t.wait_ge(c_R0.h, c_R0.at(i, 1))
                    t.wait_ge(c_TT.h, c_TT.at(i, NL * GROUPS))
                else:
                    t.wait_ge(c_R1.h, c_R1.at(i, 3))
                for h in range(NH):
                    last = t.matmul(bank(3 + ch, DV, h * DV), TT[2 * ch + h // HG][:, h % HG, :], R[:, h, :], start=True, stop=True)
                last.then_inc(c_X.h, 1)

            def c_O_(i, ch):
                t.wait_ge(c_U.h, c_U.at(i, ch + 1))
                for h in range(NH):
                    last = t.matmul(bank(5 + ch, DV, h * DV), AT[2 * ch + h // HG][:, h % HG, :], U[:, h, :], start=True, stop=True)
                last.then_inc(c_O.h, 1)

            def c_S_(i):
                t.wait_ge(c_Uw.h, c_Uw.at(i, 1))
                for h in range(NH):
                    last = t.matmul(bank(7, DV, h * DV), ktok[h // 4][:, h % 4, :], Uw[:, h, :], start=True, stop=True)
                last.then_inc(c_Sp.h, 1)

            def c_kS_(i):
                t.wait_ge(c_S.h, c_S.at(i, 1))
                for h in range(NH):
                    last = t.matmul(bank(7, DV, h * DV), kq[:, h, 0, P:2 * P], S1[:, h, :], start=True, stop=True)
                last.then_inc(c_kS.h, 1)
                t.wait_ge(c_U.h, c_U.at(i, 1))
                for h in range(NH):
                    last = t.matmul(bank(3, DV, h * DV), kq[:, h, 1, P:2 * P], S1[:, h, :], start=True, stop=True)
                last.then_inc(c_O2.h, 1)

            def c_turn_o(i):
                t.wait_ge(c_og.h, c_og.at(i, 1))
                for blk in range(2):
                    for j in range(TILES):
                        last = t.transpose(bank(3, P, blk * T + j * P), og[:, j, blk * P:(blk + 1) * P], ident)
                last.then_inc(c_oTp.h, 1)

            def c_out_(i):
                t.wait_ge(c_oT.h, c_oT.at(i, 1))
                for j in range(TILES):
                    for blk in range(2):
                        last = t.matmul(bank(4, D, j * D), oT[:, blk, j * P:(j + 1) * P], w_o1[:, blk, :], start=blk == 0, stop=blk == 1)
                last.then_inc(c_out.h, 1)

            def d_qkv(i):
                t.wait_ge(ln_h[3].h, ln_h[3].at(i, 1))
                for n in range(2):
                    last = t.matmul(bank(3, T, n * T), at_w[:, n, :], hy[:], start=True, stop=True)
                last.then_inc(d_qk.h, 1)
                for j in range(TILES):
                    last = t.matmul(bank(4, D, j * D), hy[:, j * P:(j + 1) * P], at_w[:, 2, :], start=True, stop=True)
                last.then_inc(d_vp.h, 1)

            def d_scores(i):
                t.wait_ge(d_qks.h, d_qks.at(i, 2))
                for j in range(TILES):
                    last = t.matmul(bank(5, T, j * T), qkT[:, 0, j * P:(j + 1) * P], qkT[:, 1, :], start=True, stop=True)
                last.then_inc(d_sc.h, 1)

            def d_turn_p(i):
                t.wait_ge(d_p.h, d_p.at(i, 2))
                for kt in range(TILES):
                    for j in range(TILES):
                        last = t.transpose(bank(6, P, kt * T + j * P), prob[:, j, kt * P:(kt + 1) * P], ident)
                last.then_inc(d_pT.h, 1)

            def d_av_(i):
                t.wait_ge(d_pTs.h, d_pTs.at(i, 1))
                t.wait_ge(d_v.h, d_v.at(i, 1))
                for kt in range(TILES):
                    last = t.matmul(bank(7, T), v_sb[:, kt, :], probT[:, kt, :], start=kt == 0, stop=kt == TILES - 1)
                last.then_inc(d_avp.h, 1)

            def d_a(i):
                t.wait_ge(d_av.h, d_av.at(i, 1))
                t.matmul(bank(3, T), at_w[:, 3, :], avT, start=True, stop=True).then_inc(d_ap.h, 1)

            def d_gates(i):
                t.wait_ge(d_xx.h, d_xx.at(i, 1))
                for j in range(TILES):
                    last = t.matmul(bank(4, E1, j * E1), xxT[:, j * P:(j + 1) * P], gate_w[:], start=True, stop=True)
                last.then_inc(d_glp.h, 1)

            def d_turn_g(i):
                t.wait_ge(d_gt.h, d_gt.at(i, 4))
                for j in range(TILES):
                    last = t.transpose(PS[0:E1, 6, j * P:(j + 1) * P], gt[:, j, :], ident)
                last.then_inc(d_gTp.h, 1)

            def d_yinit_(i):
                t.wait_ge(d_gT.h, d_gT.at(i, 1))
                for j in range(TILES):
                    t.matmul(bank(5, D, j * D), xxT[:, j * P:(j + 1) * P], ident, start=True, stop=False)
                    last = t.matmul(bank(5, D, j * D), gT[:, j * P:(j + 1) * P], down1b[:], start=False, stop=True)
                last.then_inc(d_yi.h, 1)

            def d_up_(i, e, half):
                if e == 0:
                    t.wait_ge(d_xx.h, d_xx.at(i, 1))
                    if half == 1:
                        t.wait_ge(d_g1.h, d_g1.at(i, 1))
                else:
                    hidden = d_hma if half == 0 else d_hmv
                    t.wait_ge(hidden.h, hidden.at(i, 2 * e))
                for q in range(2):
                    m = 2 * half + q
                    last = t.matmul(bank(3 + half, T, q * T), up1[:, e, m * P:(m + 1) * P], xxT, start=True, stop=True)
                last.then_inc(d_up.h, 1)

            def d_down(i, e, j):
                bk = 6 + e % 2
                if j == 0:
                    t.wait_ge(d_hma.h, d_hma.at(i, 2 * e + 2))
                    t.wait_ge(d_hmv.h, d_hmv.at(i, 2 * e + 2))
                    if e >= 2:
                        t.wait_ge(d_acc.h, d_acc.at(i, 2 * (e - 1)))
                for m in range(HB1):
                    last = t.matmul(bank(bk, D, j * D), hm[e % 2][:, m, j * P:(j + 1) * P], down1[:, HB1 * e + m, :],
                                    start=m == 0, stop=m == HB1 - 1)
                if j == TILES - 1:
                    last.then_inc(d_eo.h, 1)

            follow(t, TURNS["tensor"], dict(a_turn=lambda i: turn_x(i, 0, 0), a_in=a_in, a_xproj=a_xproj, a_dt=a_dt_, a_scan=a_scan, a_out=a_out_,
                           b_turn=lambda i: turn_x(i, 1, 0), b_logits=b_logits, b_up=b_up_, b_coef=b_coef, b_out=b_out_,
                           c_turn=lambda i: turn_x(i, 2, 0), c_ba=c_ba_, c_proj=c_proj, c_turn_k=c_turn_k, c_turn_v=c_turn_v,
                           c_decay=c_decay, c_logd=c_logd, c_prod=c_prod, lev_T=lev_T, lev_Z=lev_Z, lev_TT=lev_TT, c_X=c_X_,
                           c_O=c_O_, c_S=c_S_, c_kS=c_kS_, c_turn_o=c_turn_o, c_out=c_out_, d_turn=lambda i: turn_x(i, 3, 7),
                           d_qkv=d_qkv, d_scores=d_scores, d_turn_p=d_turn_p, d_av=d_av_, d_a=d_a, d_gates=d_gates,
                           d_turn_g=d_turn_g, d_yinit=d_yinit_, d_up=d_up_, d_down=d_down))

        @block.vector
        def _(v):
            v.wait_ge(loaded, LOADED)
            v.memset(sp[:], 0.0).then_inc(prep_dve, 1)
            v.wait_ge(silu_c, 1)
            ec = xc[:, 0, 0:2 * NB].rearrange("p (l b) -> p l b", l=2)
            v.tensor_scalar(ec, ec, 1.0, None, ALU.add).then_inc(silu_c, 1)
            v.wait_ge(silu_c, 2)
            v.reciprocal(ec, ec).then_inc(prep_dve, 1)
            v.wait_ge(prep_dve, 2)
            v.tensor_tensor(cT[:], cT[:], ec, ALU.mult).then_inc(prep_dve, 1)
            v.wait_ge(mod_done, 1)
            v.tensor_copy(shift_scale[:].rearrange("p n b -> p (n b)"), bank(4, 8 * NB)).then_inc(prep_dve, 1)
            v.wait_ge(prep_dve, 4)
            for n in range(4):
                v.tensor_scalar(shift_scale[:, 2 * n + 1, :], shift_scale[:, 2 * n + 1, :], 1.0, None, ALU.add).then_inc(prep_dve, 1)
            g4 = PS[0:NB, 5, :]
            sgn = inv[0:NB, 0]
            mag = inv[0:NB, 1]
            neg = inv[0:NB, 2]
            v.tensor_scalar(sgn, g4, 0.0, 2.0, ALU.is_ge, ALU.mult).then_inc(prep_dve, 1)
            v.tensor_scalar(mag, g4, -1.0, -0.25, ALU.mult, ALU.min).then_inc(prep_dve, 1)
            v.wait_ge(prep_dve, 10)
            v.tensor_scalar(neg, g4, -0.25, None, ALU.min).then_inc(silu_c, 1)
            v.wait_ge(silu_c, 3)
            v.tensor_tensor(mag, mag, neg, ALU.min).then_inc(silu_c, 1)
            v.tensor_scalar(sgn, sgn, 1.0, -1.0, ALU.subtract, ALU.mult).then_inc(silu_c, 1)
            v.wait_ge(silu_c, 5)
            v.tensor_tensor(gates[:].rearrange("b n d -> b (n d)"), sgn, mag, ALU.mult).then_inc(prep_dve, 1)
            v.wait_ge(prep_dve, 11)
            v.tensor_scalar(gates[:, 0, :], gates[:, 0, :], 0.5, None, ALU.mult).then_inc(prep_dve, 1)
            v.wait_ge(prep_dve, 12)
            v.wait_ge(prep_act, 7)
            v.wait_ge(prep_pool, 1)

            def norm(i, n):
                st, m, y = stats[n // 3], mv[n // 3], xn[n // 3]
                if n == 0:
                    v.wait_ge(x_loaded.h, x_loaded.at(i, 16))
                for j in range(TILES):
                    v.bn_stats(st[:, j, :], x[n][:, j, :]).then_inc(ln_step[n].h, 1)
                v.wait_ge(ln_step[n].h, ln_step[n].at(i, 2))
                v.tensor_copy(*carrier)
                for j in range(TILES):
                    v.bn_aggr(m[:, j, :], st[:, j, :]).then_inc(ln_step[n].h, 1)
                v.wait_ge(ln_step[n].h, ln_step[n].at(i, 4))
                v.tensor_scalar(m[:, :, 1], m[:, :, 1], LN_EPS, None, ALU.add).then_inc(ln_var[n].h, 1)

            def norm2(i, n):
                m, y = mv[n // 3], xn[n // 3]
                v.wait_ge(ln_rstd[n].h, ln_rstd[n].at(i, 1))
                for j in range(TILES):
                    last = v.tensor_scalar(y[:, j, :], x[n][:, j, :], m[:, j, 0:1], m[:, j, 1:2], ALU.subtract, ALU.mult)
                last.then_inc(ln_x[n].h, 1)

            def residual(i, n, branch):
                r = branch if n == 3 else xn[n // 2]
                if n % 2 == 0:
                    gates_loaded = gx_loaded if n == 0 else gy_loaded
                    v.wait_ge(gates_loaded.h, gates_loaded.at(i, 16))
                v.tensor_tensor(r[:], branch, gates_bc[:, n:n + 1, :].broadcast_to([P, TILES, D]), ALU.mult).then_inc(gated[n].h, 1)
                v.wait_ge(gated[n].h, gated[n].at(i, 1))
                v.tensor_tensor(x[n + 1][:], x2_kept[:] if n == 2 else x[n][:], r[:], ALU.add).then_inc(x_new[n].h, 1)
                if n < 3:
                    v.wait_ge(x_new[n].h, x_new[n].at(i, 1))

            def tiles(bk):
                return bank(bk, TILES * D).rearrange("p (j d) -> p j d", d=D)

            def softplus16_in(i, which, src):
                v.scalar_tensor_tensor(sp[:, 1, :], src, -1.0, src, ALU.mult, ALU.min).then_inc(sp_in.h, 1)

            def softplus16(i, which, src):
                k = [SP_STEPS * which]

                def step(ins):
                    ins.then_inc(sp_step.h, 1)
                    k[0] += 1
                    v.wait_ge(sp_step.h, sp_step.at(i, k[0]))

                v.wait_ge(sp_e.h, sp_e.at(i, which + 1))
                step(v.tensor_scalar(sp[:, 2, :], sp[:, 1, :], 2.0, None, ALU.add))
                step(v.reciprocal(sp[:, 2, :], sp[:, 2, :]))
                step(v.scalar_tensor_tensor(sp[:, 3, :], sp[:, 1, :], 2.0, sp[:, 2, :], ALU.mult, ALU.mult))
                step(v.scalar_tensor_tensor(sp[:, 4, :], sp[:, 3, :], 0.25, sp[:, 3, :], ALU.mult, ALU.mult))
                step(v.tensor_scalar(sp[:, 5, :], sp[:, 4, :], 1.0 / (2 * LOG1P_TERMS + 1), None, ALU.mult))
                a_, b_ = 5, 6
                for m in range(LOG1P_TERMS - 1, 0, -1):
                    step(v.scalar_tensor_tensor(sp[:, b_, :], sp[:, a_, :], 1.0 / (2 * m + 1), sp[:, 4, :], ALU.add, ALU.mult))
                    a_, b_ = b_, a_
                step(v.scalar_tensor_tensor(sp[:, 7, :], sp[:, a_, :], 1.0, sp[:, 3, :], ALU.add, ALU.mult))
                step(v.scalar_tensor_tensor(sp[:, 0, :], src, 0.0, sp[:, 7, :], ALU.max, ALU.add))
                assert k[0] == SP_STEPS * (which + 1)

            lg2 = lg[:].rearrange("p j e -> p (j e)")

            def a_zgate(i):
                v.wait_ge(a_zth.h, a_zth.at(i, 1))
                v.scalar_tensor_tensor(zs, th, 1.0, bank(2).rearrange("p (c t) -> p c t", c=CB), ALU.add, ALU.mult).then_inc(a_zs.h, 1)

            def a_conv_(i):
                v.wait_ge(a_pad.h, a_pad.at(i, 1))
                for k in range(TAPS):
                    for c in range(CB):
                        if k == 0:
                            v.tensor_scalar(xc[:, c, :], pad0[:, c, 0:T], conv0[:, c, 0:1], conv0b[:, c:c + 1], ALU.mult, ALU.add).then_inc(a_conv.h, 1)
                        else:
                            v.wait_ge(a_conv.h, a_conv.at(i, CB * (k - 1) + c + 1))
                            v.scalar_tensor_tensor(xc[:, c, :], pad0[:, c, k:k + T], conv0[:, c, k:k + 1], xc[:, c, :],
                                                   ALU.mult, ALU.add).then_inc(a_conv.h, 1)

            def a_silu2(i):
                v.wait_ge(a_uth.h, a_uth.at(i, 1))
                v.scalar_tensor_tensor(u2, th, 1.0, xc, ALU.add, ALU.mult).then_inc(a_u.h, 1)

            def a_split_(i):
                v.wait_ge(a_bc.h, a_bc.at(i, 2))
                v.tensor_copy(bc3[:], bcf[:]).then_inc(a_split.h, 1)
                v.wait_ge(a_split.h, a_split.at(i, 1))
                v.tensor_tensor(bcr[:], bcf[:], bc3[:], ALU.subtract).then_inc(a_split.h, 1)
                v.wait_ge(a_split.h, a_split.at(i, 2))
                v.tensor_copy(bcm[:], bcr[:]).then_inc(a_split.h, 1)
                v.wait_ge(a_split.h, a_split.at(i, 3))
                v.tensor_tensor(bcf[:], bcr[:], bcm[:], ALU.subtract).then_inc(a_split.h, 1)
                v.tensor_copy(bc3[32:64, :], bcm[32:64, :]).then_inc(a_split.h, 1)
                v.wait_ge(a_split.h, a_split.at(i, 4))
                v.tensor_copy(bc3[64:96, :], bcf[64:96, :]).then_inc(a_split.h, 1)

            def a_soft1(i):
                v.wait_ge(a_u.h, a_u.at(i, 1))
                v.wait_ge(a_dtp.h, a_dtp.at(i, 1))
                for c in range(CB):
                    v.tensor_scalar(vb[:, c, :], bank(1, T, c * T), b_dt[:, c:c + 1], None, ALU.add).then_inc(a_vb.h, 1)
                v.wait_ge(a_vb.h, a_vb.at(i, 2))
                v.scalar_tensor_tensor(ev, vb, -1.0, vb, ALU.mult, ALU.min).then_inc(a_na.h, 1)

            def a_step(i):
                v.wait_ge(a_ln.h, a_ln.at(i, 1))
                v.scalar_tensor_tensor(dt, vb, 0.0, ev, ALU.max, ALU.add).then_inc(a_dt.h, 1)
                v.wait_ge(a_dt.h, a_dt.at(i, 1))
                v.wait_ge(a_split.h, a_split.at(i, 6))
                v.scalar_tensor_tensor(dtu, dt, 0.5, u2, ALU.mult, ALU.mult).then_inc(a_dtu.h, 1)

            def a_drive(i, st):
                if st < NG:
                    if st == 0:
                        v.wait_ge(a_dtu.h, a_dtu.at(i, 1))
                    v.wait_ge(a_B.h, a_B.at(i, st + 1))
                    if st >= 2:
                        v.wait_ge(a_h.h, a_h.at(i, st - 1))
                    v.tensor_tensor(drive[st % 2].rearrange("p (q c t) -> p q c t", q=SG, c=CB),
                                    bank(0).rearrange("p (q t) -> p q t", t=T).unsqueeze(2).broadcast_to([P, SG, CB, T]),
                                    dtu.unsqueeze(1).broadcast_to([P, SG, CB, T]), ALU.mult).then_inc(a_drv.h, 1)

            def a_scan(i, st):
                if st == 0:
                    a_drive(i, 0)
                a_drive(i, st + 1)
                if st < NG:
                    v.wait_ge(a_dec.h, a_dec.at(i, st + 1))
                    v.wait_ge(a_drv.h, a_drv.at(i, st + 1))
                    if st >= 2:
                        v.wait_ge(a_yp.h, a_yp.at(i, st - 1))
                    v.tensor_tensor_scan(state[st % 2], decay[st % 2], drive[st % 2], 0.0, ALU.mult, ALU.add).then_inc(a_h.h, 1)
                if 1 <= st <= NG:
                    v.wait_ge(a_rd.h, a_rd.at(i, st))
                    if st >= 3:
                        v.wait_ge(a_y.h, a_y.at(i, max(st - 3, 1)))
                        v.wait_ge(a_yq.h, a_yq.at(i, st - 2))
                    r = state[(st - 1) % 2]
                    v.tensor_tensor(ypart[(st - 1) % 2], r[:, 0:512], r[:, 512:1024], ALU.add).then_inc(a_yp.h, 1)

            def a_y_(i):
                v.wait_ge(a_y.h, a_y.at(i, NG - 1))
                v.wait_ge(a_yq.h, a_yq.at(i, NG))
                for c in range(CB):
                    v.scalar_tensor_tensor(ysT[:, c, :], u2[:, c, :], d_half[:, c:c + 1], ysum[:] if c else bank(2, T), ALU.mult, ALU.add).then_inc(a_y1.h, 1)
                for c in range(CB):
                    v.wait_ge(a_y1.h, a_y1.at(i, c + 1))
                    v.tensor_tensor(ysT[:, c, :], ysT[:, c, :], zs[:, c, :], ALU.mult).then_inc(a_ys.h, 1)

            def a_res(i):
                v.wait_ge(a_out.h, a_out.at(i, 1))
                residual(i, 0, tiles(1))

            def b_logits2(i):
                v.wait_ge(b_lgp.h, b_lgp.at(i, 1))
                v.tensor_tensor(lg[:], bank(1, TILES * E0).rearrange("p (j e) -> p j e", e=E0),
                                rout_b[:].unsqueeze(1).broadcast_to([P, TILES, E0]), ALU.add).then_inc(b_lg.h, 1)
                v.wait_ge(b_lg.h, b_lg.at(i, 1))
                softplus16_in(i, 0, lg2)

            def b_select(i):
                v.wait_ge(b_root.h, b_root.at(i, 1))
                v.tensor_copy(*carrier)
                for j in range(TILES):
                    last = v.max(top[:, j, :], lg[:, j, :])
                last.then_inc(b_sel.h, 1)
                v.wait_ge(b_sel.h, b_sel.at(i, 1))
                v.tensor_copy(*carrier)
                for j in range(TILES):
                    last = v.max_index(topi[:, j, :], top[:, j, :], lg[:, j, :])
                last.then_inc(b_sel.h, 1)
                v.wait_ge(b_sel.h, b_sel.at(i, 2))
                v.tensor_copy(topf[:], topi[:]).then_inc(b_sel.h, 1)
                v.wait_ge(b_sel.h, b_sel.at(i, 3))
                for j in range(TILES):
                    for n in range(2):
                        last = v.tensor_scalar(pick[:, j, n, :], con[:, C_IOTA:C_IOTA + 8], topf[:, j, n:n + 1], top[:, j, n:n + 1],
                                               ALU.is_equal, ALU.mult)
                last.then_inc(b_sel.h, 1)
                v.wait_ge(b_sel.h, b_sel.at(i, 4))
                v.tensor_tensor(cf[:, :, 0:8], pick[:, :, 0, :], pick[:, :, 1, :], ALU.add).then_inc(b_cf.h, 1)

            def b_coef(i):
                v.wait_ge(b_cfTp.h, b_cfTp.at(i, 1))
                v.tensor_copy(cfT[:], PS[0:9, 1, 0:T]).then_inc(b_cfT.h, 1)

            def b_up_(i, m):
                m -= 1
                if m >= 0:
                    M = P if m < 4 else H0
                    if m < 4:
                        v.wait_ge(b_half.h, b_half.at(i, m + 1))
                        v.wait_ge(b_cfb.h, b_cfb.at(i, m + 1))
                        if m >= 2:
                            v.wait_ge(b_hs.h, b_hs.at(i, m - 1))
                        v.tensor_tensor(mix0[:, m % 2, :], half0[:, m % 2, :], bank(1, T), ALU.mult).then_inc(b_mix.h, 1)
                        v.wait_ge(b_mix.h, b_mix.at(i, m + 1))
                    v.wait_ge(b_th.h, b_th.at(i, m + 1))
                    src = mix0 if m < 4 else half0
                    v.scalar_tensor_tensor(hs0[0:M, m, :], thh[0:M, m % 2, :], 1.0, src[0:M, m % 2, :], ALU.add, ALU.mult).then_inc(b_hs.h, 1)

            def b_res(i):
                v.wait_ge(b_out.h, b_out.at(i, 1))
                if not isinstance(i, int):
                    v.wait_ge(x_kept.h, x_kept.at(i - 1, 1))
                residual(i, 1, tiles(2))

            def c_beta(i):
                v.wait_ge(c_bap.h, c_bap.at(i, 1))
                v.tensor_copy(bax[:].rearrange("p j n -> p (j n)"), bank(1, TILES * 2 * NH)).then_inc(c_ba.h, 1)
                v.wait_ge(c_ba.h, c_ba.at(i, 1))
                v.tensor_tensor(lg[:], bax[:, :, NH:2 * NH], dt_bias[:].unsqueeze(1).broadcast_to([P, TILES, NH]), ALU.add).then_inc(c_b1.h, 1)
                v.wait_ge(c_b1.h, c_b1.at(i, 1))
                softplus16_in(i, 1, lg2)
                v.wait_ge(c_ebeta.h, c_ebeta.at(i, 1))
                v.tensor_scalar(beta[:], beta[:], 1.0, None, ALU.add).then_inc(c_b1.h, 1)
                v.wait_ge(c_b1.h, c_b1.at(i, 2))
                v.reciprocal(beta[:], beta[:]).then_inc(c_b1.h, 1)

            def c_soft2(i):
                softplus16(i, 1, lg2)
                v.tensor_tensor(gl[:], sp[:, 0, :].rearrange("p (j h) -> p j h", h=NH), expA[:].unsqueeze(1).broadcast_to([P, TILES, NH]),
                                ALU.mult).then_inc(c_g.h, 1)
                v.wait_ge(c_gvt.h, c_gvt.at(i, 1))
                v.scalar_tensor_tensor(gv, gvt, 1.0, bank(2).rearrange("p (c v) -> p c v", c=TILES), ALU.add, ALU.mult).then_inc(c_gv.h, 1)

            def c_proj(i, m):
                if 0 <= m - 3 < 9:
                    n = m - 3
                    if n == 0 and not isinstance(i, int):
                        v.wait_ge(c_og.h, c_og.at(i - 1, 1))
                    v.wait_ge(c_th.h, c_th.at(i, n + 1))
                    v.scalar_tensor_tensor(kq[:, n] if n < 8 else v2, th1[n % 2], 1.0, xc1[n % 3], ALU.add, ALU.mult).then_inc(c_kq.h, 1)
                m -= 1
                if 0 <= m < 9:
                    v.wait_ge(c_pad.h, c_pad.at(i, m + 1))
                    v.wait_ge(c_tap.h, c_tap.at(i, m + 1))
                    for k in range(TAPS - 1):
                        for n in range(2):
                            w = conv1[:, 2 * m + n, k:k + 1]
                            src = pad1[m % 2][:, n, k:k + T]
                            dst = xc1[m % 3][:, n, :]
                            if k >= 1:
                                v.wait_ge(c_conv.h, c_conv.at(i, 6 * m + 2 * (k - 1) + n + 1))
                            v.scalar_tensor_tensor(dst, src, w, dst, ALU.mult, ALU.add).then_inc(c_conv.h, 1)

            def c_scales(i):
                v.wait_ge(c_ssp.h, c_ssp.at(i, 8))
                v.tensor_copy(ssq[:].rearrange("p a b c -> p (a b c)"), bank(2, 32)).then_inc(c_ss.h, 1)
                v.wait_ge(c_ss.h, c_ss.at(i, 1))
                v.tensor_scalar(rk2[:], ssq[:, 0], 4 * L2_EPS, None, ALU.add).then_inc(c_ss.h, 1)
                v.tensor_scalar(vscale[:], ssq[:, 0], 0.25, L2_EPS, ALU.mult, ALU.add).then_inc(c_ss.h, 1)
                v.tensor_scalar(rq[:], ssq[:, 1], float(P), 4 * L2_EPS * P, ALU.mult, ALU.add).then_inc(c_ss.h, 1)
                v.wait_ge(c_ss.h, c_ss.at(i, 4))
                v.reciprocal(rk2[:], rk2[:]).then_inc(c_ss.h, 1)
                v.wait_ge(c_ss.h, c_ss.at(i, 5))
                v.tensor_tensor(cU[:], beta[:], rk2[:], ALU.mult).then_inc(c_ss.h, 1)
                v.wait_ge(c_ss.h, c_ss.at(i, 6))
                v.tensor_scalar(negc[:], cU[:], -1.0, None, ALU.mult).then_inc(c_ss.h, 1)

            def c_prod(i, gr, half):
                ch, hg = gr // 2, gr % 2
                n = 2 * gr + half
                if half == 0:
                    v.wait_ge(c_et.h, c_et.at(i, gr + 1))
                if n == 0:
                    v.wait_ge(c_ss.h, c_ss.at(i, 7))
                v.wait_ge(c_kk.h, c_kk.at(i, n + 1))
                for y in range(2):
                    hh = 2 * half + y
                    v.scalar_tensor_tensor(MT[gr][:, hh, :], bank(n % 2, P, y * 256), negc[:, ch, hg * HG + hh:hg * HG + hh + 1],
                                           et[gr % 2][:, hh, :], ALU.mult, ALU.mult).then_inc(c_MT.h, 1)
                v.tensor_tensor(AT[gr][:, 2 * half:2 * half + 2, :],
                                bank(n % 2).rearrange("p (y k t) -> p y k t", y=2, k=2)[:, :, 1, :],
                                et[gr % 2][:, 2 * half:2 * half + 2, :], ALU.mult).then_inc(c_AT.h, 1)

            def c_first(i, gr):
                v.wait_ge(c_MTs.h, c_MTs.at(i, gr + 1))
                v.tensor_tensor(TT[gr], MT[gr], con[:, C_MASK2:C_MASK2 + P].unsqueeze(1).broadcast_to([P, HG, P]), ALU.mult).then_inc(c_t2.h, 1)
                v.wait_ge(c_t2.h, c_t2.at(i, 2 * gr + 1))
                v.tensor_tensor(TT[gr], TT[gr], ident.unsqueeze(1).broadcast_to([P, HG, P]), ALU.add).then_inc(c_t2.h, 1)

            def lev_Z(i, l, gr):
                v.wait_ge(c_Z.h, c_Z.at(i, l * GROUPS + gr + 1))
                v.tensor_tensor(WW[gr], bank(3 + gr % 2).rearrange("p (h t) -> p h t", h=HG),
                                con[:, C_MERGE + l * P:C_MERGE + (l + 1) * P].unsqueeze(1).broadcast_to([P, HG, P]),
                                ALU.mult).then_inc(c_W.h, 1)

            def by_head(ap):
                return ap.unsqueeze(2).broadcast_to([P, NH, DV])

            def heads(bk):
                return bank(bk, 256).rearrange("p (h v) -> p h v", v=DV)

            def c_R_(i, ch):
                if ch == 0:
                    v.wait_ge(c_vtok.h, c_vtok.at(i, 1))
                    v.wait_ge(c_eGS.h, c_eGS.at(i, 1))
                    v.wait_ge(c_root.h, c_root.at(i, 2))
                    v.tensor_tensor(R[:], vtok[:, 0], by_head(vscale[:, 0]), ALU.mult).then_inc(c_R0.h, 1)
                else:
                    v.wait_ge(c_kS.h, c_kS.at(i, 1))
                    v.tensor_tensor(kSd[:], heads(7), by_head(eGS[:, 1, 0]), ALU.mult).then_inc(c_R1.h, 1)
                    v.tensor_tensor(R[:], vtok[:, 1], by_head(vscale[:, 1]), ALU.mult).then_inc(c_R1.h, 1)
                    v.wait_ge(c_R1.h, c_R1.at(i, 2))
                    v.tensor_tensor(R[:], R[:], kSd[:], ALU.subtract).then_inc(c_R1.h, 1)

            def c_U_(i, ch):
                v.wait_ge(c_X.h, c_X.at(i, ch + 1))
                if ch == 1:
                    v.wait_ge(c_O.h, c_O.at(i, 1))
                v.tensor_tensor(U[:], heads(3 + ch), by_head(cU[:, ch]), ALU.mult).then_inc(c_U.h, 1)
                if ch == 0:
                    v.wait_ge(c_U.h, c_U.at(i, 1))
                    v.tensor_tensor(Uw[:], U[:], by_head(eGS[:, 0, 1]), ALU.mult).then_inc(c_Uw.h, 1)

            def c_o_(i, ch):
                if ch == 0:
                    v.wait_ge(c_O.h, c_O.at(i, 1))
                    v.tensor_tensor(ou[:, 0], heads(5), by_head(rq[:, 0]), ALU.mult).then_inc(c_o.h, 1)
                else:
                    v.wait_ge(c_O2.h, c_O2.at(i, 1))
                    v.wait_ge(c_R1.h, c_R1.at(i, 3))
                    v.tensor_tensor(o2s[:], heads(3), by_head(eGS[:, 1, 0]), ALU.mult).then_inc(c_o.h, 1)
                    v.wait_ge(c_o.h, c_o.at(i, 2))
                    v.wait_ge(c_O.h, c_O.at(i, 2))
                    v.tensor_tensor(o2s[:], heads(6), o2s[:], ALU.add).then_inc(c_o.h, 1)
                    v.wait_ge(c_o.h, c_o.at(i, 3))
                    v.tensor_tensor(ou[:, 1], o2s[:], by_head(rq[:, 1]), ALU.mult).then_inc(c_o.h, 1)

            def c_rms_(i):
                v.wait_ge(c_osq.h, c_osq.at(i, 1))
                v.tensor_reduce(rms[:], osq, X, ALU.add).then_inc(c_rms.h, 1)
                v.wait_ge(c_rms.h, c_rms.at(i, 1))
                v.tensor_scalar(rms[:], rms[:], 1.0 / DV, RMS_EPS, ALU.mult, ALU.add).then_inc(c_rms.h, 1)

            def c_gated(i):
                v.wait_ge(c_rrms.h, c_rrms.at(i, 1))
                v.tensor_tensor(og.rearrange("p c (h v) -> p (c h) v", v=DV), ou[:].rearrange("p c h v -> p (c h) v"),
                                rms[:].rearrange("p c h -> p (c h)").unsqueeze(2).broadcast_to([P, TILES * NH, DV]), ALU.mult).then_inc(c_rms.h, 1)
                v.wait_ge(c_rms.h, c_rms.at(i, 3))
                v.wait_ge(c_gnw.h, c_gnw.at(i, 1))
                v.tensor_tensor(og, og, gnw[:], ALU.mult).then_inc(c_og.h, 1)

            def c_res(i):
                v.wait_ge(c_out.h, c_out.at(i, 1))
                v.wait_ge(x_kept.h, x_kept.at(i, 1))
                residual(i, 2, tiles(4))

            def d_v_(i):
                v.wait_ge(d_vp.h, d_vp.at(i, 1))
                v.tensor_copy(v_sb[:].rearrange("p j d -> p (j d)"), bank(4, TILES * D)).then_inc(d_v.h, 1)

            def d_max(i):
                v.wait_ge(d_sc.h, d_sc.at(i, 1))
                v.tensor_reduce(smax[:, 0:2], bank(5).rearrange("p (j t) -> p j t", t=T), X, ALU.max).then_inc(d_mx.h, 1)
                v.wait_ge(d_mx.h, d_mx.at(i, 1))
                v.tensor_scalar(smax[:, 2:4], smax[:, 0:2], -float(D) ** -0.5, None, ALU.mult).then_inc(d_mx.h, 1)

            def d_prob(i):
                v.wait_ge(d_e.h, d_e.at(i, 2))
                v.reciprocal(ssum[:, 2:4], ssum[:, 0:2]).then_inc(d_rs.h, 1)
                v.wait_ge(d_rs.h, d_rs.at(i, 1))
                for n in range(TILES):
                    v.tensor_scalar(prob[:, n, :], prob[:, n, :], ssum[:, 2 + n:3 + n], None, ALU.mult).then_inc(d_p.h, 1)

            def d_xx_(i):
                v.wait_ge(d_ap.h, d_ap.at(i, 1))
                v.scalar_tensor_tensor(xxT, bank(3, T), at_b[:, 3:4], hT[1][:], ALU.add, ALU.add).then_inc(d_xx.h, 1)

            def d_gsub(i):
                v.wait_ge(d_glp.h, d_glp.at(i, 1))
                v.tensor_tensor(gt[:], bank(4, TILES * E1).rearrange("p (j e) -> p j e", e=E1),
                                gate_b[:].unsqueeze(1).broadcast_to([P, TILES, E1]), ALU.add).then_inc(d_g1.h, 1)
                v.wait_ge(d_g1.h, d_g1.at(i, 1))
                v.tensor_reduce(gm[:, 0:2], gt[:], X, ALU.max).then_inc(d_g1.h, 1)
                v.wait_ge(d_g1.h, d_g1.at(i, 2))
                for j in range(TILES):
                    v.tensor_scalar(gt[:, j, :], gt[:, j, :], gm[:, j:j + 1], None, ALU.subtract).then_inc(d_g1.h, 1)

            def d_gnorm(i):
                v.wait_ge(d_ge.h, d_ge.at(i, 1))
                v.tensor_reduce(gm[:, 2:4], gt[:], X, ALU.add).then_inc(d_gt.h, 1)
                v.wait_ge(d_gt.h, d_gt.at(i, 1))
                v.reciprocal(gm[:, 2:4], gm[:, 2:4]).then_inc(d_gt.h, 1)
                v.wait_ge(d_gt.h, d_gt.at(i, 2))
                for j in range(TILES):
                    v.tensor_scalar(gt[:, j, :], gt[:, j, :], gm[:, 2 + j:3 + j], None, ALU.mult).then_inc(d_gt.h, 1)

            def d_turn_g(i):
                v.wait_ge(d_gTp.h, d_gTp.at(i, 1))
                v.tensor_copy(gT[:], PS[0:E1, 6, 0:T]).then_inc(d_gT.h, 1)

            def d_up_(i, e, half):
                if half == 1:
                    v.wait_ge(d_up.h, d_up.at(i, 2 * e + 2))
                    if e >= 2:
                        v.wait_ge(d_eo.h, d_eo.at(i, e - 1))
                    for q in range(2):
                        v.tensor_scalar(hm[e % 2][:, 2 + q, :], bank(4, T, q * T), up1b[:, HB1 * e + 2 + q:HB1 * e + 3 + q], 0.0,
                                        ALU.add, ALU.max).then_inc(d_hmv.h, 1)

            def d_mix(i, e):
                if e == 0:
                    v.wait_ge(d_y0.h, d_y0.at(i, 1))
                v.wait_ge(d_eo.h, d_eo.at(i, e + 1))
                for j in range(TILES):
                    if e >= 1:
                        v.wait_ge(d_acc.h, d_acc.at(i, 2 * (e - 1) + j + 1))
                    v.scalar_tensor_tensor(yacc[:, j, :], bank(6 + e % 2, D, j * D), gt[:, j, e:e + 1], yacc[:, j, :],
                                           ALU.mult, ALU.add).then_inc(d_acc.h, 1)

            def d_res(i):
                v.wait_ge(d_acc.h, d_acc.at(i, 2 * E1))
                residual(i, 3, yacc)

            follow(v, TURNS["vector"], dict(a_norm=lambda i: norm(i, 0), a_norm2=lambda i: norm2(i, 0), a_conv=a_conv_, a_zgate=a_zgate,
                           a_silu2=a_silu2, a_split=a_split_, a_soft=a_soft1, a_step=a_step, a_scan=a_scan, a_y=a_y_, a_res=a_res,
                           b_norm=lambda i: norm(i, 1), b_norm2=lambda i: norm2(i, 1), b_logits=b_logits2,
                           b_soft2=lambda i: softplus16(i, 0, lg2), b_select=b_select, b_coef=b_coef, b_up=b_up_, b_res=b_res,
                           c_norm=lambda i: norm(i, 2), c_norm2=lambda i: norm2(i, 2), c_beta=c_beta, c_soft2=c_soft2,
                           c_proj=c_proj, c_scales=c_scales, c_prod=c_prod, c_first=c_first, lev_Z=lev_Z, c_R=c_R_, c_U=c_U_,
                           c_o=c_o_, c_rms=c_rms_, c_gated=c_gated, c_res=c_res, d_norm=lambda i: norm(i, 3),
                           d_norm2=lambda i: norm2(i, 3), d_v=d_v_, d_max=d_max, d_prob=d_prob, d_xx=d_xx_, d_gsub=d_gsub,
                           d_gnorm=d_gnorm, d_turn_g=d_turn_g, d_up=d_up_, d_mix=d_mix, d_res=d_res))


def kernel(**k):
    import concourse.bacc as bacc
    from concourse.bass_utils import run_bass_kernel_spmd as run

    n = {key: np.asarray(val) for key, val in k.items()}
    NB = n["L0_attn_x"].shape[0]
    conv1 = np.concatenate([
        np.stack([n["L1_attn_conv_k"].reshape(NH, P, TAPS), n["L1_attn_conv_q"].reshape(NH, P, TAPS)], 1).reshape(2 * NH * P, TAPS),
        n["L1_attn_conv_v"]])
    up0b = np.zeros((BLK0 * P,), np.float32)
    up0b[:E0 * H0] = n["L0_ffn_rb1"].reshape(-1)
    up0b[E0 * H0:9 * H0] = n["L0_ffn_sb1"]
    down0 = np.zeros((BLK0 * P, D), np.float32)
    down0[:E0 * H0] = n["L0_ffn_rW2"].reshape(E0 * H0, D)
    down0[E0 * H0:9 * H0] = n["L0_ffn_sW2"]
    arrays = {
        "x": n["L0_attn_x"], "con": constants(), "c0T": n["L0_c"].T, "c1T": n["L1_c"].T,
        "wmod0": n["L0_wmod"], "wmod1": n["L1_wmod"],
        "w_inT": n["L0_attn_W_in"].T, "conv_w0": n["L0_attn_conv_w"], "conv_b0": n["L0_attn_conv_b"].reshape(CB, P).T,
        "w_bc3": np.tile(n["L0_attn_W_xproj"][RANK:].T, (1, 3)), "w_rankT": n["L0_attn_W_xproj"][:RANK].T, "w_dtT": n["L0_attn_W_dt"].T, "b_dt": n["L0_attn_b_dt"].reshape(CB, P).T,
        "A_log0": n["L0_attn_A_log"], "D_skip": n["L0_attn_D_skip"].reshape(CB, P).T, "w_outT": n["L0_attn_W_out"].T,
        "routT": n["L0_ffn_routing_W"].T, "exp_bias": n["L0_ffn_expert_bias"],
        "up0": np.concatenate([n["L0_ffn_rW1"].transpose(1, 0, 2).reshape(D, E0 * H0), n["L0_ffn_sW1"]], 1),
        "up0b": up0b.reshape(BLK0, P).T, "down0": down0,
        "down0b": np.concatenate([n["L0_ffn_rb2"], n["L0_ffn_sb2"][None]], 0),
        "Wk1": n["L1_attn_Wk"], "Wq1": n["L1_attn_Wq"], "Wv1": n["L1_attn_Wv"], "Wg1": n["L1_attn_Wg"],
        "conv1": conv1, "Wb1": n["L1_attn_Wb"], "Wa1": n["L1_attn_Wa"], "A_log1": n["L1_attn_A_log"],
        "dt_bias1": n["L1_attn_dt_bias"], "norm_w": n["L1_attn_norm_w"], "Wo1": n["L1_attn_Wo"],
        "fWq": n["L1_ffn_Wq"], "fWk": n["L1_ffn_Wk"], "fWv": n["L1_ffn_Wv"], "fWo": n["L1_ffn_Wo"],
        "fb": np.stack([n["L1_ffn_bq"], n["L1_ffn_bk"], n["L1_ffn_bv"], n["L1_ffn_bo"]], 1),
        "fWg": n["L1_ffn_Wg"], "fbg": n["L1_ffn_bg"], "W1": n["L1_ffn_W1"], "b1": n["L1_ffn_b1"].reshape(E1 * HB1, P).T,
        "W2": n["L1_ffn_W2"], "b2": n["L1_ffn_b2"],
    }
    arrays = {key: np.ascontiguousarray(val) for key, val in arrays.items()}
    nc = bacc.Bacc("TRN2", target_bir_lowering=False, num_devices=1)
    aps = {key: nc.dram_tensor("in_" + key, val.shape, F32, kind="ExternalInput").ap() for key, val in arrays.items()}
    out = nc.dram_tensor("out", n["L0_attn_x"].shape, F32, kind="ExternalOutput").ap()
    build(nc, aps, out, NB)
    r = run(nc, [{"in_" + key: val for key, val in arrays.items()}], core_ids=[0])
    return r.results[0]["out"]
```
